# Optimizing a Trainium2 kernel written in Bass

```python
import numpy as np
import jax
import jax.numpy as jnp

def _softmax(x, axis=-1):
    return jax.nn.softmax(x, axis=axis)

def _gelu(x):
    return jax.nn.gelu(x, approximate=True)

def _silu(x):
    return jax.nn.silu(x)

def _sigmoid(x):
    return jax.nn.sigmoid(x)

def _layernorm(x, axis=-1, eps=1e-05):
    m = jnp.mean(x, axis=axis, keepdims=True)
    v = jnp.var(x, axis=axis, keepdims=True)
    return (x - m) / jnp.sqrt(v + eps)

def _scatter_add(tgt, idx, src, axis=0):
    return tgt.at[idx].add(src)

def _segment_sum(src, seg, n):
    return jax.ops.segment_sum(src, seg, n)
kernel_name = 'mk_adaln_attn_ffn_d1_seqx_r4_64647f'

def setup_inputs(seed: int=0):
    np.random.seed(seed)
    _w = jnp.asarray

    def _rec_inputs():
        import jax
        import jax.numpy as jnp
        _rk = jax.random.key(seed)
        x = -0.003407 + 1.001 * jax.random.normal(jax.random.fold_in(_rk, 1), (32, 64, 512), jnp.float32)
        _lenS = 64 - jax.random.randint(jax.random.fold_in(_rk, 7), (32,), 0, max(1, 64 // 4) + 1, jnp.int32)
        _lenS2 = 64 - jax.random.randint(jax.random.fold_in(_rk, 8), (32,), 0, max(1, 64 // 4) + 1, jnp.int32)
        itok_Bx257_0_4111 = jax.random.randint(jax.random.fold_in(_rk, 11), (32, 257), 0, 1028, jnp.int32)
        itok_B_37_3939 = jax.random.randint(jax.random.fold_in(_rk, 12), (32,), 37, 985, jnp.int32)
        itok_B_0_15 = jax.random.randint(jax.random.fold_in(_rk, 13), (32,), 0, 16, jnp.int32)
        return (x, itok_Bx257_0_4111, itok_B_37_3939, itok_B_0_15)
    x, itok_Bx257_0_4111, itok_B_37_3939, itok_B_0_15 = _rec_inputs()

    def _L0_cond_setup():
        import jax, jax.numpy as jnp
        import numpy as np
        H, G, HD = (8, 4, 64)
        GSZ = H // G
        BLOCK = 16
        WINDOW = 256
        SCALE = 256.0 ** (-0.5)
        EPS = 1e-06
        THETA = 10000.0
        B, T, D = (16, 4, 512)
        NBLK = 257

        def _rms(x, scale):
            var = jnp.mean(x * x, axis=-1, keepdims=True)
            return x * jax.lax.rsqrt(var + EPS) * (1.0 + scale)

        def _rope(x, pos):
            half = HD // 2
            inv = 1.0 / THETA ** (jnp.arange(half, dtype=jnp.float32) / half)
            ang = pos[:, :, None].astype(jnp.float32) * inv
            cos = jnp.cos(ang)[:, None, :, :]
            sin = jnp.sin(ang)[:, None, :, :]
            x1, x2 = (x[..., :half], x[..., half:])
            return jnp.concatenate([x1 * cos - x2 * sin, x2 * cos + x1 * sin], axis=-1)
        key = jax.random.key(seed)
        ks = jax.random.split(key, 10)
        inv_d = 1.0 / np.sqrt(D)
        return {'x': jax.random.normal(ks[0], (B, T, D), jnp.float32), 'Wq': jax.random.normal(ks[1], (H * HD, D), jnp.float32) * inv_d, 'Wk': jax.random.normal(ks[2], (G * HD, D), jnp.float32) * inv_d, 'Wv': jax.random.normal(ks[3], (G * HD, D), jnp.float32) * inv_d, 'Wo': jax.random.normal(ks[4], (D, H * HD), jnp.float32) * inv_d, 'q_norm_scale': jax.random.normal(ks[5], (HD,), jnp.float32) * 0.02, 'k_norm_scale': jax.random.normal(ks[6], (HD,), jnp.float32) * 0.02, 'k_blocks': jax.random.normal(ks[7], (B * NBLK, G, BLOCK, HD), jnp.float32), 'v_blocks': jax.random.normal(ks[8], (B * NBLK, G, BLOCK, HD), jnp.float32), 'block_tables': jnp.arange(B * NBLK, dtype=jnp.int32).reshape(B, NBLK), 'kv_lens': jax.random.randint(ks[9], (B,), 0, 1024, dtype=jnp.int32)}
    _L0_cond_all = _L0_cond_setup()
    _L0_cond_in = {k: v for k, v in _L0_cond_all.items() if k in ('Wq', 'Wk', 'Wv', 'Wo', 'q_norm_scale', 'k_norm_scale', 'k_blocks', 'v_blocks')}
    del _L0_cond_all

    def _L0_attn_setup():
        import jax, jax.numpy as jnp
        import numpy as np
        HIDDEN = 512
        HEADS = 16
        HEAD_DIM = HIDDEN // HEADS
        key = jax.random.key(seed)
        ks = jax.random.split(key, 9)
        B, S = (2, 512)
        x = jax.random.normal(ks[0], (B, S, HIDDEN), dtype=jnp.float32)
        scale = 1.0 / np.sqrt(HIDDEN)
        Wq = jax.random.normal(ks[1], (HIDDEN, HIDDEN), dtype=jnp.float32) * scale
        Wk = jax.random.normal(ks[2], (HIDDEN, HIDDEN), dtype=jnp.float32) * scale
        Wv = jax.random.normal(ks[3], (HIDDEN, HIDDEN), dtype=jnp.float32) * scale
        Wo = jax.random.normal(ks[4], (HIDDEN, HIDDEN), dtype=jnp.float32) * scale
        bq = jnp.zeros((HIDDEN,), dtype=jnp.float32)
        bk = jnp.zeros((HIDDEN,), dtype=jnp.float32)
        bv = jnp.zeros((HIDDEN,), dtype=jnp.float32)
        bo = jnp.zeros((HIDDEN,), dtype=jnp.float32)
        return {'x': x, 'Wq': Wq, 'bq': bq, 'Wk': Wk, 'bk': bk, 'Wv': Wv, 'bv': bv, 'Wo': Wo, 'bo': bo}
    _L0_attn_all = _L0_attn_setup()
    _L0_attn_in = {k: v for k, v in _L0_attn_all.items() if k in ('Wq', 'bq', 'Wk', 'bk', 'Wv', 'bv', 'Wo', 'bo')}
    del _L0_attn_all

    def _L0_cond2_setup():
        import jax, jax.numpy as jnp
        import numpy as np
        key = jax.random.key(seed)
        k1, k2, k3, k4 = jax.random.split(key, 4)
        B, S, IN, OUT, E = (64, 64, 512, 512, 16)
        bound = 1.0 / np.sqrt(IN)
        x = jax.random.normal(k1, (B, S, IN), dtype=jnp.float32)
        idx = jax.random.randint(k2, (B,), 0, E, dtype=jnp.int64)
        W = jax.random.uniform(k3, (E, IN, OUT), dtype=jnp.float32, minval=-bound, maxval=bound)
        b = jnp.full((E, OUT), 0.1, dtype=jnp.float32)
        return {'x': x, 'id': idx, 'W': W, 'b': b}
    _L0_cond2_all = _L0_cond2_setup()
    _L0_cond2_in = {k: v for k, v in _L0_cond2_all.items() if k in ('W', 'b')}
    del _L0_cond2_all

    def _L0_ffn_setup():
        import jax, jax.numpy as jnp
        import numpy as np
        CAPACITY = 0.125
        HEAD_DIM = 128
        N_HEADS = 16
        N_KV_HEADS = 8
        ROPE_THETA = 10000.0
        EPS = 1e-06

        def _rms_norm(x, w):
            return x * jax.lax.rsqrt(jnp.mean(x * x, axis=-1, keepdims=True) + EPS) * w

        def _rotate_half(t):
            h = t.shape[-1] // 2
            return jnp.concatenate([-t[..., h:], t[..., :h]], axis=-1)
        key = jax.random.key(seed)
        ks = jax.random.split(key, 12)
        B, T, D = (4, 1024, 512)
        I = 2048
        s = 0.02
        return {'hidden_states': jax.random.normal(ks[0], (B, T, D), jnp.float32), 'w_router': jax.random.normal(ks[1], (D,), jnp.float32) * s, 'wq': jax.random.normal(ks[2], (D, N_HEADS * HEAD_DIM), jnp.float32) * s, 'bq': jnp.zeros((N_HEADS * HEAD_DIM,), jnp.float32), 'wk': jax.random.normal(ks[3], (D, N_KV_HEADS * HEAD_DIM), jnp.float32) * s, 'bk': jnp.zeros((N_KV_HEADS * HEAD_DIM,), jnp.float32), 'wv': jax.random.normal(ks[4], (D, N_KV_HEADS * HEAD_DIM), jnp.float32) * s, 'bv': jnp.zeros((N_KV_HEADS * HEAD_DIM,), jnp.float32), 'wo': jax.random.normal(ks[5], (N_HEADS * HEAD_DIM, D), jnp.float32) * s, 'w_gate': jax.random.normal(ks[6], (D, I), jnp.float32) * s, 'w_up': jax.random.normal(ks[7], (D, I), jnp.float32) * s, 'w_down': jax.random.normal(ks[8], (I, D), jnp.float32) * s, 'ln1_w': jnp.ones((D,), jnp.float32), 'ln2_w': jnp.ones((D,), jnp.float32)}
    _L0_ffn_all = _L0_ffn_setup()
    _L0_ffn_in = {k: v for k, v in _L0_ffn_all.items() if k in ('w_router', 'wq', 'bq', 'wk', 'bk', 'wv', 'bv', 'wo', 'w_gate', 'w_up', 'w_down', 'ln1_w', 'ln2_w')}
    del _L0_ffn_all
    return {'x': x, 'itok_Bx257_0_4111': itok_Bx257_0_4111, 'itok_B_37_3939': itok_B_37_3939, 'itok_B_0_15': itok_B_0_15, 'L0_cond_Wq': _L0_cond_in['Wq'], 'L0_cond_Wk': _L0_cond_in['Wk'], 'L0_cond_Wv': _L0_cond_in['Wv'], 'L0_cond_Wo': _L0_cond_in['Wo'], 'L0_cond_q_norm_scale': _L0_cond_in['q_norm_scale'], 'L0_cond_k_norm_scale': _L0_cond_in['k_norm_scale'], 'L0_cond_k_blocks': _L0_cond_in['k_blocks'], 'L0_cond_v_blocks': _L0_cond_in['v_blocks'], 'L0_attn_Wq': _L0_attn_in['Wq'], 'L0_attn_bq': _L0_attn_in['bq'], 'L0_attn_Wk': _L0_attn_in['Wk'], 'L0_attn_bk': _L0_attn_in['bk'], 'L0_attn_Wv': _L0_attn_in['Wv'], 'L0_attn_bv': _L0_attn_in['bv'], 'L0_attn_Wo': _L0_attn_in['Wo'], 'L0_attn_bo': _L0_attn_in['bo'], 'L0_cond2_W': _L0_cond2_in['W'], 'L0_cond2_b': _L0_cond2_in['b'], 'L0_ffn_w_router': _L0_ffn_in['w_router'], 'L0_ffn_wq': _L0_ffn_in['wq'], 'L0_ffn_bq': _L0_ffn_in['bq'], 'L0_ffn_wk': _L0_ffn_in['wk'], 'L0_ffn_bk': _L0_ffn_in['bk'], 'L0_ffn_wv': _L0_ffn_in['wv'], 'L0_ffn_bv': _L0_ffn_in['bv'], 'L0_ffn_wo': _L0_ffn_in['wo'], 'L0_ffn_w_gate': _L0_ffn_in['w_gate'], 'L0_ffn_w_up': _L0_ffn_in['w_up'], 'L0_ffn_w_down': _L0_ffn_in['w_down'], 'L0_ffn_ln1_w': _L0_ffn_in['ln1_w'], 'L0_ffn_ln2_w': _L0_ffn_in['ln2_w']}

def reference(x, itok_Bx257_0_4111, itok_B_37_3939, itok_B_0_15, L0_cond_Wq, L0_cond_Wk, L0_cond_Wv, L0_cond_Wo, L0_cond_q_norm_scale, L0_cond_k_norm_scale, L0_cond_k_blocks, L0_cond_v_blocks, L0_attn_Wq, L0_attn_bq, L0_attn_Wk, L0_attn_bk, L0_attn_Wv, L0_attn_bv, L0_attn_Wo, L0_attn_bo, L0_cond2_W, L0_cond2_b, L0_ffn_w_router, L0_ffn_wq, L0_ffn_bq, L0_ffn_wk, L0_ffn_bk, L0_ffn_wv, L0_ffn_bv, L0_ffn_wo, L0_ffn_w_gate, L0_ffn_w_up, L0_ffn_w_down, L0_ffn_ln1_w, L0_ffn_ln2_w):
    import jax
    import jax.numpy as jnp

    def _L0_cond_ref(x, Wq, Wk, Wv, Wo, q_norm_scale, k_norm_scale, k_blocks, v_blocks, block_tables, kv_lens):
        import jax, jax.numpy as jnp
        import numpy as np
        H, G, HD = (8, 4, 64)
        GSZ = H // G
        BLOCK = 16
        WINDOW = 256
        SCALE = 256.0 ** (-0.5)
        EPS = 1e-06
        THETA = 10000.0
        B, T, D = (16, 4, 512)
        NBLK = 257

        def _rms(x, scale):
            var = jnp.mean(x * x, axis=-1, keepdims=True)
            return x * jax.lax.rsqrt(var + EPS) * (1.0 + scale)

        def _rope(x, pos):
            half = HD // 2
            inv = 1.0 / THETA ** (jnp.arange(half, dtype=jnp.float32) / half)
            ang = pos[:, :, None].astype(jnp.float32) * inv
            cos = jnp.cos(ang)[:, None, :, :]
            sin = jnp.sin(ang)[:, None, :, :]
            x1, x2 = (x[..., :half], x[..., half:])
            return jnp.concatenate([x1 * cos - x2 * sin, x2 * cos + x1 * sin], axis=-1)
        Bx, Tx, _ = x.shape
        q = jnp.einsum('btd,od->bto', x, Wq).reshape(Bx, Tx, H, HD).transpose(0, 2, 1, 3)
        k = jnp.einsum('btd,od->bto', x, Wk).reshape(Bx, Tx, G, HD).transpose(0, 2, 1, 3)
        v = jnp.einsum('btd,od->bto', x, Wv).reshape(Bx, Tx, G, HD).transpose(0, 2, 1, 3)
        q = _rms(q, q_norm_scale)
        k = _rms(k, k_norm_scale)
        pos = kv_lens[:, None] + jnp.arange(Tx, dtype=jnp.int32)
        q = _rope(q, pos)
        k = _rope(k, pos)
        slot = pos // BLOCK
        off = pos % BLOCK
        blk = jnp.take_along_axis(block_tables, slot, axis=1)
        k_blocks = k_blocks.at[blk, :, off, :].set(k.transpose(0, 2, 1, 3))
        v_blocks = v_blocks.at[blk, :, off, :].set(v.transpose(0, 2, 1, 3))
        k_all = k_blocks[block_tables].transpose(0, 2, 1, 3, 4).reshape(Bx, G, -1, HD)
        v_all = v_blocks[block_tables].transpose(0, 2, 1, 3, 4).reshape(Bx, G, -1, HD)
        S = k_all.shape[2]
        qg = q.reshape(Bx, G, GSZ, Tx, HD)
        scores = jnp.einsum('bghtd,bgsd->bghts', qg, k_all) * SCALE
        kpos = jnp.arange(S, dtype=jnp.int32)
        allowed = (kpos[None, None, :] <= pos[:, :, None]) & (kpos[None, None, :] > pos[:, :, None] - WINDOW)
        scores = jnp.where(allowed[:, None, None, :, :], scores, -jnp.inf)
        p = jax.nn.softmax(scores, axis=-1)
        o = jnp.einsum('bghts,bgsd->bghtd', p, v_all).reshape(Bx, H, Tx, HD)
        o = o.transpose(0, 2, 1, 3).reshape(Bx, Tx, H * HD)
        return jnp.einsum('bto,do->btd', o, Wo)

    def _L0_attn_ref(x, Wq, bq, Wk, bk, Wv, bv, Wo, bo):
        import jax, jax.numpy as jnp
        import numpy as np
        HIDDEN = 512
        HEADS = 16
        HEAD_DIM = HIDDEN // HEADS
        B, S, H = x.shape
        nh, hd = (HEADS, HEAD_DIM)
        q = (x @ Wq.T + bq).reshape(B, S, nh, hd).transpose(0, 2, 1, 3)
        k = (x @ Wk.T + bk).reshape(B, S, nh, hd).transpose(0, 2, 1, 3)
        v = (x @ Wv.T + bv).reshape(B, S, nh, hd).transpose(0, 2, 1, 3)
        scores = jnp.einsum('bhqd,bhkd->bhqk', q, k) / np.sqrt(hd)
        causal = jnp.tril(jnp.ones((S, S), dtype=bool))
        scores = jnp.where(causal[None, None], scores, -jnp.inf)
        probs = jax.nn.softmax(scores, axis=-1)
        attn = jnp.einsum('bhqk,bhkd->bhqd', probs, v)
        y = attn.transpose(0, 2, 1, 3).reshape(B, S, H)
        return y @ Wo.T + bo

    def _L0_cond2_ref(x, id, W, b):
        import jax, jax.numpy as jnp
        import numpy as np
        Wg = W[id]
        bg = b[id]
        out = jnp.einsum('bsi,bio->bso', x, Wg) + bg[:, None, :]
        return out

    def _L0_ffn_ref(hidden_states, w_router, wq, bq, wk, bk, wv, bv, wo, w_gate, w_up, w_down, ln1_w, ln2_w):
        import jax, jax.numpy as jnp
        import numpy as np
        CAPACITY = 0.125
        HEAD_DIM = 128
        N_HEADS = 16
        N_KV_HEADS = 8
        ROPE_THETA = 10000.0
        EPS = 1e-06

        def _rms_norm(x, w):
            return x * jax.lax.rsqrt(jnp.mean(x * x, axis=-1, keepdims=True) + EPS) * w

        def _rotate_half(t):
            h = t.shape[-1] // 2
            return jnp.concatenate([-t[..., h:], t[..., :h]], axis=-1)
        B, T, D = hidden_states.shape
        k = max(1, int(T * CAPACITY))
        scores = jnp.einsum('btd,d->bt', hidden_states, w_router)
        _, idx = jax.lax.top_k(scores, k)
        idx = jnp.sort(idx, axis=-1)
        b = jnp.arange(B)[:, None]
        sel = hidden_states[b, idx]
        sel_scores = scores[b, idx]
        S = B * k
        x = sel.reshape(S, D)
        pos = idx.reshape(S)
        inv_freq = 1.0 / ROPE_THETA ** (jnp.arange(0, HEAD_DIM, 2, dtype=jnp.float32) / HEAD_DIM)
        ang = pos.astype(jnp.float32)[:, None] * inv_freq
        cos = jnp.concatenate([jnp.cos(ang), jnp.cos(ang)], axis=-1)[:, None, :]
        sin = jnp.concatenate([jnp.sin(ang), jnp.sin(ang)], axis=-1)[:, None, :]
        h = _rms_norm(x, ln1_w)
        q = (h @ wq + bq).reshape(S, N_HEADS, HEAD_DIM)
        kk = (h @ wk + bk).reshape(S, N_KV_HEADS, HEAD_DIM)
        v = (h @ wv + bv).reshape(S, N_KV_HEADS, HEAD_DIM)
        q = q * cos + _rotate_half(q) * sin
        kk = kk * cos + _rotate_half(kk) * sin
        rep = N_HEADS // N_KV_HEADS
        kk = jnp.repeat(kk, rep, axis=1)
        v = jnp.repeat(v, rep, axis=1)
        att = jnp.einsum('shd,thd->hst', q, kk) / np.sqrt(HEAD_DIM)
        causal = jnp.tril(jnp.ones((S, S), bool))
        att = jnp.where(causal[None], att, jnp.finfo(att.dtype).min)
        att = jax.nn.softmax(att, axis=-1)
        attn_out = jnp.einsum('hst,thd->shd', att, v).reshape(S, N_HEADS * HEAD_DIM) @ wo
        x1 = x + attn_out
        h2 = _rms_norm(x1, ln2_w)
        mlp = jax.nn.silu(h2 @ w_gate) * (h2 @ w_up) @ w_down
        processed = x1 + mlp
        gate = jax.nn.sigmoid(sel_scores).reshape(S, 1)
        gated = gate * processed + (1.0 - gate) * x
        output = hidden_states.at[b, idx].set(gated.reshape(B, k, D))
        return output
    x = x + _L0_attn_ref(_L0_cond_ref(x, L0_cond_Wq, L0_cond_Wk, L0_cond_Wv, L0_cond_Wo, L0_cond_q_norm_scale, L0_cond_k_norm_scale, L0_cond_k_blocks, L0_cond_v_blocks, itok_Bx257_0_4111, itok_B_37_3939), L0_attn_Wq, L0_attn_bq, L0_attn_Wk, L0_attn_bk, L0_attn_Wv, L0_attn_bv, L0_attn_Wo, L0_attn_bo)
    x = x + _L0_ffn_ref(_L0_cond2_ref(x, itok_B_0_15, L0_cond2_W, L0_cond2_b), L0_ffn_w_router, L0_ffn_wq, L0_ffn_bq, L0_ffn_wk, L0_ffn_bk, L0_ffn_wv, L0_ffn_bv, L0_ffn_wo, L0_ffn_w_gate, L0_ffn_w_up, L0_ffn_w_down, L0_ffn_ln1_w, L0_ffn_ln2_w)
    return x

_drawn_inputs = setup_inputs


def setup_inputs(seed=0):
    import zlib

    import numpy as np

    out = dict(_drawn_inputs(seed))
    spreads = {'L0_attn_bq': (0.0, 0.8),
     'L0_attn_bk': (0.0, 2.0),
     'L0_attn_bv': (0.0, 0.1),
     'L0_attn_bo': (0.0, 0.1),
     'L0_cond2_b': (0.10000000149011612, 0.6),
     'L0_ffn_bq': (0.0, 0.8),
     'L0_ffn_bk': (0.0, 0.8),
     'L0_ffn_bv': (0.0, 0.456),
     'L0_ffn_ln1_w': (1.0, 0.6),
     'L0_ffn_ln2_w': (1.0, 0.6)}
    factors = {'L0_cond_Wq': 5.34,
     'L0_cond_Wk': 8.0,
     'L0_cond_q_norm_scale': 8.0,
     'L0_cond_k_norm_scale': 64.0,
     'L0_cond_k_blocks': 5.799,
     'L0_attn_Wq': 8.0,
     'L0_attn_Wk': 8.0,
     'L0_ffn_wq': 8.0,
     'L0_ffn_wk': 8.0,
     'L0_ffn_wv': 2.934,
     'L0_ffn_w_gate': 3.06,
     'L0_ffn_w_up': 3.011,
     'L0_ffn_w_down': 3.002}
    for name, (base, spread) in spreads.items():
        noise = np.random.default_rng([zlib.crc32(name.encode()), seed]).standard_normal(out[name].shape)
        drawn = base * np.exp(spread * noise) if base else spread * noise
        out[name] = jnp.asarray(drawn.astype(out[name].dtype))
    for name, factor in factors.items():
        out[name] = (out[name] * factor).astype(out[name].dtype)
    return out
```

```python
from contextlib import ExitStack

import numpy as np

import concourse.bass as bass
from concourse import mybir

ALU = mybir.AluOpType
ACT = mybir.ActivationFunctionType
AX = mybir.AxisListType
F32 = mybir.dt.float32
I32 = mybir.dt.int32
U32 = mybir.dt.uint32

P = 128
B, T, D = 32, 64, 512
NT = B * T
PAIRS = B // 2
KD = D // P
CH, CG, CHD = 8, 4, 64
BLOCK, WINDOW, NBLK = 16, 256, 257
POOL_BLOCKS = 16 * NBLK
ROW = 2 * CG * CHD
WSLOTS = WINDOW // BLOCK + T // BLOCK + 1
NSLOTS = T // BLOCK + 1
WPOS = WSLOTS * BLOCK
SPAN = WINDOW + T
QK = CH + CG
SKIP = 1.0e6
GROUPS = 8
GP = B * WSLOTS // GROUPS
WRITERS = B * NSLOTS
NEG = -1.0e30
AH, AHD = 16, 32
HP = AH // 2
PT = 2
TURNS = PAIRS // PT
BT = 2 * PT
TT = PT * P
STEPS = BT * CG
KEEP = 8
S = B * KEEP
SN = S // P
FH, FKV, FHD = 16, 8, 128
FI = 2048
FQKV = (FH + 2 * FKV) * FHD
NQKV = FQKV // 512
NIN = FI // P
COLS = 53200
RING = 6


class Signal:

    def __init__(self, sem, per_turn, prime=0):
        self.sem, self.per_turn, self.prime = sem, per_turn, prime

    def at(self, turn, n):
        return turn * self.per_turn + (self.prime + n)


class Arena:

    def __init__(self, tensor):
        self.tensor, self.next = tensor, 0

    def take(self, *shape):
        n = int(np.prod(shape))
        assert self.next + n <= self.tensor.shape[1], (self.next, n)
        ap = self.tensor[:, self.next:self.next + n]
        self.next += n
        if len(shape) > 1:
            names = "abcdef"[:len(shape)]
            kept = {c: k for c, k in zip(names[1:], shape[1:])}
            ap = ap.rearrange(f"p ({' '.join(names)}) -> p {' '.join(names)}", **kept)
        return ap


def block_kernel(nc, a, out):
    ctx = ExitStack()
    with ctx:
        def sem(name):
            return ctx.enter_context(nc.semaphore(name))

        def sig(name, per_turn, prime=4):
            return Signal(sem(name), per_turn, prime)

        def dram(name, shape, dt=F32):
            return nc.dram_tensor(name, shape, dt).ap()

        kv_new = dram("kv_new", (NT, ROW))
        q_turned = dram("q_turned", (PAIRS, P, 512))
        xh_rows = dram("xh_rows", (NT, 2 * D))
        win_d = dram("win_d", (B, WSLOTS))
        tok_d = dram("tok_d", (B, NSLOTS * BLOCK))
        src_d = dram("src_d", (B * WSLOTS, BLOCK))
        fresh_d = dram("fresh_d", (B, T))
        pick_d = dram("pick_d", (2, B, KEEP), I32)

        ar = Arena(ctx.enter_context(nc.sbuf_tensor("arena", [P, COLS], F32)))
        ident = ar.take(P)
        mask_c = ar.take(2, SPAN)
        place_c = ar.take(2, SPAN)
        mask_a = ar.take(T)
        mask_f = ar.take(2, P)
        eps = ar.take(1)
        seq_base = ar.take(1 + PAIRS)
        CONST = ar.next
        first_seen = ar.take(B)
        score = ar.take(PAIRS)
        score_t = ar.take(PT)
        cache_idx = ar.take(2, B).bitcast(I32)
        over_idx = ar.take(2, B).bitcast(I32)
        fresh_idx = ar.take(PAIRS).bitcast(I32)
        turn_idx = ar.take(PT, 9).bitcast(I32)
        turn_seen = ar.take(BT)
        expert_id = ar.take(B).bitcast(I32)
        router = ar.take(D)
        routed_base = ar.next
        bv = ar.take(D)
        bo = ar.take(D)
        bq = ar.take(KD)
        bk = ar.take(KD)
        w_c_o = ar.take(KD, D)
        w_a_q = ar.take(KD, D)
        w_a_k = ar.take(KD, D)
        w_a_v = ar.take(KD, D)
        w_a_o = ar.take(KD, D)
        base = ar.next
        kv = ar.take(PT, 5, ROW)
        at = ar.next
        k_t = ar.take(PT, 2, 2 * SPAN)
        ar.next = at
        pa_t = ar.take(PT, HP, P)
        ar.next = at + PT * 4 * SPAN
        at = ar.next
        o_t = ar.take(KD, TT)
        ar.next = at
        oa_t = ar.take(PT, KD, P)
        at = ar.next
        y_t = ar.take(KD, TT)
        ar.next = at
        x_t = ar.take(PT, KD, P)
        ka_t = ar.take(KD, TT)
        zeroed = ar.next
        q_blk = ar.take(PT, 2, 2, 2, P)
        qa_blk = ar.take(KD, BT, 4, T)
        pc = ar.take(4, 3 * P)
        va = ar.take(PT, 2, D)
        first = ar.next
        pc_t = ar.take(2, 3 * P)
        mk = ar.take(2, SPAN)
        top_c = ar.take(4)
        neg_c = ar.take(4)
        sum_c = ar.take(2, CG)
        rec_c = ar.take(2, CG)
        oc = ar.take(2, CG * CHD)
        pa = ar.take(PT, HP, 2, T)
        top_a = ar.take(PT, 2 * HP)
        sum_a = ar.take(PT, 2 * HP)
        rec_a = ar.take(PT, 2 * HP)
        oa = ar.take(PT, 2, 2, 4, AHD)
        xr = ar.take(PT, D)
        xh = ar.take(PT, 2 * D)
        junk = ar.take(D)
        b_exp = ar.take(PT, D)
        w_exp = ar.take(BT, KD, D)
        ar.next = first
        w_qkv = ar.take(KD, 1024)
        x_in = ar.take(2, KD, P)
        kvn = ar.take(2, ROW)
        rope = ar.take(PAIRS, 96)
        scale1 = ar.take(QK, CHD)
        sq = ar.take(2, QK, CHD)
        ssum = ar.take(2, QK)
        root = ar.take(2, QK)
        inv = ar.take(2, QK)
        qk = ar.take(2, QK, 2, 32)
        turned = ar.take(2, QK, 2, 32)
        qk_cos = ar.take(2, QK, 2, 32)
        qr = ar.take(2, 512)
        q_out = ar.take(2, 512)
        ar.next = base
        pos_idx = ar.take(PAIRS).bitcast(I32)
        len_all = ar.take(PAIRS + B).bitcast(I32)
        posf = ar.take(PAIRS)
        blocks_i = ar.take(NBLK).bitcast(I32)
        blocks = ar.take(NBLK)
        lens_i = ar.take(8).bitcast(I32)
        lens = ar.take(8)
        k32 = ar.take(NBLK + WSLOTS + NSLOTS * BLOCK + 1 + BLOCK)
        slot_no = ar.take(WSLOTS)
        hit = ar.take(NBLK)
        win = ar.take(WSLOTS)
        tok = ar.take(3, NSLOTS * BLOCK)
        tok_all = ar.take(WRITERS * BLOCK)
        blk_w = ar.take(WRITERS)
        blk_r = ar.take(GROUPS)
        same = ar.take(WRITERS)
        prod = ar.take(BLOCK, WRITERS)
        src = ar.take(GROUPS, BLOCK)
        al = ar.take(2, 2, WPOS)
        idx_f = ar.take(4, SPAN)
        assert ar.next <= zeroed
        ar.next = routed_base
        ring = ar.take(RING, KD, D)
        fq = ar.take(SN, FQKV)
        fq_t = ar.take(FH, S)
        fk_t = ar.take(FKV, S)
        fbias = ar.take(FQKV)
        fo_t = ar.take(FH, S)
        sel = ar.take(SN, 2 * D)
        fh = ar.take(SN, D)
        fh_t = ar.take(KD, S)
        x1 = ar.take(SN, D)
        frope = ar.take(SN, 256)
        fcos = ar.take(2, D)
        fsin = ar.take(2, D)
        fp = ar.take(4, S)
        fp_t = ar.take(2, S)
        ln1 = ar.take(D)
        ln2 = ar.take(D)
        fjunk = ar.take(D)
        small = ar.take(64)
        score_b = ar.take(P)
        top8 = ar.take(2, KEEP)
        at8 = ar.take(2, KEEP).bitcast(U32)
        neg8 = ar.take(2, KEEP)
        sorted8 = ar.take(2, KEEP)
        pick8 = ar.take(2, 2, KEEP).bitcast(I32)
        picked = ar.take(2, SN).bitcast(I32)
        after = ar.next
        ar.next = routed_base + RING * KD * D
        act_t = ar.take(NIN, S)
        e_g = ar.take(2, S)
        r_g = ar.take(2, S)
        assert ar.next <= routed_base + RING * KD * D + SN * FQKV
        ar.next = after

        bank = [ctx.enter_context(nc.psum_tensor(f"bank{i}", [P, 512], F32)) for i in range(8)]

        s_early = sem("small_inputs_loaded")
        s_weights = sem("loop_weights_loaded")
        s_wqkv = sem("wqkv_loaded")
        s_rope = sem("rope_gathered")
        s_win_out = sem("window_blocks_stored")
        s_win_in = sem("window_blocks_back")
        s_src_out = sem("sources_stored")
        s_src_in = sem("sources_back")
        s_fresh = sem("fresh_sources_moved")
        s_pre = sem("vector_setup_step")
        s_zero = sem("zeros_written")
        s_idx_t = sem("index_transposed")
        s_idx = sem("indices_ready")
        s_vector_passed = sem("vector_passed_waits")
        s_pool_passed = sem("pool_passed_waits")
        xin_l = [sem(f"x_in_loaded{u}") for u in range(2)]
        proj = sig("projected", 1)
        squared = sig("squared", 1)
        summed = sig("squares_summed", 1)
        rooted = sig("rooted", 1)
        inverted = sig("inverted", 1)
        normed = sig("normed", 2)
        scaled = sig("scaled", 1)
        turned_p = sig("turned_by_pool", 1)
        turned_v = sig("turned_by_vector", 1)
        cosd = sig("cosine_part", 1)
        roped = sig("roped", 2)
        q_tr = sig("q_transposed", 1)
        q_copied = sig("q_copied", 1)
        q_stored = [sem(f"q_stored{u}") for u in range(2)]
        kv_stored = [sem(f"kv_stored{u}") for u in range(2)]
        same_p = sig("blocks_compared", 1)
        prod_p = sig("writers_marked", 1)
        src_v = sig("last_writer_found", 1)
        q_loaded = [sem(f"q_loaded{j}") for j in range(PT)]
        cached = [sem(f"cached_rows{j}") for j in range(PT)]
        fresh = [sem(f"fresh_rows{j}") for j in range(PT)]
        x_loaded = [sem(f"x_rows{j}") for j in range(PT)]
        we_loaded = [sem(f"expert{n}") for n in range(BT)]
        be_loaded = [sem(f"expert_bias{j}") for j in range(PT)]
        xh_stored = [sem(f"xh_stored{j}") for j in range(PT)]
        out_stored = [sem(f"out_stored{j}") for j in range(PT)]
        idx_set = sig("turn_indices", 3 * PT)
        seen_set = sig("turn_first_places", 1)
        mask_a1 = sig("mask_begun", BT)
        masks = sig("mask_made", BT)
        k_tr = sig("keys_transposed", 3 * PT)
        misc = sig("keys_and_outputs_copied", 3 * PT + BT)
        scored = sig("scored", STEPS, STEPS)
        masked = sig("masked", STEPS)
        negated = sig("max_negated", STEPS)
        exped = sig("exped", STEPS)
        p_tr = sig("probs_transposed", STEPS)
        p_act = sig("probs_copied_by_scalar", STEPS // 4)
        p_dve = sig("probs_copied_by_vector", STEPS - STEPS // 4)
        pv_done = sig("values_weighted", STEPS, STEPS)
        recd = sig("sums_inverted", BT)
        o_norm = sig("output_normed", BT)
        o_tr = sig("output_transposed", BT)
        y_done = sig("y_done", 2)
        y_act = sig("y_copied_by_scalar", 1)
        y_dve = sig("y_copied_by_vector", 1)
        qa_done = sig("qa_done", 2)
        qa_act = sig("qa_copied_by_scalar", 1)
        qa_dve = sig("qa_copied_by_vector", 1)
        ka_done = sig("ka_done", 2)
        ka_act = sig("ka_copied_by_scalar", 1)
        ka_dve = sig("ka_copied_by_vector", 1)
        sa_done = sig("sa_scored", PT)
        sa_mask = sig("sa_masked", 2 * PT)
        sa_max = sig("sa_max", PT)
        sa_sub = sig("sa_max_subtracted", PT)
        sa_exp = sig("sa_exped", PT)
        sa_sum = sig("sa_summed", PT)
        sa_rec = sig("sa_inverted", PT)
        va_done = sig("va_done", PT)
        va_cop = sig("va_copied", PT)
        pa_tr = sig("pa_transposed", PT)
        pa_cop = sig("pa_copied", PT)
        pva = sig("pva_done", PT)
        oa_norm = sig("oa_normed", PT)
        oa_tr = sig("oa_transposed", PT)
        oa_cop = sig("oa_copied", PT)
        z_done = sig("z_done", PT)
        x_bias = sig("x_plus_bias", PT)
        resid = sig("residual_added", PT)
        x_tr = sig("x_transposed", PT)
        x_cop = sig("x_copied", PT)
        c_done = sig("expert_done", PT)
        hid = sig("hidden_made", PT)
        rscore = sig("router_scored", PT)
        sc_cop = sig("scores_kept", 1)
        out_add = sig("out_rows_made", PT)
        s_fin = sem("routed_inputs_loaded")
        s_sct = sem("scores_transposed")
        s_pick = sem("pick_step")
        s_pick_out = sem("picks_stored")
        s_pick_in = sem("picks_back")
        s_sel = sem("selected_rows")
        s_gate = sem("row_gate_step")
        s_last = sem("last_rows_step")
        f_x1 = sig("f_residual_added", 0, 0)
        s_rms = sem("routed_square_root")
        s_esc = sem("routed_gate_exp")
        r_landed = [sem(f"ring_landed{n}") for n in range(RING)]
        fh_ready = sig("fh_ready", 0, 0)
        fh_tr = sig("fh_transposed", 0, 0)
        fh_cop = sig("fh_copied", 0, 0)
        fq_mm = sig("fq_done", 0, 0)
        fq_bias = sig("fq_biased", 0, 0)
        f_sin = sig("f_sin_part", 0, 0)
        f_cos = sig("f_cos_part", 0, 0)
        f_rope = sig("f_roped", 0, 0)
        fq_tr = sig("fq_transposed", 0, 0)
        fq_cop = sig("fq_copied", 0, 0)
        fs = sig("f_scored", 0, 0)
        fmask = sig("f_masked", 0, 0)
        fneg = sig("f_negated", 0, 0)
        fexp = sig("f_exped", 0, 0)
        frec = sig("f_inverted", 0, 0)
        fnorm = sig("f_normed", 0, 0)
        fp_tr = sig("f_probs_transposed", 0, 0)
        fp_cop = sig("f_probs_copied", 0, 0)
        fpv = sig("f_values_weighted", 0, 0)
        fo_cop = sig("f_outputs_copied", 0, 0)
        fwo = sig("f_projected", 0, 0)
        g_done = sig("gate_up_done", 0, 0)
        g_exp = sig("gate_exped", 0, 0)
        g_one = sig("gate_step", 0, 0)
        g_act = sig("gated_made", 0, 0)
        f_down = sig("down_done", 0, 0)
        s_fout = sem("routed_rows_stored")

        PRE_WIN = 12 + WSLOTS + 4
        PRE_ALL = PRE_WIN + 2
        PRE_IDX = PRE_ALL + 12

        def early(sp, dst, source):
            sp.dma_start(dst, source).then_inc(s_early, 16)

        def probs_copied(eng, turn, s):
            if s % 4 == 3:
                eng.wait_ge(p_act.sem, p_act.at(turn, s // 4 + 1))
            else:
                eng.wait_ge(p_dve.sem, p_dve.at(turn, s + 1 - (s + 1) // 4))

        block = ctx.enter_context(nc.Block())

        @block.sync
        def _(sp):
            for u in range(PT):
                sp.sem_inc(xh_stored[u], 16)
                sp.sem_inc(out_stored[u], 16)
                sp.sem_inc(q_stored[u], 16)
                sp.sem_inc(kv_stored[u], 16)
            early(sp, len_all, a["lens_rep"])
            early(sp, seq_base, a["consts"][:, CONST - 1 - PAIRS:CONST])
            early(sp, blocks_i[0:B, 0:NBLK], a["tables"])
            early(sp, lens_i[0:B, 0:1], a["lens"])
            early(sp, k32[0:B, :], a["consts32"])
            early(sp, ar.tensor[:, 0:CONST - 1 - PAIRS], a["consts"][:, 0:CONST - 1 - PAIRS])
            early(sp, scale1, a["qk_scale"].rearrange("p (h d) -> p h d", h=QK))
            for k in range(KD):
                sp.dma_start(w_qkv[:, k, :], a["w_qkv"][:, k, :]).then_inc(s_wqkv, 16)
            sp.wait_ge(s_pre, PRE_WIN)
            sp.dma_start(win_d, win[0:B, :]).then_inc(s_win_out, 16)
            sp.dma_start(tok_d, tok[0:B, 2, :]).then_inc(s_win_out, 16)
            sp.wait_ge(s_win_out, 32)
            with nc.allow_non_contiguous_dma(reason="a few block numbers"):
                sp.dma_start(blk_r[0:GP, :], win_d.rearrange("b s -> (b s)").rearrange("(g p) -> p g", p=GP)).then_inc(s_win_in, 16)
                sp.dma_start(blk_w[0:GP, :].rearrange("p (b s) -> p b s", s=NSLOTS),
                             win_d[:, WSLOTS - NSLOTS:WSLOTS].partition_broadcast(GP)).then_inc(s_win_in, 16)
            sp.dma_start(tok_all[0:GP, :], tok_d.rearrange("b s -> (b s)").partition_broadcast(GP)).then_inc(s_win_in, 16)
            for u in range(2):
                sp.dma_start(x_in[:, u], a["x_t"][u]).then_inc(xin_l[u], 16)
            with sp.Fori(0, PAIRS // 2 - 1) as i:
                for u in range(2):
                    t = i * 2 + u
                    sp.wait_ge(roped.sem, roped.at(t, 2))
                    sp.dma_start(kv_new[bass.ds(t * P, P), :], kvn[:, u]).then_inc(kv_stored[u], 16)
                    sp.wait_ge(proj.sem, proj.at(t, 1))
                    sp.dma_start(x_in[:, u], a["x_t"][bass.ds(t + 2, 1)].rearrange("a p k n -> p (a k) n")).then_inc(xin_l[u], 16)
                    sp.wait_ge(q_copied.sem, q_copied.at(t, 1))
                    sp.dma_start(q_turned[bass.ds(t, 1)].rearrange("a p n -> p (a n)"), q_out[:, u]).then_inc(q_stored[u], 16)
            for u in range(2):
                t = PAIRS - 2 + u
                sp.wait_ge(roped.sem, roped.at(t, 2))
                sp.dma_start(kv_new[t * P:(t + 1) * P, :], kvn[:, u]).then_inc(kv_stored[u], 16)
                sp.wait_ge(q_copied.sem, q_copied.at(t, 1))
                sp.dma_start(q_turned[t], q_out[:, u]).then_inc(q_stored[u], 16)
            sp.wait_ge(src_v.sem, src_v.at(GROUPS, 0))
            sp.dma_start(src_d.rearrange("(g p) o -> p g o", p=GP), src[0:GP]).then_inc(s_src_out, 16)
            sp.wait_ge(s_src_out, 16)
            sp.dma_start(al[0:B, 0, 1, :], src_d.rearrange("(b s) o -> b (s o)", b=B)).then_inc(s_src_in, 16)
            for dst, source in ((w_c_o, "w_c_o"), (w_a_q, "w_a_q"), (w_a_k, "w_a_k"), (w_a_v, "w_a_v"), (w_a_o, "w_a_o")):
                sp.dma_start(dst, a[source]).then_inc(s_weights, 16)
            for dst, source in ((bq, "bq"), (bk, "bk")):
                sp.dma_start(dst, a[source]).then_inc(s_weights, 16)
            for dst, source in ((bv, "bv"), (bo, "bo"), (router, "router")):
                sp.dma_start(dst, a[source].partition_broadcast(P)).then_inc(s_weights, 16)
            sp.dma_start(expert_id[0:1, :], a["experts"]).then_inc(s_weights, 16)
            sp.wait_ge(s_pre, PRE_IDX)
            sp.dma_start(fresh_d, idx_f[0:B, 1, WINDOW:SPAN]).then_inc(s_fresh, 16)
            sp.wait_ge(s_fresh, 16)
            sp.dma_start(idx_f[0:PAIRS, 2, 0:P], fresh_d.rearrange("(q b) t -> q (b t)", b=2)).then_inc(s_fresh, 16)
            for u in range(2):
                sp.wait_ge(q_stored[u], 16 * (PAIRS // 2 + 1))
            sp.wait_ge(s_weights, 16 * 11)
            sp.wait_ge(s_zero, 4)

            with sp.Fori(0, TURNS) as i:
                for j in range(PT):
                    sp.wait_ge(scored.sem, scored.at(i, 8 * (j + 1) - STEPS))
                    source = q_turned[bass.ds(i * PT + j, 1)].rearrange("a p (c n) -> p (a c) n", c=4)
                    for g2 in range(2):
                        rows = slice(64 * g2, 64 * g2 + 64)
                        sp.dma_start(q_blk[rows, j, :, :, g2, :].rearrange("p b g n -> p (b g) n"), source[rows]).then_inc(q_loaded[j], 16)
                for j in range(PT):
                    sp.wait_ge(out_stored[j], i * 16 + 16)
                    sp.dma_start(xr[:, j], a["x_rows"][bass.ds(i * PT + j, 1)].rearrange("a p n -> p (a n)")).then_inc(x_loaded[j], 16)
                    sp.wait_ge(c_done.sem, c_done.at(i, j + 1 - PT))
                    sp.wait_ge(hid.sem, hid.at(i, j + 1 - PT))
                    for b in range(2):
                        n = 2 * j + b
                        e = sp.value_load(expert_id[0:1, bass.ds(i * BT + n, 1)], min_val=0, max_val=15)
                        sp.dma_start(w_exp[:, n], a["w_exp"][bass.ds(e, 1)].rearrange("e p k n -> p (e k) n")).then_inc(we_loaded[n], 16)
                        sp.dma_start(b_exp[64 * b:64 * b + 64, j, :], a["b_exp"][bass.ds(e, 1), :].rearrange("e n -> (e n)").partition_broadcast(64)).then_inc(be_loaded[j], 16)
                for j in range(PT):
                    sp.wait_ge(hid.sem, hid.at(i, j + 1))
                    sp.dma_start(xh_rows[bass.ds((i * PT + j) * P, P), :], xh[:, j]).then_inc(xh_stored[j], 16)
                    sp.wait_ge(out_add.sem, out_add.at(i, j + 1))
                    sp.dma_start(out[bass.ds(i * PT + j, 1)].rearrange("a p n -> p (a n)"), xr[:, j]).then_inc(out_stored[j], 16)

            sp.wait_ge(c_done.sem, c_done.at(TURNS, 0))
            sp.wait_ge(x_bias.sem, x_bias.at(TURNS, 0))
            chunks = [a["f_qkv"][c] for c in range(NQKV)] + [a["f_wo"][c] for c in range(4)]
            for c in range(4):
                chunks += [a["f_gate"][c], a["f_up"][c]]
            chunks += [a["f_down"][c] for c in range(4)]
            for n, source in enumerate(chunks[:RING]):
                sp.dma_start(ring[:, n], source).then_inc(r_landed[n], 16)
            sp.wait_ge(rscore.sem, rscore.at(TURNS, 0))
            sp.wait_ge(out_add.sem, out_add.at(TURNS, 0))
            sp.dma_start(fbias, a["f_bias"].partition_broadcast(P)).then_inc(s_fin, 16)
            sp.dma_start(ln1, a["ln1"].partition_broadcast(P)).then_inc(s_fin, 16)
            sp.dma_start(ln2, a["ln2"].partition_broadcast(P)).then_inc(s_fin, 16)
            sp.wait_ge(s_pick, 11)
            for kind in range(2):
                sp.dma_start(pick_d[kind].rearrange("(q b) j -> q b j", b=2), pick8[0:PAIRS, kind]).then_inc(s_pick_out, 16)
            sp.wait_ge(s_pick_out, 32)
            with nc.allow_non_contiguous_dma(reason="256 row numbers"):
                for kind in range(2):
                    sp.dma_start(picked[:, kind, :], pick_d[kind].rearrange("b j -> (b j)").rearrange("(n q) -> q n", q=P)).then_inc(s_pick_in, 16)
            for n, source in enumerate(chunks):
                if n >= RING:
                    m = n - RING
                    if m < NQKV:
                        sp.wait_ge(fq_mm.sem, 2 * (m + 1))
                    elif m < NQKV + 4:
                        sp.wait_ge(fwo.sem, m - NQKV + 1)
                    else:
                        sp.wait_ge(g_done.sem, 4 * ((m - NQKV - 4) // 2 + 1))
                    sp.dma_start(ring[:, n % RING], source).then_inc(r_landed[n % RING], 16)
            for j in range(PT):
                sp.wait_ge(xh_stored[j], 16 * (TURNS + 1))
                sp.wait_ge(out_stored[j], 16 * (TURNS + 1))

        @block.tensor
        def _(pe):
            for g in (proj, q_tr, k_tr, scored, p_tr, pv_done, o_tr, y_done, qa_done, ka_done, sa_done, va_done, pa_tr, pva,
                      oa_tr, z_done, x_tr, c_done):
                pe.sem_inc(g.sem, g.prime)
            pe.wait_ge(s_wqkv, 16 * KD)

            def project(t, u):
                pe.wait_ge(xin_l[u], t * 8 + (16 - 8 * u))
                pe.wait_ge(normed.sem, normed.at(t, 2 - 4))
                for half in range(2):
                    for k in range(KD):
                        mm = pe.matmul(bank[2 * u + half][:], x_in[:, u, k, :], w_qkv[:, k, 512 * half:512 * half + 512],
                                       start=(k == 0), stop=(k == KD - 1))
                mm.then_inc(proj.sem, 1)

            def turn_queries(t, u):
                pe.wait_ge(roped.sem, roped.at(t, 2))
                pe.wait_ge(q_copied.sem, q_copied.at(t, 1 - 2))
                for n in range(4):
                    mm = pe.transpose(bank[4 + u][:, n * P:(n + 1) * P], qr[:, u, n * P:(n + 1) * P], ident)
                mm.then_inc(q_tr.sem, 1)

            project(0, 0)
            with pe.Fori(0, PAIRS // 2 - 1) as i:
                project(i * 2 + 1, 1)
                turn_queries(i * 2, 0)
                project(i * 2 + 2, 0)
                turn_queries(i * 2 + 1, 1)
            project(PAIRS - 1, 1)
            turn_queries(PAIRS - 2, 0)
            turn_queries(PAIRS - 1, 1)

            pe.wait_ge(q_copied.sem, q_copied.at(PAIRS, 0))
            pe.wait_ge(s_fresh, 32)
            for kind in range(2):
                for half in range(2):
                    n = 2 * kind + half
                    pe.transpose(bank[0][:, n * B:(n + 1) * B], idx_f[0:B, kind, half * P:(half + 1) * P], ident[0:B, 0:B])
            pe.transpose(bank[0][:, 4 * B:4 * B + PAIRS], idx_f[0:PAIRS, 2, 0:P], ident[0:PAIRS, 0:PAIRS]).then_inc(s_idx_t, 1)

            pe.wait_ge(s_weights, 16 * 11)
            pe.wait_ge(s_idx, 3)
            pe.wait_ge(s_zero, 4)

            def turn_keys(i, j):
                pe.wait_ge(cached[j], i * 64 + 64)
                pe.wait_ge(fresh[j], i * 80 + 80)
                for n in range(3):
                    use = 3 * j + n
                    pe.wait_ge(misc.sem, misc.at(i, use + 1 - 2))
                    cols = range(4 * n, min(4 * n + 4, 10))
                    for m in cols:
                        g, tile = m // 5, (0, 1, 4, 2, 3)[m % 5]
                        mm = pe.transpose(bank[6 + use % 2][:, (m - cols[0]) * P:(m - cols[0] + 1) * P],
                                          kv[:, j, tile, g * P:(g + 1) * P], ident)
                    mm.then_inc(k_tr.sem, 1)

            def scores(i, s):
                j, b, g = s // 8, s // 4 % 2, s % 4
                pe.wait_ge(q_loaded[j], i * 32 + 32)
                pe.wait_ge(misc.sem, misc.at(i, 3 * (j + 1)))
                pe.wait_ge(masked.sem, masked.at(i, s + 1 - 2))
                pe.matmul(bank[s % 2][:, 0:SPAN], q_blk[:, j, b, g // 2, g % 2, :],
                          k_t[:, j, g // 2, b * SPAN:(b + 1) * SPAN], start=True, stop=True).then_inc(scored.sem, 1)

            def turn_probs(i, s):
                b, g = s // 4 % 2, s % 4
                pe.wait_ge(exped.sem, exped.at(i, s + 1))
                if s >= 2:
                    probs_copied(pe, i, s - 2)
                else:
                    probs_copied(pe, i - 1, STEPS - 2 + s)
                for c in range(3):
                    mm = pe.transpose(bank[2 + s % 2][:, c * P:(c + 1) * P], pc[:, 2 * b + g % 2, c * P:(c + 1) * P], ident)
                mm.then_inc(p_tr.sem, 1)

            def weigh_values(i, s):
                j, b, g = s // 8, s // 4 % 2, s % 4
                n = s // 4
                probs_copied(pe, i, s)
                if g == 0:
                    pe.wait_ge(o_norm.sem, o_norm.at(i, n + 1 - 2))
                for c, tile in enumerate((0, 1, 4) if b == 0 else (4, 2, 3)):
                    mm = pe.matmul(bank[4 + n % 2][:, g * CHD:(g + 1) * CHD], pc_t[:, s % 2, c * P:(c + 1) * P],
                                   kv[:, j, tile, CG * CHD + g * CHD:CG * CHD + (g + 1) * CHD],
                                   start=(c == 0), stop=(c == 2))
                mm.then_inc(pv_done.sem, 1)

            def turn_outputs(i, n):
                use = 3 * PT + n
                pe.wait_ge(o_norm.sem, o_norm.at(i, n + 1))
                pe.wait_ge(misc.sem, misc.at(i, use + 1 - 2))
                for g in range(2):
                    mm = pe.transpose(bank[6 + use % 2][:, g * P:(g + 1) * P], oc[:, n % 2, g * P:(g + 1) * P], ident)
                mm.then_inc(o_tr.sem, 1)

            def attend(i):
                pe.wait_ge(x_cop.sem, x_cop.at(i, 0))
                pe.wait_ge(hid.sem, hid.at(i, 0))
                turn_keys(i, 0)
                for s in range(STEPS + 4):
                    if s < STEPS:
                        scores(i, s)
                    if s == 4:
                        turn_keys(i, 1)
                    if 2 <= s < STEPS + 2:
                        turn_probs(i, s - 2)
                    if 3 <= s < STEPS + 3:
                        weigh_values(i, s - 3)
                    if s >= 7 and (s - 7) % 4 == 0:
                        turn_outputs(i, (s - 7) // 4)

            def columns_of(i, weights, moving, first_bank, done):
                for m in range(KD):
                    for k in range(KD):
                        mm = pe.matmul(bank[first_bank + m // 2][:, (m % 2) * TT:(m % 2 + 1) * TT],
                                       weights[:, k, m * P:(m + 1) * P], moving[:, k, :], start=(k == 0), stop=(k == KD - 1))
                    if m % 2:
                        mm.then_inc(done.sem, 1)

            def self_attention(i):
                pe.wait_ge(misc.sem, misc.at(i, 3 * PT + BT))
                pe.wait_ge(masked.sem, masked.at(i, STEPS))
                columns_of(i, w_c_o, o_t, 0, y_done)
                pe.wait_ge(y_act.sem, y_act.at(i, 1))
                pe.wait_ge(y_dve.sem, y_dve.at(i, 1))
                probs_copied(pe, i, STEPS - 2)
                probs_copied(pe, i, STEPS - 1)
                columns_of(i, w_a_q, y_t, 2, qa_done)
                pe.wait_ge(o_norm.sem, o_norm.at(i, BT))
                columns_of(i, w_a_k, y_t, 4, ka_done)
                pe.wait_ge(qa_act.sem, qa_act.at(i, 1))
                pe.wait_ge(qa_dve.sem, qa_dve.at(i, 1))
                pe.wait_ge(ka_act.sem, ka_act.at(i, 1))
                pe.wait_ge(ka_dve.sem, ka_dve.at(i, 1))
                for j in range(PT):
                    for h in range(HP):
                        for b in range(2):
                            n = 2 * j + b
                            mm = pe.matmul(bank[(6, 0)[j] + h // 4][:, (h % 4) * P + b * T:(h % 4) * P + (b + 1) * T],
                                           qa_blk[:, h // 2, n, 2 * (h % 2):2 * (h % 2) + 2, :],
                                           ka_t[:, h // 2, n * T:(n + 1) * T], start=True, stop=True)
                    mm.then_inc(sa_done.sem, 1)
                for j in range(PT):
                    for k in range(KD):
                        mm = pe.matmul(bank[2 + j][:], y_t[:, k, j * P:(j + 1) * P], w_a_v[:, k, :], start=(k == 0), stop=(k == KD - 1))
                    mm.then_inc(va_done.sem, 1)
                for j in range(PT):
                    pe.wait_ge(sa_exp.sem, sa_exp.at(i, j + 1))
                    if j == 1:
                        pe.wait_ge(sa_mask.sem, sa_mask.at(i, 4))
                    for h in range(HP):
                        mm = pe.transpose(bank[(4, 0)[j] + h // 4][:, (h % 4) * P:(h % 4 + 1) * P], pa[:, j, h], ident)
                    mm.then_inc(pa_tr.sem, 1)
                    pe.wait_ge(pa_cop.sem, pa_cop.at(i, j + 1))
                    pe.wait_ge(va_cop.sem, va_cop.at(i, j + 1))
                    if j == 0:
                        pe.wait_ge(sa_mask.sem, sa_mask.at(i, 2))
                    else:
                        pe.wait_ge(va_cop.sem, va_cop.at(i, 2))
                    for h in range(HP):
                        mm = pe.matmul(bank[(6, 2)[j] + h // 4][:, (h % 4) * P:(h % 4 + 1) * P], pa_t[:, j, h, :],
                                       va[:, j, :, h * T:(h + 1) * T], start=True, stop=True)
                    mm.then_inc(pva.sem, 1)
                for j in range(PT):
                    pe.wait_ge(oa_norm.sem, oa_norm.at(i, j + 1))
                    if j == 0:
                        pe.wait_ge(pa_cop.sem, pa_cop.at(i, 1))
                    for c in range(4):
                        mm = pe.transpose(bank[(4, 6)[j]][:, c * P:(c + 1) * P], oa[:, j, c // 2, c % 2], ident)
                    mm.then_inc(oa_tr.sem, 1)
                for j in range(PT):
                    pe.wait_ge(oa_cop.sem, oa_cop.at(i, j + 1))
                    for k in range(KD):
                        mm = pe.matmul(bank[(5, 7)[j]][:], oa_t[:, j, k, :], w_a_o[:, k, :], start=(k == 0), stop=(k == KD - 1))
                    mm.then_inc(z_done.sem, 1)

            def experts(i):
                for j in range(PT):
                    pe.wait_ge(resid.sem, resid.at(i, j + 1))
                    if j == 0:
                        pe.wait_ge(pa_cop.sem, pa_cop.at(i, 2))
                    else:
                        pe.wait_ge(oa_norm.sem, oa_norm.at(i, 2))
                    for k in range(KD):
                        mm = pe.transpose(bank[(0, 2)[j]][:, k * P:(k + 1) * P], xh[:, j, k * P:(k + 1) * P], ident)
                    mm.then_inc(x_tr.sem, 1)
                for j in range(PT):
                    pe.wait_ge(x_cop.sem, x_cop.at(i, j + 1))
                    for b in range(2):
                        pe.wait_ge(we_loaded[2 * j + b], i * 16 + 16)
                    for k in range(KD):
                        for b in range(2):
                            mm = pe.matmul(bank[(1, 3)[j]][64 * b:64 * b + 64, :], x_t[:, j, k, b * T:(b + 1) * T],
                                           w_exp[:, 2 * j + b, k, :], start=(k == 0), stop=(k == KD - 1))
                    mm.then_inc(c_done.sem, 1)

            with pe.Fori(0, TURNS) as i:
                attend(i)
                self_attention(i)
                experts(i)

            pe.wait_ge(sc_cop.sem, sc_cop.at(TURNS, 0))
            pe.wait_ge(x_cop.sem, x_cop.at(TURNS, 0))
            pe.transpose(bank[0][0:PAIRS, 0:P], score, ident).then_inc(s_sct, 1)

            def turn_rows(n, use):
                pe.wait_ge(fh_ready.sem, fh_ready.at(0, use + 1))
                if use == 0:
                    pe.wait_ge(hid.sem, hid.at(TURNS, 0))
                if use >= 2:
                    pe.wait_ge(fo_cop.sem, fo_cop.at(0, FH))
                for k in range(KD):
                    mm = pe.transpose(bank[1 + n][:, k * P:(k + 1) * P], fh[:, n, k * P:(k + 1) * P], ident)
                mm.then_inc(fh_tr.sem, 1)

            def turn_heads(c, n):
                use = 2 * c + n
                pe.wait_ge(f_rope.sem, f_rope.at(0, use + 1))
                if use >= 4:
                    pe.wait_ge(fq_cop.sem, fq_cop.at(0, use + 1 - 4))
                else:
                    pe.wait_ge(fh_cop.sem, fh_cop.at(0, 2))
                    pe.wait_ge(s_pick, 1)
                for h in range(4):
                    mm = pe.transpose(bank[use % 4][:, h * P:(h + 1) * P], fq[:, n, c * 512 + h * P:c * 512 + (h + 1) * P], ident)
                mm.then_inc(fq_tr.sem, 1)

            for n in range(SN):
                turn_rows(n, n)
            for c in range(NQKV):
                pe.wait_ge(r_landed[c % RING], 16 * (c // RING + 1))
                for n in range(SN):
                    use = 2 * c + n
                    if c == 0:
                        pe.wait_ge(fh_cop.sem, fh_cop.at(0, n + 1))
                    if use >= 4:
                        pe.wait_ge(fq_bias.sem, fq_bias.at(0, use + 1 - 4))
                    for k in range(KD):
                        mm = pe.matmul(bank[4 + use % 4][:], fh_t[:, k, n * P:(n + 1) * P], ring[:, c % RING, k, :], start=(k == 0), stop=(k == KD - 1))
                    mm.then_inc(fq_mm.sem, 1)
                if 2 <= c < 8:
                    for n in range(SN):
                        turn_heads(c - 2, n)
            def f_scores(t):
                h, n = t // 2, t % 2
                if t < 4:
                    pe.wait_ge(fq_cop.sem, fq_cop.at(0, 12))
                    pe.wait_ge(fq_bias.sem, fq_bias.at(0, 16))
                if t >= 2:
                    pe.wait_ge(fmask.sem, fmask.at(0, t + 1 - 2))
                pe.matmul(bank[t % 2][:, 0:(n + 1) * P], fq_t[:, h, n * P:(n + 1) * P], fk_t[:, h // 2, 0:(n + 1) * P],
                          start=True, stop=True).then_inc(fs.sem, 1)

            def f_turn(t):
                n = t % 2
                pe.wait_ge(fnorm.sem, fnorm.at(0, t + 1))
                if t >= 2:
                    pe.wait_ge(fp_cop.sem, fp_cop.at(0, t + 1 - 2))
                for c in range(n + 1):
                    mm = pe.transpose(bank[2 + t % 2][:, c * P:(c + 1) * P], fp[:, t % 4, c * P:(c + 1) * P], ident)
                mm.then_inc(fp_tr.sem, 1)

            def f_weigh(t):
                h, n = t // 2, t % 2
                pe.wait_ge(fp_cop.sem, fp_cop.at(0, t + 1))
                if h >= 4 and n == 0:
                    pe.wait_ge(fo_cop.sem, fo_cop.at(0, h + 1 - 4))
                for c in range(n + 1):
                    v0 = (FH + FKV) * FHD + (h // 2) * FHD
                    mm = pe.matmul(bank[4 + h % 4][:, n * P:(n + 1) * P], fq[:, c, v0:v0 + FHD], fp_t[:, t % 2, c * P:(c + 1) * P],
                                   start=(c == 0), stop=(c == n))
                mm.then_inc(fpv.sem, 1)

            for t in range(2 * FH + 3):
                if t < 2 * FH:
                    f_scores(t)
                if 2 <= t < 2 * FH + 2:
                    f_turn(t - 2)
                if t >= 3:
                    f_weigh(t - 3)
            pe.wait_ge(fo_cop.sem, fo_cop.at(0, FH))
            for h in range(FH):
                c = NQKV + h // 4
                pe.wait_ge(r_landed[c % RING], 16 * (c // RING + 1))
                for n in range(SN):
                    mm = pe.matmul(bank[6 + n][:], fo_t[:, h, n * P:(n + 1) * P], ring[:, c % RING, h % 4, :], start=(h == 0), stop=(h == FH - 1))
                if h % 4 == 3:
                    mm.then_inc(fwo.sem, 1)
            for n in range(SN):
                turn_rows(n, 2 + n)
            for f in range(NIN):
                c = NQKV + 4 + 2 * (f // 4)
                if f == 0:
                    pe.wait_ge(fh_cop.sem, fh_cop.at(0, 4))
                    pe.wait_ge(fo_cop.sem, fo_cop.at(0, FH))
                for w in range(2):
                    pe.wait_ge(r_landed[(c + w) % RING], 16 * ((c + w) // RING + 1))
                if f >= 4:
                    pe.wait_ge(g_act.sem, g_act.at(0, f + 1 - 4))
                for w in range(2):
                    for k in range(KD):
                        mm = pe.matmul(bank[(3, 4, 5, 0)[f % 4]][:, w * S:(w + 1) * S], ring[:, (c + w) % RING, k, (f % 4) * P:(f % 4 + 1) * P],
                                       fh_t[:, k, :], start=(k == 0), stop=(k == KD - 1))
                mm.then_inc(g_done.sem, 1)
            pe.wait_ge(fh_ready.sem, fh_ready.at(0, 4))
            for f in range(NIN):
                c = NQKV + 12 + f // 4
                pe.wait_ge(r_landed[c % RING], 16 * (c // RING + 1))
                pe.wait_ge(g_act.sem, g_act.at(0, f + 1))
                for n in range(SN):
                    mm = pe.matmul(bank[6 + n][:], act_t[:, f, n * P:(n + 1) * P], ring[:, c % RING, f % 4, :], start=(f == 0), stop=(f == NIN - 1))
                if f % 4 == 3:
                    mm.then_inc(f_down.sem, 1)

        @block.scalar
        def _(act):
            for g in (squared, rooted, q_copied, misc, exped, p_act, y_act, qa_act, ka_act, sa_exp, pa_cop, oa_cop, x_cop):
                act.sem_inc(g.sem, g.prime)

            act.wait_ge(s_early, 16 * 7)
            with act.Fori(0, PAIRS // 2) as i:
                for u in range(2):
                    t = i * 2 + u
                    act.wait_ge(proj.sem, proj.at(t, 1))
                    act.wait_ge(summed.sem, summed.at(t, 1 - 2))
                    nc.scalar.activation(sq[:, u, 0:CH].rearrange("p h d -> p (h d)"), bank[2 * u][:], ACT.Square)
                    nc.scalar.activation(sq[:, u, CH:QK].rearrange("p h d -> p (h d)"), bank[2 * u + 1][:, 0:CG * CHD], ACT.Square)
                    act.wait_ge(kv_stored[u], i * 16 + 16)
                    nc.scalar.copy(kvn[:, u, CG * CHD:], bank[2 * u + 1][:, CG * CHD:]).then_inc(squared.sem, 1)
                    act.wait_ge(summed.sem, summed.at(t, 1))
                    act.wait_ge(inverted.sem, inverted.at(t, 1 - 2))
                    nc.scalar.activation(root[:, u], ssum[:, u], ACT.Sqrt, bias=eps, scale=1.0 / CHD).then_inc(rooted.sem, 1)
                    act.wait_ge(q_tr.sem, q_tr.at(t, 1))
                    act.wait_ge(q_stored[u], i * 16 + 16)
                    nc.scalar.copy(q_out[:, u].rearrange("p (b n t) -> p n b t", b=2, n=4),
                                   bank[4 + u][:].rearrange("p (n b t) -> p n b t", n=4, b=2)).then_inc(q_copied.sem, 1)

            act.wait_ge(s_weights, 16 * 11)
            act.wait_ge(s_zero, 4)
            for u in range(2):
                act.wait_ge(q_stored[u], 16 * (PAIRS // 2 + 1))
                act.wait_ge(kv_stored[u], 16 * (PAIRS // 2 + 1))

            def copy_keys(i, j):
                act.wait_ge(scored.sem, scored.at(i, 8 * (j + 1) - STEPS))
                act.wait_ge(pva.sem, pva.at(i, 0))
                for n in range(3):
                    use = 3 * j + n
                    act.wait_ge(k_tr.sem, k_tr.at(i, use + 1))
                    w = 4 * P if n < 2 else 2 * P
                    flat = k_t[:, j].rearrange("p g n -> p (g n)")
                    nc.scalar.copy(flat[:, n * 4 * P:n * 4 * P + w], bank[6 + use % 2][:, 0:w]).then_inc(misc.sem, 1)

            def exp_scores(i, s):
                n, b, g = s // 4, s // 4 % 2, s % 4
                act.wait_ge(negated.sem, negated.at(i, s + 1))
                if g == 0:
                    act.wait_ge(recd.sem, recd.at(i, n + 1 - 2))
                cols = pc[:, 2 * b + g % 2, b * T:b * T + SPAN]
                nc.scalar.activation(cols, cols, ACT.Exp, bias=neg_c[:, s % 4:s % 4 + 1], scale=1.0 / 16.0,
                                     accum_out=sum_c[:, b, g:g + 1]).then_inc(exped.sem, 1)

            def copy_probs(i, s):
                act.wait_ge(p_tr.sem, p_tr.at(i, s + 1))
                act.wait_ge(pv_done.sem, pv_done.at(i, s + 1 - 2))
                nc.scalar.copy(pc_t[:, s % 2], bank[2 + s % 2][:, 0:3 * P]).then_inc(p_act.sem, 1)

            def copy_outputs(i, n):
                use = 3 * PT + n
                act.wait_ge(o_tr.sem, o_tr.at(i, n + 1))
                act.wait_ge(z_done.sem, z_done.at(i, 0))
                nc.scalar.copy(o_t[:, :, n * T:(n + 1) * T].rearrange("p (g c) t -> p g c t", g=2),
                               bank[6 + use % 2][:, 0:2 * P].rearrange("p (g c t) -> p g c t", g=2, c=2)).then_inc(misc.sem, 1)

            def attend(i):
                copy_keys(i, 0)
                for s in range(STEPS + 4):
                    if s == 4:
                        copy_keys(i, 1)
                    if s < STEPS:
                        exp_scores(i, s)
                    if 2 <= s < STEPS + 2 and (s - 2) % 4 == 3:
                        copy_probs(i, s - 2)
                    if s >= 7 and (s - 7) % 4 == 0:
                        copy_outputs(i, (s - 7) // 4)

            def self_attention(i):
                act.wait_ge(y_done.sem, y_done.at(i, 2))
                nc.scalar.copy(y_t[:, 2:4].rearrange("p m t -> p (m t)"), bank[1][:]).then_inc(y_act.sem, 1)
                act.wait_ge(qa_done.sem, qa_done.at(i, 1))
                for m in range(2):
                    for h in range(4):
                        r = slice(32 * h, 32 * h + 32)
                        ins = nc.scalar.activation(qa_blk[r, m, :, h, :], bank[2][r, m * TT:(m + 1) * TT].rearrange("p (b t) -> p b t", b=BT),
                                                   ACT.Identity, bias=bq[r, m:m + 1])
                ins.then_inc(qa_act.sem, 1)
                act.wait_ge(ka_done.sem, ka_done.at(i, 1))
                for m in range(2):
                    ins = nc.scalar.activation(ka_t[:, m, :], bank[4][:, m * TT:(m + 1) * TT], ACT.Identity, bias=bk[:, m:m + 1])
                ins.then_inc(ka_act.sem, 1)
                for j in range(PT):
                    act.wait_ge(sa_sub.sem, sa_sub.at(i, j + 1))
                    nc.scalar.activation(pa[:, j], pa[:, j], ACT.Exp).then_inc(sa_exp.sem, 1)
                for j in range(PT):
                    act.wait_ge(pa_tr.sem, pa_tr.at(i, j + 1))
                    for half in range(2):
                        ins = nc.scalar.copy(pa_t[:, j, 4 * half:4 * half + 4].rearrange("p h n -> p (h n)"), bank[(4, 0)[j] + half][:])
                    ins.then_inc(pa_cop.sem, 1)
                for j in range(PT):
                    act.wait_ge(oa_tr.sem, oa_tr.at(i, j + 1))
                    for c in range(2):
                        ins = nc.scalar.copy(oa_t[:, j, 2 * c:2 * c + 2].rearrange("p h (b t) -> p b h t", b=2),
                                             bank[(4, 6)[j]][:, 2 * c * P:2 * (c + 1) * P].rearrange("p (b h t) -> p b h t", b=2, h=2))
                    ins.then_inc(oa_cop.sem, 1)
                for j in range(PT):
                    act.wait_ge(x_tr.sem, x_tr.at(i, j + 1))
                    nc.scalar.copy(x_t[:, j].rearrange("p k n -> p (k n)"), bank[(0, 2)[j]][:]).then_inc(x_cop.sem, 1)

            with act.Fori(0, TURNS) as i:
                attend(i)
                self_attention(i)

            def root_mean_square(n, use):
                source = sel[:, n, D:] if use < 2 else x1[:, n]
                nc.scalar.activation(fjunk, source, ACT.Square, accum_out=small[:, use:use + 1]).then_inc(s_rms, 1)
                act.wait_ge(s_rms, 2 * use + 1)
                nc.scalar.activation(small[:, 4 + use:5 + use], small[:, use:use + 1], ACT.Sqrt, bias=eps, scale=1.0 / D).then_inc(s_rms, 1)

            def copy_rows(n, use):
                act.wait_ge(fh_tr.sem, fh_tr.at(0, use + 1))
                nc.scalar.copy(fh_t[:, :, n * P:(n + 1) * P], bank[1 + n][:].rearrange("p (k n) -> p k n", k=KD)).then_inc(fh_cop.sem, 1)

            act.wait_ge(s_sel, 64)
            for n in range(SN):
                if n == 1:
                    act.wait_ge(s_rms, 2)
                root_mean_square(n, n)
            for n in range(SN):
                copy_rows(n, n)
            for c in range(6):
                for n in range(SN):
                    act.wait_ge(fq_tr.sem, fq_tr.at(0, 2 * c + n + 1))
                    dst = fq_t[:, 4 * c:4 * c + 4, n * P:(n + 1) * P] if c < 4 else fk_t[:, 4 * (c - 4):4 * (c - 4) + 4, n * P:(n + 1) * P]
                    nc.scalar.copy(dst, bank[(2 * c + n) % 4][:].rearrange("p (h n) -> p h n", h=4)).then_inc(fq_cop.sem, 1)
            for t in range(2 * FH + 4):
                if t < 2 * FH:
                    n = t % 2
                    act.wait_ge(fneg.sem, fneg.at(0, t + 1))
                    if t >= 4:
                        act.wait_ge(frec.sem, frec.at(0, t + 1 - 4))
                    nc.scalar.activation(fp[:, t % 4, 0:(n + 1) * P], fp[:, t % 4, 0:(n + 1) * P], ACT.Exp,
                                         bias=small[:, 20 + t % 4:21 + t % 4], scale=float(FHD) ** -0.5,
                                         accum_out=small[:, 24 + t % 4:25 + t % 4]).then_inc(fexp.sem, 1)
                if t >= 4 and t % 2 == 0:
                    h = (t - 4) // 2
                    act.wait_ge(fpv.sem, fpv.at(0, 2 * h + 2))
                    nc.scalar.copy(fo_t[:, h], bank[4 + h % 4][:, 0:S]).then_inc(fo_cop.sem, 1)
            for n in range(SN):
                act.wait_ge(f_x1.sem, f_x1.at(0, n + 1))
                act.wait_ge(s_rms, 2 * (2 + n))
                root_mean_square(n, 2 + n)
            for n in range(SN):
                copy_rows(n, 2 + n)
            for n in range(SN):
                nc.scalar.activation(small[:, 12 + n:13 + n], small[:, 8 + n:9 + n], ACT.Exp, scale=-1.0).then_inc(s_esc, 1)
            for f in range(NIN):
                act.wait_ge(g_done.sem, g_done.at(0, f + 1))
                if f >= 2:
                    act.wait_ge(g_act.sem, g_act.at(0, f + 1 - 2))
                nc.scalar.activation(e_g[:, f % 2], bank[(3, 4, 5, 0)[f % 4]][:, 0:S], ACT.Exp, scale=-1.0).then_inc(g_exp.sem, 1)

        @block.vector
        def _(dve):
            for g in (summed, inverted, normed, scaled, turned_v, cosd, roped, same_p, src_v, masked, negated, p_dve, recd, o_norm,
                      y_dve, qa_dve, ka_dve, sa_mask, sa_max, sa_sum, sa_rec, va_cop, oa_norm, resid, hid, rscore, sc_cop):
                dve.sem_inc(g.sem, g.prime)

            steps = [0]

            def step(ins):
                steps[0] += 1
                ins.then_inc(s_pre, 1)
                dve.wait_ge(s_pre, steps[0])

            dve.wait_ge(s_early, 16 * 7)
            step(nc.vector.tensor_copy(posf, len_all[:, 0:PAIRS]))
            step(nc.vector.tensor_scalar(pos_idx, posf, seq_base[:, 0:1], None, ALU.add))
            step(nc.vector.tensor_scalar(first_seen, len_all[:, PAIRS:], -1.0, float(WINDOW), ALU.mult, ALU.add))
            step(nc.vector.tensor_copy(blocks[0:B], blocks_i[0:B]))
            step(nc.vector.tensor_scalar(lens_i[0:B, 1:2], lens_i[0:B, 0:1], 4, None, ALU.logical_shift_right))
            step(nc.vector.tensor_scalar(lens_i[0:B, 2:3], lens_i[0:B, 0:1], BLOCK - 1, None, ALU.bitwise_and))
            for k in range(4):
                step(nc.vector.tensor_scalar(lens_i[0:B, 3 + k:4 + k], lens_i[0:B, 0:1], k, 1, ALU.logical_shift_right, ALU.bitwise_and))
            step(nc.vector.tensor_copy(lens[0:B, 0:7], lens_i[0:B, 0:7]))
            iota_blk = k32[0:B, 0:NBLK]
            iota_slot = k32[0:B, NBLK:NBLK + WSLOTS]
            iota_new = k32[0:B, NBLK + WSLOTS:NBLK + WSLOTS + NSLOTS * BLOCK]
            token1 = k32[0:B, NBLK + WSLOTS + NSLOTS * BLOCK:NBLK + WSLOTS + NSLOTS * BLOCK + 1]
            iota_off = k32[0:B, NBLK + WSLOTS + NSLOTS * BLOCK + 1:]
            step(nc.vector.tensor_scalar(slot_no[0:B], iota_slot, lens[0:B, 1:2], float(-WINDOW // BLOCK), ALU.add, ALU.add))
            for k in range(WSLOTS):
                step(nc.vector.scalar_tensor_tensor(out=hit[0:B], in0=iota_blk, scalar=slot_no[0:B, k:k + 1], in1=blocks[0:B],
                                                    op0=ALU.is_equal, op1=ALU.mult, accum_out=win[0:B, k:k + 1]))
            step(nc.vector.tensor_scalar(tok[0:B, 0], iota_new, lens[0:B, 2:3], None, ALU.subtract))
            step(nc.vector.tensor_scalar(tok[0:B, 1], tok[0:B, 0], 0.0, None, ALU.is_ge))
            step(nc.vector.scalar_tensor_tensor(out=tok[0:B, 1], in0=tok[0:B, 0], scalar=float(T), in1=tok[0:B, 1], op0=ALU.is_lt, op1=ALU.mult))
            step(nc.vector.scalar_tensor_tensor(out=tok[0:B, 2], in0=tok[0:B, 0], scalar=token1, in1=tok[0:B, 1], op0=ALU.add, op1=ALU.mult))
            assert steps[0] == PRE_WIN
            step(nc.vector.scalar_tensor_tensor(out=al[0:B, 0, 0].rearrange("p (s o) -> p s o", o=BLOCK),
                                                in0=win[0:B].unsqueeze(2).to_broadcast([B, WSLOTS, BLOCK]), scalar=float(BLOCK),
                                                in1=iota_off.unsqueeze(1).to_broadcast([B, WSLOTS, BLOCK]), op0=ALU.mult, op1=ALU.add))
            step(nc.vector.tensor_scalar(scale1, scale1, 1.0, None, ALU.add))
            assert steps[0] == PRE_ALL

            dve.wait_ge(s_rope, 16 * PAIRS)
            dve.wait_ge(s_win_in, 48)
            with dve.Fori(0, PAIRS // 2) as i:
                dve.wait_ge(prod_p.sem, prod_p.at(i, 0))
                nc.vector.tensor_tensor(same[0:GP], blk_w[0:GP], blk_r[0:GP, bass.ds(i, 1)].to_broadcast([GP, WRITERS]),
                                        ALU.is_equal).then_inc(same_p.sem, 1)
                for u in range(2):
                    t = i * 2 + u
                    dve.wait_ge(squared.sem, squared.at(t, 1))
                    nc.vector.tensor_reduce(ssum[:, u], sq[:, u], AX.X, ALU.add).then_inc(summed.sem, 1)
                    dve.wait_ge(rooted.sem, rooted.at(t, 1))
                    nc.vector.reciprocal(inv[:, u], root[:, u]).then_inc(inverted.sem, 1)
                    dve.wait_ge(inverted.sem, inverted.at(t, 1))
                    dve.wait_ge(turned_p.sem, turned_p.at(t, 1 - 2))
                    for lo, hi, half in ((0, CH, 0), (CH, QK, 1)):
                        nc.vector.tensor_tensor(qk[:, u, lo:hi].rearrange("p h a d -> p h (a d)"),
                                                bank[2 * u + half][:, 0:(hi - lo) * CHD].rearrange("p (h d) -> p h d", h=hi - lo),
                                                inv[:, u, lo:hi].unsqueeze(2).to_broadcast([P, hi - lo, CHD]), ALU.mult).then_inc(normed.sem, 1)
                    dve.wait_ge(normed.sem, normed.at(t, 2))
                    flat = qk[:, u].rearrange("p h a d -> p h (a d)")
                    nc.vector.tensor_tensor(flat, flat, scale1, ALU.mult).then_inc(scaled.sem, 1)
                    dve.wait_ge(scaled.sem, scaled.at(t, 1))
                    cos = rope[:, bass.ds(t, 1), 0:32].unsqueeze(2).to_broadcast([P, QK, 2, 32])
                    sin = rope[:, bass.ds(t, 1), 64:96].to_broadcast([P, QK, 32])
                    nc.vector.tensor_tensor(qk_cos[:, u], qk[:, u], cos, ALU.mult).then_inc(cosd.sem, 1)
                    nc.vector.tensor_tensor(turned[:, u, :, 1, :], qk[:, u, :, 0, :], sin, ALU.mult).then_inc(turned_v.sem, 1)
                    dve.wait_ge(cosd.sem, cosd.at(t, 1))
                    dve.wait_ge(turned_v.sem, turned_v.at(t, 1))
                    dve.wait_ge(turned_p.sem, turned_p.at(t, 1))
                    dve.wait_ge(q_tr.sem, q_tr.at(t, 1 - 2))
                    nc.vector.tensor_tensor(qr[:, u], qk_cos[:, u, 0:CH].rearrange("p h a d -> p (h a d)"),
                                            turned[:, u, 0:CH].rearrange("p h a d -> p (h a d)"), ALU.add).then_inc(roped.sem, 1)
                    dve.wait_ge(kv_stored[u], i * 16 + 16)
                    nc.vector.tensor_tensor(kvn[:, u, 0:CG * CHD], qk_cos[:, u, CH:].rearrange("p h a d -> p (h a d)"),
                                            turned[:, u, CH:].rearrange("p h a d -> p (h a d)"), ALU.add).then_inc(roped.sem, 1)
                dve.wait_ge(prod_p.sem, prod_p.at(i, 1))
                nc.vector.tensor_reduce(src[0:GP, bass.ds(i, 1)].rearrange("p a o -> p (a o)"), prod[0:GP], AX.X, ALU.max).then_inc(src_v.sem, 1)

            dve.wait_ge(s_src_in, 16)
            cur, n = 0, WPOS
            for k in (3, 2, 1, 0):
                n -= 1 << k
                here, there = al[0:B, cur], al[0:B, 1 - cur, :, 0:n]
                step(nc.vector.tensor_tensor(there, here[:, :, 1 << k:n + (1 << k)], here[:, :, 0:n], ALU.subtract))
                step(nc.vector.scalar_tensor_tensor(out=there, in0=there, scalar=lens[0:B, 3 + k:4 + k], in1=here[:, :, 0:n], op0=ALU.mult, op1=ALU.add))
                cur = 1 - cur
            rows, last = al[0:B, cur, 0, 0:SPAN], al[0:B, cur, 1, 0:SPAN]
            step(nc.vector.tensor_scalar(idx_f[0:B, 3], last, 0.0, SKIP, ALU.is_gt, ALU.mult))
            step(nc.vector.tensor_tensor(idx_f[0:B, 0], rows, idx_f[0:B, 3], ALU.add))
            step(nc.vector.tensor_scalar(idx_f[0:B, 3], last, 0.0, SKIP, ALU.is_equal, ALU.mult))
            step(nc.vector.scalar_tensor_tensor(out=idx_f[0:B, 1], in0=last, scalar=-1.0, in1=idx_f[0:B, 3], op0=ALU.add, op1=ALU.add))
            assert steps[0] == PRE_IDX
            dve.wait_ge(s_idx_t, 1)
            nc.vector.tensor_copy(cache_idx.rearrange("p h b -> p (h b)"), bank[0][:, 0:2 * B]).then_inc(s_idx, 1)
            nc.vector.tensor_copy(over_idx.rearrange("p h b -> p (h b)"), bank[0][:, 2 * B:4 * B]).then_inc(s_idx, 1)
            nc.vector.tensor_copy(fresh_idx, bank[0][:, 4 * B:4 * B + PAIRS]).then_inc(s_idx, 1)

            dve.wait_ge(s_weights, 16 * 11)
            dve.wait_ge(s_zero, 4)
            for u in range(2):
                dve.wait_ge(q_stored[u], 16 * (PAIRS // 2 + 1))
                dve.wait_ge(kv_stored[u], 16 * (PAIRS // 2 + 1))

            def mask_scores(i, s):
                n, b, g = s // 4, s // 4 % 2, s % 4
                dve.wait_ge(scored.sem, scored.at(i, s + 1))
                if g == 0:
                    dve.wait_ge(masks.sem, masks.at(i, n + 1))
                dve.wait_ge(p_tr.sem, p_tr.at(i, s + 1 - 2))
                dve.wait_ge(exped.sem, exped.at(i, s + 1 - 4))
                dve.sem_inc(s_vector_passed, 1)
                nc.vector.tensor_tensor_reduce(out=pc[:, 2 * b + g % 2, b * T:b * T + SPAN], in0=bank[s % 2][:, 0:SPAN], in1=mk[:, b],
                                               scale=1.0, scalar=-3.0e38, op0=ALU.add, op1=ALU.max,
                                               accum_out=top_c[:, s % 4:s % 4 + 1]).then_inc(masked.sem, 1)
                dve.wait_ge(masked.sem, masked.at(i, s + 1))
                nc.vector.tensor_scalar(neg_c[:, s % 4:s % 4 + 1], top_c[:, s % 4:s % 4 + 1], -1.0 / 16.0, None, ALU.mult).then_inc(negated.sem, 1)

            def copy_probs(i, s):
                dve.wait_ge(p_tr.sem, p_tr.at(i, s + 1))
                dve.wait_ge(pv_done.sem, pv_done.at(i, s + 1 - 2))
                nc.vector.tensor_copy(pc_t[:, s % 2], bank[2 + s % 2][:, 0:3 * P]).then_inc(p_dve.sem, 1)

            def norm_outputs(i, n):
                dve.wait_ge(exped.sem, exped.at(i, 4 * n + 4))
                nc.vector.reciprocal(rec_c[:, n % 2], sum_c[:, n % 2]).then_inc(recd.sem, 1)
                dve.wait_ge(recd.sem, recd.at(i, n + 1))
                dve.wait_ge(pv_done.sem, pv_done.at(i, 4 * n + 4))
                dve.wait_ge(o_tr.sem, o_tr.at(i, n + 1 - 2))
                nc.vector.tensor_tensor(oc[:, n % 2].rearrange("p (g d) -> p g d", g=CG),
                                        bank[4 + n % 2][:, 0:CG * CHD].rearrange("p (g d) -> p g d", g=CG),
                                        rec_c[:, n % 2].unsqueeze(2).to_broadcast([P, CG, CHD]), ALU.mult).then_inc(o_norm.sem, 1)

            def attend(i):
                for s in range(STEPS + 3):
                    if s < STEPS:
                        mask_scores(i, s)
                    if 2 <= s < STEPS + 2 and (s - 2) % 4 != 3:
                        copy_probs(i, s - 2)
                    if s >= 6 and (s - 6) % 4 == 0:
                        norm_outputs(i, (s - 6) // 4)

            def self_attention(i):
                dve.wait_ge(y_done.sem, y_done.at(i, 1))
                dve.wait_ge(c_done.sem, c_done.at(i, 0))
                nc.vector.tensor_copy(y_t[:, 0:2].rearrange("p m t -> p (m t)"), bank[0][:]).then_inc(y_dve.sem, 1)
                dve.wait_ge(qa_done.sem, qa_done.at(i, 2))
                for m in range(2):
                    for h in range(4):
                        r = slice(32 * h, 32 * h + 32)
                        ins = nc.vector.tensor_scalar(qa_blk[r, 2 + m, :, h, :], bank[3][r, m * TT:(m + 1) * TT].rearrange("p (b t) -> p b t", b=BT),
                                                      bq[r, 2 + m:3 + m], None, ALU.add)
                ins.then_inc(qa_dve.sem, 1)
                dve.wait_ge(ka_done.sem, ka_done.at(i, 2))
                for m in range(2):
                    ins = nc.vector.tensor_scalar(ka_t[:, 2 + m, :], bank[5][:, m * TT:(m + 1) * TT], bk[:, 2 + m:3 + m], None, ALU.add)
                ins.then_inc(ka_dve.sem, 1)
                for j in range(PT):
                    dve.wait_ge(sa_done.sem, sa_done.at(i, j + 1))
                    for half in range(2):
                        nc.vector.scalar_tensor_tensor(out=pa[:, j, 4 * half:4 * half + 4].rearrange("p h b t -> p (h b) t"),
                                                       in0=bank[(6, 0)[j] + half][:].rearrange("p (n t) -> p n t", t=T), scalar=float(AHD) ** -0.5,
                                                       in1=mask_a.unsqueeze(1).to_broadcast([P, 8, T]), op0=ALU.mult, op1=ALU.add).then_inc(sa_mask.sem, 1)
                    dve.wait_ge(sa_mask.sem, sa_mask.at(i, 2 * j + 2))
                    nc.vector.tensor_reduce(top_a[:, j], pa[:, j].rearrange("p h b t -> p (h b) t"), AX.X, ALU.max).then_inc(sa_max.sem, 1)
                for j in range(PT):
                    dve.wait_ge(va_done.sem, va_done.at(i, j + 1))
                    for b in range(2):
                        r = slice(64 * b, 64 * b + 64)
                        ins = nc.vector.tensor_tensor(va[r, j, b, :], bank[2 + j][r, :], bv[r, :], ALU.add)
                    ins.then_inc(va_cop.sem, 1)
                for j in range(PT):
                    dve.wait_ge(sa_exp.sem, sa_exp.at(i, j + 1))
                    nc.vector.tensor_reduce(sum_a[:, j], pa[:, j].rearrange("p h b t -> p (h b) t"), AX.X, ALU.add).then_inc(sa_sum.sem, 1)
                    dve.wait_ge(sa_sum.sem, sa_sum.at(i, j + 1))
                    nc.vector.reciprocal(rec_a[:, j], sum_a[:, j]).then_inc(sa_rec.sem, 1)
                    dve.wait_ge(sa_rec.sem, sa_rec.at(i, j + 1))
                    dve.wait_ge(pva.sem, pva.at(i, j + 1))
                    for c in range(2):
                        for r in range(2):
                            rows_r = slice(64 * r, 64 * r + 64)
                            ins = nc.vector.tensor_tensor(
                                oa[rows_r, j, c].rearrange("p b h d -> p h b d"),
                                bank[(6, 2)[j] + c][rows_r, :].rearrange("p (h b r d) -> p h b r d", b=2, r=2, d=AHD)[:, :, :, r, :],
                                rec_a[rows_r, j, 8 * c:8 * c + 8].rearrange("p (h b) -> p h b", b=2).unsqueeze(3).to_broadcast([64, 4, 2, AHD]), ALU.mult)
                    ins.then_inc(oa_norm.sem, 1)
                for j in range(PT):
                    dve.wait_ge(z_done.sem, z_done.at(i, j + 1))
                    dve.wait_ge(x_bias.sem, x_bias.at(i, j + 1))
                    dve.wait_ge(xh_stored[j], i * 16 + 16)
                    nc.vector.tensor_tensor(xh[:, j, 0:D], bank[(5, 7)[j]][:], xr[:, j], ALU.add).then_inc(resid.sem, 1)
                for j in range(PT):
                    dve.wait_ge(c_done.sem, c_done.at(i, j + 1))
                    dve.wait_ge(be_loaded[j], i * 32 + 32)
                    nc.vector.tensor_tensor(xh[:, j, D:], bank[(1, 3)[j]][:], b_exp[:, j], ALU.add).then_inc(hid.sem, 1)
                    dve.wait_ge(hid.sem, hid.at(i, j + 1))
                    dve.wait_ge(rscore.sem, rscore.at(i, j))
                    dve.wait_ge(sc_cop.sem, sc_cop.at(i, 0))
                    nc.vector.tensor_tensor_reduce(out=junk, in0=xh[:, j, D:], in1=router, scale=1.0, scalar=0.0, op0=ALU.mult, op1=ALU.add,
                                                   accum_out=score_t[:, j:j + 1]).then_inc(rscore.sem, 1)
                dve.wait_ge(rscore.sem, rscore.at(i, PT))
                nc.vector.tensor_copy(score[:, bass.ds(i * PT, PT)], score_t).then_inc(sc_cop.sem, 1)

            with dve.Fori(0, TURNS) as i:
                attend(i)
                self_attention(i)

            picks = [0]

            def pick_step(ins):
                picks[0] += 1
                ins.then_inc(s_pick, 1)
                dve.wait_ge(s_pick, picks[0])

            Q = PAIRS
            for j in range(PT):
                dve.wait_ge(xh_stored[j], 16 * (TURNS + 1))
                dve.wait_ge(out_stored[j], 16 * (TURNS + 1))
            dve.wait_ge(s_sct, 1)
            pick_step(nc.vector.tensor_copy(score_b[0:Q], bank[0][0:Q, 0:P]))
            for b in range(2):
                pick_step(nc.vector.max(top8[0:Q, b], score_b[0:Q, b * T:(b + 1) * T]))
            for b in range(2):
                pick_step(nc.vector.max_index(at8[0:Q, b], top8[0:Q, b], score_b[0:Q, b * T:(b + 1) * T]))
            pick_step(nc.vector.tensor_scalar(neg8[0:Q], at8[0:Q], -1.0, None, ALU.mult))
            for b in range(2):
                pick_step(nc.vector.max(sorted8[0:Q, b], neg8[0:Q, b]))
            pick_step(nc.vector.tensor_scalar(pick8[0:Q, 0], sorted8[0:Q], -1.0, None, ALU.mult))
            for b in range(2):
                pick_step(nc.vector.tensor_scalar(pick8[0:Q, 1, b], sorted8[0:Q, b], -1.0, seq_base[0:Q, 1 + b:2 + b], ALU.mult, ALU.add))
            assert picks[0] == 11

            def norm_rows(n, use):
                dve.wait_ge(s_rms, 2 * (use + 1))
                nc.vector.reciprocal(small[:, 16 + use:17 + use], small[:, 4 + use:5 + use]).then_inc(s_gate, 1)
                dve.wait_ge(s_gate, use + 1 if use < 2 else use + 3)
                if use >= 2:
                    dve.wait_ge(fh_tr.sem, fh_tr.at(0, 2))
                source, weight = (sel[:, n, D:], ln1) if use < 2 else (x1[:, n], ln2)
                nc.vector.scalar_tensor_tensor(out=fh[:, n], in0=source, scalar=small[:, 16 + use:17 + use], in1=weight,
                                               op0=ALU.mult, op1=ALU.mult).then_inc(fh_ready.sem, 1)

            dve.wait_ge(s_sel, 64)
            dve.wait_ge(s_fin, 48)
            for n in range(SN):
                norm_rows(n, n)
            for n in range(SN):
                nc.vector.tensor_tensor_reduce(out=x1[:, n], in0=sel[:, n, D:], in1=router, scale=1.0, scalar=0.0, op0=ALU.mult, op1=ALU.add,
                                               accum_out=small[:, 8 + n:9 + n]).then_inc(s_gate, 1)
            for c in range(NQKV):
                for n in range(SN):
                    use = 2 * c + n
                    x = fq[:, n, c * 512:(c + 1) * 512]
                    dve.wait_ge(fq_mm.sem, fq_mm.at(0, use + 1))
                    nc.vector.tensor_tensor(x, bank[4 + use % 4][:], fbias[:, c * 512:(c + 1) * 512], ALU.add).then_inc(fq_bias.sem, 1)
                    if c < 6:
                        dve.wait_ge(fq_bias.sem, fq_bias.at(0, use + 1))
                        halves = x.rearrange("p (h a d) -> p h a d", a=2, d=64)
                        co, si = fcos[:, n], fsin[:, n].rearrange("p (h a d) -> p h a d", a=2, d=64)
                        nc.vector.tensor_tensor(co.rearrange("p (h d) -> p h d", d=64), x.rearrange("p (h d) -> p h d", d=64),
                                                frope[:, n, 0:64].unsqueeze(1).to_broadcast([P, 8, 64]), ALU.mult)
                        nc.vector.tensor_tensor(si[:, :, 0, :], halves[:, :, 1, :], frope[:, n, 128:192].unsqueeze(1).to_broadcast([P, 4, 64]), ALU.mult)
                        nc.vector.tensor_tensor(si[:, :, 1, :], halves[:, :, 0, :], frope[:, n, 192:256].unsqueeze(1).to_broadcast([P, 4, 64]),
                                                ALU.mult).then_inc(f_sin.sem, 1)
                        dve.wait_ge(f_sin.sem, f_sin.at(0, use + 1))
                        nc.vector.tensor_tensor(x, co, fsin[:, n], ALU.add).then_inc(f_rope.sem, 1)
            for t in range(2 * FH + 3):
                if t < 2 * FH:
                    n, w = t % 2, (t % 2 + 1) * P
                    dve.wait_ge(fs.sem, fs.at(0, t + 1))
                    if t >= 4:
                        dve.wait_ge(fp_tr.sem, fp_tr.at(0, t + 1 - 4))
                    mask = mask_f[:, 1] if n == 0 else mask_f.rearrange("p a n -> p (a n)")
                    nc.vector.tensor_tensor_reduce(out=fp[:, t % 4, 0:w], in0=bank[t % 2][:, 0:w], in1=mask, scale=1.0, scalar=-3.0e38,
                                                   op0=ALU.add, op1=ALU.max, accum_out=small[:, 32 + t % 4:33 + t % 4]).then_inc(fmask.sem, 1)
                    dve.wait_ge(fmask.sem, fmask.at(0, t + 1))
                    nc.vector.tensor_scalar(small[:, 20 + t % 4:21 + t % 4], small[:, 32 + t % 4:33 + t % 4], -float(FHD) ** -0.5, None,
                                            ALU.mult).then_inc(fneg.sem, 1)
                if 1 <= t <= 2 * FH:
                    r = t - 1
                    w = (r % 2 + 1) * P
                    dve.wait_ge(fexp.sem, fexp.at(0, r + 1))
                    nc.vector.reciprocal(small[:, 28 + r % 4:29 + r % 4], small[:, 24 + r % 4:25 + r % 4]).then_inc(frec.sem, 1)
                    dve.wait_ge(frec.sem, frec.at(0, r + 1))
                    nc.vector.tensor_scalar(fp[:, r % 4, 0:w], fp[:, r % 4, 0:w], small[:, 28 + r % 4:29 + r % 4], None, ALU.mult).then_inc(fnorm.sem, 1)
                if 2 <= t < 2 * FH + 2:
                    r = t - 2
                    w = (r % 2 + 1) * P
                    dve.wait_ge(fp_tr.sem, fp_tr.at(0, r + 1))
                    if r >= 2:
                        dve.wait_ge(fpv.sem, fpv.at(0, r + 1 - 2))
                    nc.vector.tensor_copy(fp_t[:, r % 2, 0:w], bank[2 + r % 2][:, 0:w]).then_inc(fp_cop.sem, 1)
            dve.wait_ge(fwo.sem, fwo.at(0, 4))
            for n in range(SN):
                nc.vector.tensor_tensor(x1[:, n], bank[6 + n][:], sel[:, n, D:], ALU.add).then_inc(f_x1.sem, 1)
            for n in range(SN):
                norm_rows(n, 2 + n)
            dve.wait_ge(s_esc, 2)
            nc.vector.tensor_scalar(small[:, 12:14], small[:, 12:14], 1.0, None, ALU.add).then_inc(s_gate, 1)
            dve.wait_ge(s_gate, 7)
            nc.vector.reciprocal(small[:, 14:16], small[:, 12:14]).then_inc(s_gate, 1)
            dve.wait_ge(s_gate, 8)
            nc.vector.tensor_scalar(small[:, 36:38], small[:, 14:16], -1.0, 1.0, ALU.mult, ALU.add).then_inc(s_gate, 1)
            for f in range(NIN):
                gb = bank[(3, 4, 5, 0)[f % 4]]
                r = r_g[:, f % 2]
                dve.wait_ge(g_exp.sem, g_exp.at(0, f + 1))
                nc.vector.tensor_scalar(r, e_g[:, f % 2], 1.0, None, ALU.add).then_inc(g_one.sem, 1)
                dve.wait_ge(g_one.sem, g_one.at(0, 3 * f + 1))
                nc.vector.reciprocal(r, r).then_inc(g_one.sem, 1)
                dve.wait_ge(g_one.sem, g_one.at(0, 3 * f + 2))
                nc.vector.tensor_tensor(r, r, gb[:, 0:S], ALU.mult).then_inc(g_one.sem, 1)
                dve.wait_ge(g_one.sem, g_one.at(0, 3 * f + 3))
                nc.vector.tensor_tensor(act_t[:, f], r, gb[:, S:2 * S], ALU.mult).then_inc(g_act.sem, 1)
            dve.wait_ge(f_down.sem, f_down.at(0, 4))
            dve.wait_ge(s_gate, 9)
            dve.wait_ge(fh_tr.sem, fh_tr.at(0, 4))
            last_n = [0]

            def last_step(ins):
                last_n[0] += 1
                ins.then_inc(s_last, 1)
                dve.wait_ge(s_last, last_n[0])

            for n in range(SN):
                last_step(nc.vector.tensor_tensor(x1[:, n], bank[6 + n][:], x1[:, n], ALU.add))
                last_step(nc.vector.tensor_scalar(x1[:, n], x1[:, n], small[:, 14 + n:15 + n], None, ALU.mult))
                last_step(nc.vector.scalar_tensor_tensor(out=fh[:, n], in0=sel[:, n, D:], scalar=small[:, 36 + n:37 + n], in1=x1[:, n],
                                                         op0=ALU.mult, op1=ALU.add))
                last_step(nc.vector.tensor_tensor(fh[:, n], fh[:, n], sel[:, n, 0:D], ALU.add))

        @block.gpsimd
        def _(pool):
            for g in (turned_p, prod_p, idx_set, seen_set, mask_a1, masks, x_bias, sa_sub, out_add):
                pool.sem_inc(g.sem, g.prime)
            for part in (q_blk.rearrange("p a b c d n -> p (a b c d n)"), qa_blk.rearrange("p a b c n -> p (a b c n)"),
                         pc.rearrange("p a n -> p (a n)"), va.rearrange("p a b n -> p (a b n)")):
                nc.gpsimd.memset(part, 0.0).then_inc(s_zero, 1)

            def gather(dst, table, idx, top):
                return pool.indirect_dma_start(out=dst, out_offset=None, in_=table, in_offset=bass.IndirectOffsetOnAxis(ap=idx, axis=0),
                                               bounds_check=top, oob_is_err=False)

            pool.wait_ge(s_pre, 2)
            for t in range(PAIRS):
                gather(rope[:, t], a["rope"], pos_idx[:, t:t + 1], NBLK * BLOCK - 1).then_inc(s_rope, 16)
            pool.wait_ge(s_rope, 16 * PAIRS)
            pool.wait_ge(s_win_in, 48)
            with pool.Fori(0, PAIRS // 2) as i:
                for u in range(2):
                    t = i * 2 + u
                    pool.wait_ge(scaled.sem, scaled.at(t, 1))
                    pool.wait_ge(roped.sem, roped.at(t, 2 - 4))
                    nc.gpsimd.tensor_tensor(turned[:, u, :, 0, :], qk[:, u, :, 1, :], rope[:, bass.ds(t, 1), 32:64].to_broadcast([P, QK, 32]),
                                            ALU.mult).then_inc(turned_p.sem, 1)
                    if u == 0:
                        pool.wait_ge(same_p.sem, same_p.at(i, 1))
                        pool.wait_ge(src_v.sem, src_v.at(i, 0))
                        nc.gpsimd.tensor_tensor(prod[0:GP], tok_all[0:GP].rearrange("p (w o) -> p o w", o=BLOCK),
                                                same[0:GP].unsqueeze(1).to_broadcast([GP, BLOCK, WRITERS]), ALU.mult).then_inc(prod_p.sem, 1)

            pool.wait_ge(s_weights, 16 * 11)
            pool.wait_ge(s_idx, 3)
            for u in range(2):
                pool.wait_ge(q_stored[u], 16 * (PAIRS // 2 + 1))
                pool.wait_ge(kv_stored[u], 16 * (PAIRS // 2 + 1))

            def set_indices(i, j):
                pool.wait_ge(pv_done.sem, pv_done.at(i, 8 * (j + 1) - STEPS))
                nc.gpsimd.tensor_copy(turn_idx[:, j, 0:4].rearrange("p (b h) -> p h b", h=2), cache_idx[:, :, bass.ds(i * BT + 2 * j, 2)]).then_inc(idx_set.sem, 1)
                nc.gpsimd.tensor_copy(turn_idx[:, j, 4:8].rearrange("p (b h) -> p h b", h=2), over_idx[:, :, bass.ds(i * BT + 2 * j, 2)]).then_inc(idx_set.sem, 1)
                nc.gpsimd.tensor_copy(turn_idx[:, j, 8:9], fresh_idx[:, bass.ds(i * PT + j, 1)]).then_inc(idx_set.sem, 1)
                pool.wait_ge(idx_set.sem, idx_set.at(i, 3 * j + 3))
                pool.sem_inc(s_pool_passed, 1)

            def gather_cached(i, j):
                set_indices(i, j)
                for n in range(4):
                    gather(kv[:, j, n], a["cache"], turn_idx[:, j, n:n + 1], POOL_BLOCKS * BLOCK - 1).then_inc(cached[j], 16)

            def gather_fresh(i, j):
                pool.wait_ge(cached[j], i * 64 + 64)
                pool.sem_inc(s_pool_passed, 1)
                for n in (4, 0, 1, 2, 3):
                    col = 8 if n == 4 else 4 + n
                    gather(kv[:, j, n], kv_new, turn_idx[:, j, col:col + 1], NT - 1).then_inc(fresh[j], 16)

            def make_mask(i, n):
                b = n % 2
                pool.wait_ge(masked.sem, masked.at(i, 4 * (n - 1)))
                pool.sem_inc(s_pool_passed, 1)
                nc.gpsimd.tensor_scalar(mk[:, b], place_c[:, b], turn_seen[:, n:n + 1], NEG, ALU.is_lt, ALU.mult).then_inc(mask_a1.sem, 1)
                pool.wait_ge(mask_a1.sem, mask_a1.at(i, n + 1))
                nc.gpsimd.tensor_tensor(mk[:, b], mk[:, b], mask_c[:, b], ALU.add).then_inc(masks.sem, 1)

            def turn(i, more):
                nc.gpsimd.tensor_copy(turn_seen, first_seen[:, bass.ds(i * BT, BT)]).then_inc(seen_set.sem, 1)
                pool.wait_ge(seen_set.sem, seen_set.at(i, 1))
                make_mask(i, 0)
                make_mask(i, 1)
                for j in range(PT):
                    pool.wait_ge(x_loaded[j], i * 16 + 16)
                    nc.gpsimd.tensor_tensor(xr[:, j], xr[:, j], bo, ALU.add).then_inc(x_bias.sem, 1)
                make_mask(i, 2)
                make_mask(i, 3)
                if more:
                    gather_cached(i + 1, 0)
                for j in range(PT):
                    pool.wait_ge(sa_max.sem, sa_max.at(i, j + 1))
                    scores = pa[:, j].rearrange("p h b t -> p (h b) t")
                    nc.gpsimd.tensor_tensor(scores, scores, top_a[:, j].unsqueeze(2).to_broadcast([P, 2 * HP, T]), ALU.subtract).then_inc(sa_sub.sem, 1)
                if more:
                    gather_cached(i + 1, 1)
                    gather_fresh(i + 1, 0)
                    gather_fresh(i + 1, 1)
                for j in range(PT):
                    pool.wait_ge(hid.sem, hid.at(i, j + 1))
                    nc.gpsimd.tensor_tensor(xr[:, j], xh[:, j, 0:D], xh[:, j, D:], ALU.add).then_inc(out_add.sem, 1)

            for j in range(PT):
                gather_cached(0, j)
            for j in range(PT):
                gather_fresh(0, j)
            with pool.Fori(0, TURNS - 1) as i:
                turn(i, True)
            turn(TURNS - 1, False)

            pool.wait_ge(s_pick_in, 32)
            for n in range(SN):
                gather(sel[:, n], xh_rows, picked[:, 1, n:n + 1], NT - 1).then_inc(s_sel, 16)
                gather(frope[:, n], a["f_rope"], picked[:, 0, n:n + 1], T - 1).then_inc(s_sel, 16)
            for n in range(SN):
                pool.wait_ge(s_last, 4 * (n + 1))
                pool.indirect_dma_start(out=out.rearrange("q p n -> (q p) n"), out_offset=bass.IndirectOffsetOnAxis(ap=picked[:, 1, n:n + 1], axis=0),
                                        in_=fh[:, n], in_offset=None, bounds_check=NT - 1, oob_is_err=False).then_inc(s_fout, 16)
            pool.wait_ge(s_fout, 32)


def build(nc, ins, out_shape):
    args = {}
    for name, (shape, dt) in ins.items():
        args[name] = nc.dram_tensor(f"in_{name}", shape, dt, kind="ExternalInput").ap()
    out = nc.dram_tensor("out_0", out_shape, F32, kind="ExternalOutput").ap()
    block_kernel(nc, args, out)


def constants():
    f = np.float32
    t = np.arange(T)
    c = np.arange(WINDOW)
    seen = np.where(c[None, :] > t[:, None], 0.0, NEG)
    new = np.where(t[None, :] <= t[:, None], 0.0, NEG)
    far = np.full(T, 1.0e9)
    mask_c = np.stack([np.concatenate([seen, new], 1), np.concatenate([new, seen], 1)], 1)
    place = np.stack([np.concatenate([c, far]), np.concatenate([far, c])], 0)
    causal = np.where(np.arange(P)[None, :] <= np.arange(P)[:, None], 0.0, NEG)
    p = np.arange(P)
    seq = np.zeros((P, 1 + PAIRS))
    seq[:, 0] = p % T
    seq[:, 1] = p * P
    seq[:, 2] = p * P + T
    consts = np.concatenate([
        np.eye(P), np.tile(mask_c, (2, 1, 1)).reshape(P, -1), np.broadcast_to(place.reshape(1, -1), (P, 2 * SPAN)),
        np.tile(new, (2, 1)), np.concatenate([np.zeros((P, P)), causal], 1), np.full((P, 1), 1e-6), seq], 1).astype(f)
    b = np.arange(B)[:, None]
    consts32 = np.concatenate([
        np.broadcast_to(np.arange(NBLK), (B, NBLK)), np.broadcast_to(np.arange(WSLOTS), (B, WSLOTS)),
        np.broadcast_to(np.arange(NSLOTS * BLOCK), (B, NSLOTS * BLOCK)), b * T + 1,
        np.broadcast_to(np.arange(BLOCK), (B, BLOCK))], 1).astype(f)
    half = CHD // 2
    inv = (f(1.0) / np.power(f(10000.0), np.arange(half, dtype=f) / f(half))).astype(f)
    ang = np.arange(NBLK * BLOCK, dtype=f)[:, None] * inv
    rope = np.concatenate([np.cos(ang), -np.sin(ang), np.sin(ang)], 1).astype(f)
    inv = (f(1.0) / np.power(f(10000.0), np.arange(0, FHD, 2, dtype=f) / f(FHD))).astype(f)
    ang = np.arange(T, dtype=f)[:, None] * inv
    f_rope = np.concatenate([np.cos(ang), np.cos(ang), -np.sin(ang), np.sin(ang)], 1).astype(f)
    return {"consts": consts, "consts32": consts32, "rope": rope, "f_rope": f_rope}


def laid_out(v):
    c = np.ascontiguousarray

    def parts(w):
        return c(w.reshape(w.shape[0] // P, P, w.shape[1]).transpose(1, 0, 2))

    def chunks(w):
        k = w.reshape(w.shape[0] // 512, KD, P, w.shape[1] // 512, 512)
        return c(k.transpose(3, 0, 2, 1, 4).reshape(-1, P, KD, 512))

    x = v["x"].reshape(PAIRS, P, KD, P)
    lens, tables = v["itok_B_37_3939"], v["itok_Bx257_0_4111"]
    d = {
        "x_t": c(x.transpose(0, 3, 2, 1)),
        "x_rows": v["x"].reshape(PAIRS, P, D),
        "lens_rep": c(np.concatenate([np.repeat(lens.reshape(PAIRS, 2).T, T, axis=0), np.broadcast_to(lens, (P, B))], 1)),
        "lens": lens.reshape(B, 1),
        "tables": tables,
        "experts": v["itok_B_0_15"].reshape(1, B),
        "qk_scale": c(np.broadcast_to(np.concatenate([np.tile(v["L0_cond_q_norm_scale"], CH), np.tile(v["L0_cond_k_norm_scale"], CG)]), (P, QK * CHD))),
        "w_qkv": parts(np.concatenate([v["L0_cond_Wq"].reshape(2, 2, 2, CHD, D).transpose(0, 2, 1, 3, 4).reshape(CH * CHD, D), v["L0_cond_Wk"], v["L0_cond_Wv"]], 0).T),
        "cache": np.concatenate([v["L0_cond_k_blocks"].transpose(0, 2, 1, 3).reshape(POOL_BLOCKS * BLOCK, CG * CHD),
                                 v["L0_cond_v_blocks"].transpose(0, 2, 1, 3).reshape(POOL_BLOCKS * BLOCK, CG * CHD)], 1),
        "w_c_o": c(v["L0_cond_Wo"].T.reshape(2, 2, 2, CHD, D).transpose(1, 3, 0, 2, 4).reshape(P, KD, D)),
        "w_a_q": parts(v["L0_attn_Wq"].T), "w_a_k": parts(v["L0_attn_Wk"].T), "w_a_v": parts(v["L0_attn_Wv"].T),
        "w_a_o": c(v["L0_attn_Wo"].T.reshape(2, 4, 2, AHD, D).transpose(1, 3, 0, 2, 4).reshape(P, KD, D)),
        "bq": c(v["L0_attn_bq"].reshape(KD, P).T), "bk": c(v["L0_attn_bk"].reshape(KD, P).T),
        "bv": v["L0_attn_bv"], "bo": v["L0_attn_bo"], "router": v["L0_ffn_w_router"],
        "w_exp": c(v["L0_cond2_W"].reshape(16, KD, P, D).transpose(0, 2, 1, 3)),
        "b_exp": v["L0_cond2_b"],
        "f_qkv": chunks(np.concatenate([v["L0_ffn_wq"], v["L0_ffn_wk"], v["L0_ffn_wv"]], 1)),
        "f_bias": np.concatenate([v["L0_ffn_bq"], v["L0_ffn_bk"], v["L0_ffn_bv"]]),
        "f_wo": chunks(v["L0_ffn_wo"]), "f_gate": chunks(v["L0_ffn_w_gate"]), "f_up": chunks(v["L0_ffn_w_up"]),
        "f_down": chunks(v["L0_ffn_w_down"]), "ln1": v["L0_ffn_ln1_w"], "ln2": v["L0_ffn_ln2_w"],
    }
    d.update(constants())
    return {k: c(x) for k, x in d.items()}


def kernel(**inputs):
    import numpy as _np
    import concourse.bacc as _bacc
    from concourse import mybir as _mybir
    from concourse.bass_utils import run_bass_kernel_spmd as _run

    nc = _bacc.Bacc("TRN2", target_bir_lowering=False, num_devices=1)
    arrays = laid_out({k: _np.asarray(x) for k, x in inputs.items()})
    build(nc, {k: (x.shape, _mybir.dt.from_np(x.dtype)) for k, x in arrays.items()}, (PAIRS, P, D))
    r = _run(nc, [{f"in_{k}": x for k, x in arrays.items()}], core_ids=[0])
    return r.results[0]["out_0"].reshape(B, T, D)
```

```python
from contextlib import ExitStack

import numpy as np

import concourse.bass as bass
from concourse import mybir

ALU = mybir.AluOpType
ACT = mybir.ActivationFunctionType
AX = mybir.AxisListType
F32 = mybir.dt.float32
I32 = mybir.dt.int32
U32 = mybir.dt.uint32

P = 128
B, T, D = 32, 64, 512
NT = B * T
PAIRS = B // 2
KD = D // P
CH, CG, CHD = 8, 4, 64
BLOCK, WINDOW, NBLK = 16, 256, 257
POOL_BLOCKS = 16 * NBLK
ROW = 2 * CG * CHD
WSLOTS = WINDOW // BLOCK + T // BLOCK + 1
NSLOTS = T // BLOCK + 1
WPOS = WSLOTS * BLOCK
SPAN = WINDOW + T
QK = CH + CG
SKIP = 1.0e6
GROUPS = 8
GP = B * WSLOTS // GROUPS
WRITERS = B * NSLOTS
NEG = -1.0e30
AH, AHD = 16, 32
HP = AH // 2
PT = 2
TURNS = PAIRS // PT
BT = 2 * PT
TT = PT * P
STEPS = BT * CG
KEEP = 8
S = B * KEEP
SN = S // P
FH, FKV, FHD = 16, 8, 128
FI = 2048
FQKV = (FH + 2 * FKV) * FHD
NQKV = FQKV // 512
NIN = FI // P
COLS = 53200
RING = 6


class Signal:

    def __init__(self, sem, per_turn, prime=0):
        self.sem, self.per_turn, self.prime = sem, per_turn, prime

    def at(self, turn, n):
        return turn * self.per_turn + (self.prime + n)


class Arena:

    def __init__(self, tensor):
        self.tensor, self.next = tensor, 0

    def take(self, *shape):
        n = int(np.prod(shape))
        assert self.next + n <= self.tensor.shape[1], (self.next, n)
        ap = self.tensor[:, self.next:self.next + n]
        self.next += n
        if len(shape) > 1:
            names = "abcdef"[:len(shape)]
            kept = {c: k for c, k in zip(names[1:], shape[1:])}
            ap = ap.rearrange(f"p ({' '.join(names)}) -> p {' '.join(names)}", **kept)
        return ap


def block_kernel(nc, a, out):
    ctx = ExitStack()
    with ctx:
        def sem(name):
            return ctx.enter_context(nc.semaphore(name))

        def sig(name, per_turn, prime=4):
            return Signal(sem(name), per_turn, prime)

        def dram(name, shape, dt=F32):
            return nc.dram_tensor(name, shape, dt).ap()

        kv_new = dram("kv_new", (NT, ROW))
        q_turned = dram("q_turned", (PAIRS, P, 512))
        xh_rows = dram("xh_rows", (NT, 2 * D))
        win_d = dram("win_d", (B, WSLOTS))
        tok_d = dram("tok_d", (B, NSLOTS * BLOCK))
        src_d = dram("src_d", (B * WSLOTS, BLOCK))

        ar = Arena(ctx.enter_context(nc.sbuf_tensor("arena", [P, COLS], F32)))
        ident = ar.take(P)
        mask_c = ar.take(2, SPAN)
        place_c = ar.take(2, SPAN)
        mask_a = ar.take(T)
        mask_f = ar.take(2, P)
        eps = ar.take(1)
        one = ar.take(1)
        seq_base = ar.take(1 + PAIRS)
        CONST = ar.next
        first_seen = ar.take(B)
        score = ar.take(PAIRS)
        score_t = ar.take(PT)
        cache_idx = ar.take(2, B).bitcast(I32)
        over_idx = ar.take(2, B).bitcast(I32)
        fresh_idx = ar.take(PAIRS).bitcast(I32)
        turn_idx = ar.take(PT, 9).bitcast(I32)
        turn_seen = ar.take(BT)
        expert_id = ar.take(B).bitcast(I32)
        router = ar.take(D)
        bv = ar.take(D)
        bo = ar.take(D)
        bq = ar.take(KD)
        bk = ar.take(KD)
        routed_base = ar.next
        w_c_o = ar.take(KD, D)
        w_a_q = ar.take(KD, D)
        w_a_k = ar.take(KD, D)
        w_a_v = ar.take(KD, D)
        w_a_o = ar.take(KD, D)
        base = ar.next
        kv = ar.take(PT, 5, ROW)
        at = ar.next
        k_t = ar.take(PT, 2, 2 * SPAN)
        ar.next = at
        pa_t = ar.take(PT, HP, P)
        ar.next = at
        st = ar.take(PT, 2, 512)
        ar.next = at + PT * 4 * SPAN
        at = ar.next
        o_t = ar.take(KD, TT)
        ar.next = at
        oa_t = ar.take(PT, KD, P)
        at = ar.next
        y_t = ar.take(KD, TT)
        ar.next = at
        x_t = ar.take(PT, KD, P)
        ka_t = ar.take(KD, TT)
        zeroed = ar.next
        q_blk = ar.take(PT, 2, 2, 2, P)
        qa_blk = ar.take(KD, BT, 4, T)
        pc = ar.take(4, 3 * P)
        va = ar.take(PT, 2, D)
        first = ar.next
        pc_t = ar.take(2, 3 * P)
        mk = ar.take(2, SPAN)
        top_c = ar.take(4)
        neg_c = ar.take(4)
        sum_c = ar.take(2, CG)
        rec_c = ar.take(2, CG)
        oc = ar.take(2, CG * CHD)
        pa = ar.take(PT, HP, 2, T)
        top_a = ar.take(PT, 2 * HP)
        sum_a = ar.take(PT, 2 * HP)
        rec_a = ar.take(PT, 2 * HP)
        oa = ar.take(PT, 2, 2, 4, AHD)
        xr = ar.take(PT, D)
        xh = ar.take(PT, 2 * D)
        junk = ar.take(D)
        b_exp = ar.take(PT, D)
        w_exp = ar.take(BT, KD, D)
        ar.next = first
        w_qkv = ar.take(KD, 1024)
        x_in = ar.take(2, KD, P)
        kvn = ar.take(2, ROW)
        rope = ar.take(PAIRS, 96)
        scale1 = ar.take(QK, CHD)
        sq = ar.take(QK, CHD)
        ssum = ar.take(2, QK)
        root = ar.take(2, QK)
        inv = ar.take(2, QK)
        qk = ar.take(2, QK, 2, 32)
        turned = ar.take(2, QK, 2, 32)
        qk_cos = ar.take(2, QK, 2, 32)
        qr = ar.take(2, 512)
        q_out = ar.take(2, 512)
        prod = [ar.take(BLOCK, WRITERS)]
        ar.next = base
        pos_idx = ar.take(PAIRS).bitcast(I32)
        len_all = ar.take(PAIRS + B).bitcast(I32)
        posf = ar.take(PAIRS)
        blocks_i = ar.take(NBLK).bitcast(I32)
        blocks = ar.take(NBLK)
        lens_i = ar.take(8).bitcast(I32)
        lens = ar.take(8)
        k32 = ar.take(NBLK + WSLOTS + NSLOTS * BLOCK + 1 + BLOCK)
        slot_no = ar.take(WSLOTS)
        hit = ar.take(NBLK)
        win = ar.take(WSLOTS)
        tok = ar.take(3, NSLOTS * BLOCK)
        tok_all = ar.take(WRITERS * BLOCK)
        blk_w = ar.take(WRITERS)
        blk_r = ar.take(GROUPS)
        same = ar.take(2, WRITERS)
        prod.append(ar.take(BLOCK, WRITERS))
        src = ar.take(GROUPS, BLOCK)
        al = ar.take(2, 2, WPOS)
        idx_f = ar.take(4, SPAN)
        assert ar.next <= zeroed
        ar.next = routed_base
        ring = ar.take(RING, KD, D)
        fq = ar.take(SN, FQKV)
        fq_t = ar.take(FH, S)
        fk_t = ar.take(FKV, S)
        fbias = ar.take(FQKV)
        fo_t = ar.take(FH, S)
        sel = ar.take(SN, 2 * D)
        fh = ar.take(SN, D)
        fh_t = ar.take(KD, S)
        x1 = ar.take(SN, D)
        frope = ar.take(SN, 256)
        fcos = ar.take(2, D)
        fsin = ar.take(2, D)
        fp = ar.take(4, P + S)
        fp_t = ar.take(2, P + S)
        f_top, f_neg, f_sum, f_rec = (ar.take(4, SN) for _ in range(4))
        ln1 = ar.take(D)
        ln2 = ar.take(D)
        fjunk = ar.take(D)
        small = ar.take(64)
        score_b = ar.take(P)
        top8 = ar.take(2, KEEP)
        at8 = ar.take(2, KEEP).bitcast(U32)
        neg8 = ar.take(2, KEEP)
        sorted8 = ar.take(2, KEEP)
        pick8 = ar.take(2, 2, KEEP)
        spread = ar.take(2, PAIRS, 2 * KEEP)
        pre = ar.take(SN, D)
        picked = ar.take(2, SN).bitcast(I32)
        after = ar.next
        ar.next = routed_base + RING * KD * D
        act_t = ar.take(NIN, S)
        e_g = ar.take(2, S)
        r_g = ar.take(2, S)
        assert ar.next <= routed_base + RING * KD * D + SN * FQKV
        ar.next = after

        bank = [ctx.enter_context(nc.psum_tensor(f"bank{i}", [P, 512], F32)) for i in range(8)]

        s_early = sem("small_inputs_loaded")
        s_weights = sem("loop_weights_loaded")
        s_lens = sem("lengths_loaded")
        s_consts = sem("constants_loaded")
        s_wqkv = [sem(f"wqkv_loaded{k}") for k in range(KD)]
        s_rope = sem("rope_gathered")
        s_win_out = sem("window_blocks_stored")
        s_win_in = sem("window_blocks_back")
        s_src_out = sem("sources_stored")
        s_src_in = sem("sources_back")
        s_pre = sem("vector_setup_step")
        s_zero = sem("zeros_written")
        s_idx_t = sem("index_transposed")
        s_idx = sem("indices_ready")
        s_passed = sem("passed_waits")
        xin_l = [sem(f"x_in_loaded{u}") for u in range(2)]
        proj = sig("projected", 1)
        summed = sig("squares_summed", 1)
        v_copied = sig("new_values_copied", 1)
        rooted = sig("rooted", 1)
        inverted = sig("inverted", 1)
        normed = sig("normed", 2)
        scaled = sig("scaled", 1)
        turned_p = sig("turned_by_pool", 1)
        turned_v = sig("turned_by_vector", 1)
        cosd = sig("cosine_part", 1)
        roped = sig("roped", 2)
        q_tr = sig("q_transposed", 1)
        q_copied = sig("q_copied", 1)
        q_stored = [sem(f"q_stored{u}") for u in range(2)]
        kv_stored = [sem(f"kv_stored{u}") for u in range(2)]
        same_p = sig("blocks_compared", 1)
        prod_p = sig("writers_marked", 1)
        src_v = sig("last_writer_found", 1)
        q_loaded = [sem(f"q_loaded{j}") for j in range(PT)]
        cached = [sem(f"cached_rows{j}") for j in range(PT)]
        fresh = [sem(f"fresh_rows{j}") for j in range(PT)]
        x_loaded = [sem(f"x_rows{j}") for j in range(PT)]
        we_loaded = [sem(f"expert{n}") for n in range(BT)]
        be_loaded = [sem(f"expert_bias{j}") for j in range(PT)]
        xh_stored = [sem(f"xh_stored{j}") for j in range(PT)]
        out_stored = [sem(f"out_stored{j}") for j in range(PT)]
        idx_set = sig("turn_indices", 3 * PT)
        seen_set = sig("turn_first_places", 1)
        mask_a1 = sig("mask_begun", BT)
        masks = sig("mask_made", BT)
        k_tr = sig("keys_transposed", 3 * PT)
        misc = sig("keys_and_outputs_copied", 3 * PT + BT)
        scored = sig("scored", STEPS, STEPS)
        masked = sig("masked", STEPS)
        negated = sig("max_negated", STEPS)
        exped = sig("exped", STEPS)
        p_tr = sig("probs_transposed", STEPS)
        p_act = sig("probs_copied_by_scalar", STEPS // 4)
        p_dve = sig("probs_copied_by_vector", STEPS - STEPS // 4)
        pv_done = sig("values_weighted", STEPS, STEPS)
        recd = sig("sums_inverted", BT)
        o_norm = sig("output_normed", BT)
        o_tr = sig("output_transposed", BT)
        y_done = sig("y_done", 2)
        y_act = sig("y_copied_by_scalar", 1)
        y_dve = sig("y_copied_by_vector", 1)
        qa_done = sig("qa_done", 2)
        qa_act = sig("qa_copied_by_scalar", 1)
        qa_dve = sig("qa_copied_by_vector", 1)
        ka_done = sig("ka_done", 2)
        ka_act = sig("ka_copied_by_scalar", 1)
        ka_dve = sig("ka_copied_by_vector", 1)
        st_done = sig("sa_scored_by_key", 2 * PT)
        st_act = sig("sa_scores_copied_by_scalar", PT)
        st_dve = sig("sa_scores_copied_by_vector", PT)
        sa_done = sig("sa_scored", PT)
        sa_mask = sig("sa_masked", 2 * PT)
        sa_max = sig("sa_max", PT)
        sa_sub = sig("sa_max_subtracted", PT)
        sa_exp = sig("sa_exped", PT)
        sa_sum = sig("sa_summed", PT)
        sa_rec = sig("sa_inverted", PT)
        va_done = sig("va_done", PT)
        va_cop = sig("va_copied", PT)
        pa_tr = sig("pa_transposed", PT)
        pa_cop = sig("pa_copied", PT)
        pva = sig("pva_done", PT)
        oa_norm = sig("oa_normed", PT)
        oa_tr = sig("oa_transposed", PT)
        oa_cop = sig("oa_copied", PT)
        z_done = sig("z_done", PT)
        x_bias = sig("x_plus_bias", PT)
        resid = sig("residual_added", PT)
        x_tr = sig("x_transposed", PT)
        x_cop = sig("x_copied", PT)
        c_done = sig("expert_done", PT)
        hid = sig("hidden_made", PT)
        rscore = sig("router_scored", PT)
        sc_cop = sig("scores_kept", 1)
        out_add = sig("out_rows_made", PT)
        s_fin = sem("routed_inputs_loaded")
        s_sct = sem("scores_transposed")
        s_pick = sem("pick_step")
        s_sel = [sem(f"selected_rows{n}") for n in range(SN)]
        s_frope = sem("routed_rope_gathered")
        s_gate = sem("row_gate_step")
        s_last = sem("last_rows_step")
        f_x1 = sig("f_residual_added", 0, 0)
        s_rms = sem("routed_square_root")
        s_esc = sem("routed_gate_exp")
        r_landed = [sem(f"ring_landed{n}") for n in range(RING)]
        fh_ready = sig("fh_ready", 0, 0)
        fh_tr = sig("fh_transposed", 0, 0)
        fh_cop = sig("fh_copied", 0, 0)
        fq_mm = sig("fq_done", 0, 0)
        fq_bias = sig("fq_biased", 0, 0)
        f_sin = sig("f_sin_part", 0, 0)
        f_cos = sig("f_cos_part", 0, 0)
        f_rope = sig("f_roped", 0, 0)
        fq_tr = sig("fq_transposed", 0, 0)
        fq_cop = sig("fq_copied", 0, 0)
        fs = sig("f_scored", 0, 0)
        fmask = sig("f_masked", 0, 0)
        fneg = sig("f_negated", 0, 0)
        fexp = sig("f_exped", 0, 0)
        frec = sig("f_inverted", 0, 0)
        fnorm = sig("f_normed", 0, 0)
        fp_tr = sig("f_probs_transposed", 0, 0)
        fp_cop = sig("f_probs_copied", 0, 0)
        fpv = sig("f_values_weighted", 0, 0)
        fo_cop = sig("f_outputs_copied", 0, 0)
        fwo = sig("f_projected", 0, 0)
        g_done = sig("gate_up_done", 0, 0)
        g_exp = sig("gate_exped", 0, 0)
        g_one = sig("gate_step", 0, 0)
        g_act = sig("gated_made", 0, 0)
        f_down = sig("down_done", 0, 0)
        s_fout = sem("routed_rows_stored")

        PRE_WIN = 12 + WSLOTS + 4
        PRE_ALL = PRE_WIN + 2
        PRE_IDX = PRE_ALL + 13
        PICKS = 13

        def probs_copied(eng, turn, s):
            if s % 4 == 3:
                eng.wait_ge(p_act.sem, p_act.at(turn, s // 4 + 1))
            else:
                eng.wait_ge(p_dve.sem, p_dve.at(turn, s + 1 - (s + 1) // 4))

        block = ctx.enter_context(nc.Block())

        @block.sync
        def _(sp):
            for u in range(PT):
                sp.sem_inc(xh_stored[u], 16)
                sp.sem_inc(out_stored[u], 16)
                sp.sem_inc(q_stored[u], 16)
                sp.sem_inc(kv_stored[u], 16)
            sp.dma_start(len_all, a["lens_rep"]).then_inc(s_lens, 16)
            sp.dma_start(seq_base, a["consts"][:, CONST - 1 - PAIRS:CONST]).then_inc(s_lens, 16)
            sp.dma_start(x_in[:, 0], a["x_t"][0]).then_inc(xin_l[0], 16)
            for k in range(KD):
                sp.dma_start(w_qkv[:, k, :], a["w_qkv"][:, k, :]).then_inc(s_wqkv[k], 16)
            sp.dma_start(x_in[:, 1], a["x_t"][1]).then_inc(xin_l[1], 16)
            sp.wait_ge(s_pre, PRE_WIN)
            sp.dma_start(win_d, win[0:B, :]).then_inc(s_win_out, 16)
            sp.dma_start(tok_d, tok[0:B, 2, :]).then_inc(s_win_out, 16)
            sp.wait_ge(s_win_out, 32)
            with nc.allow_non_contiguous_dma(reason="a few block numbers"):
                sp.dma_start(blk_r[0:GP, :], win_d.rearrange("b s -> (b s)").rearrange("(g p) -> p g", p=GP)).then_inc(s_win_in, 16)
                sp.dma_start(blk_w[0:GP, :].rearrange("p (b s) -> p b s", s=NSLOTS),
                             win_d[:, WSLOTS - NSLOTS:WSLOTS].partition_broadcast(GP)).then_inc(s_win_in, 16)
            sp.dma_start(tok_all[0:GP, :], tok_d.rearrange("b s -> (b s)").partition_broadcast(GP)).then_inc(s_win_in, 16)

            def load_x(t, u):
                sp.wait_ge(proj.sem, proj.at(t, 1))
                sp.dma_start(x_in[:, u], a["x_t"][bass.ds(t + 2, 1)].rearrange("a p k n -> p (a k) n")).then_inc(xin_l[u], 16)

            def store_kv(t, u):
                sp.wait_ge(roped.sem, roped.at(t, 2))
                sp.wait_ge(v_copied.sem, v_copied.at(t, 1))
                sp.dma_start(kv_new[bass.ds(t * P, P), :], kvn[:, u]).then_inc(kv_stored[u], 16)

            def store_q(t, u):
                sp.wait_ge(q_copied.sem, q_copied.at(t, 1))
                sp.dma_start(q_turned[bass.ds(t, 1)].rearrange("a p n -> p (a n)"), q_out[:, u]).then_inc(q_stored[u], 16)

            for t in range(2):
                load_x(t, t)
                store_kv(t, t)

            def two_tiles(i):
                for u in range(2):
                    load_x(i * 2 + u, u)
                    store_kv(i * 2 + u, u)
                    store_q(i * 2 + u - 2, u)

            with sp.Fori(1, 5) as i:
                two_tiles(i)
            sp.wait_ge(src_v.sem, src_v.at(GROUPS, 0))
            sp.dma_start(src_d.rearrange("(g p) o -> p g o", p=GP), src[0:GP]).then_inc(s_src_out, 16)
            sp.wait_ge(s_src_out, 16)
            sp.dma_start(al[0:B, 0, 1, :], src_d.rearrange("(b s) o -> b (s o)", b=B)).then_inc(s_src_in, 16)
            with sp.Fori(5, 7) as i:
                two_tiles(i)
            for t in (PAIRS - 2, PAIRS - 1):
                store_kv(t, t % 2)
                store_q(t - 2, t % 2)
            for t in (PAIRS - 2, PAIRS - 1):
                store_q(t, t % 2)
            for u in range(2):
                sp.wait_ge(q_stored[u], 16 * (PAIRS // 2 + 1))
            sp.wait_ge(s_weights, 16 * 11)
            sp.wait_ge(s_zero, 4)

            def load_queries(i):
                for j in range(PT):
                    sp.wait_ge(scored.sem, scored.at(i, 8 * (j + 1) - STEPS))
                    source = q_turned[bass.ds(i * PT + j, 1)].rearrange("a p (c n) -> p (a c) n", c=4)
                    for g2 in range(2):
                        rows = slice(64 * g2, 64 * g2 + 64)
                        sp.dma_start(q_blk[rows, j, :, :, g2, :].rearrange("p b g n -> p (b g) n"), source[rows]).then_inc(q_loaded[j], 16)

            def load_turn(i):
                for j in range(PT):
                    sp.wait_ge(out_stored[j], i * 16 + 16)
                    sp.dma_start(xr[:, j], a["x_rows"][bass.ds(i * PT + j, 1)].rearrange("a p n -> p (a n)")).then_inc(x_loaded[j], 16)
                    sp.wait_ge(c_done.sem, c_done.at(i, j + 1 - PT))
                    sp.wait_ge(hid.sem, hid.at(i, j + 1 - PT))
                    for b in range(2):
                        n = 2 * j + b
                        e = sp.value_load(expert_id[0:1, bass.ds(i * BT + n, 1)], min_val=0, max_val=15)
                        sp.dma_start(w_exp[:, n], a["w_exp"][bass.ds(e, 1)].rearrange("e p k n -> p (e k) n")).then_inc(we_loaded[n], 16)
                        sp.dma_start(b_exp[64 * b:64 * b + 64, j, :], a["b_exp"][bass.ds(e, 1), :].rearrange("e n -> (e n)").partition_broadcast(64)).then_inc(be_loaded[j], 16)

            def store_turn(i):
                for j in range(PT):
                    sp.wait_ge(hid.sem, hid.at(i, j + 1))
                    sp.dma_start(xh_rows[bass.ds((i * PT + j) * P, P), :], xh[:, j]).then_inc(xh_stored[j], 16)
                    sp.wait_ge(out_add.sem, out_add.at(i, j + 1))
                    sp.dma_start(out[bass.ds(i * PT + j, 1)].rearrange("a p n -> p (a n)"), xr[:, j]).then_inc(out_stored[j], 16)

            load_queries(0)
            with sp.Fori(0, TURNS - 1) as i:
                load_turn(i)
                load_queries(i + 1)
                store_turn(i)
            load_turn(TURNS - 1)
            chunks = [a["f_qkv"][c] for c in range(NQKV)] + [a["f_wo"][c] for c in range(4)]
            for c in range(4):
                chunks += [a["f_gate"][c], a["f_up"][c]]
            chunks += [a["f_down"][c] for c in range(4)]
            for slot, left in ((5, pv_done), (0, y_done), (1, qa_done), (2, ka_done), (3, va_done), (4, z_done)):
                sp.wait_ge(left.sem, left.at(TURNS, 0))
                sp.dma_start(ring[:, slot], chunks[slot]).then_inc(r_landed[slot], 16)
            store_turn(TURNS - 1)
            sp.wait_ge(rscore.sem, rscore.at(TURNS, 0))
            sp.wait_ge(out_add.sem, out_add.at(TURNS, 0))
            sp.dma_start(fbias, a["f_bias"].partition_broadcast(P)).then_inc(s_fin, 16)
            sp.dma_start(ln1, a["ln1"].partition_broadcast(P)).then_inc(s_fin, 16)
            sp.dma_start(ln2, a["ln2"].partition_broadcast(P)).then_inc(s_fin, 16)
            for n, source in enumerate(chunks[RING:]):
                if n < NQKV:
                    sp.wait_ge(fq_mm.sem, 2 * (n + 1))
                elif n < NQKV + 4:
                    sp.wait_ge(fwo.sem, 1 + n - NQKV + 1)
                else:
                    sp.wait_ge(g_done.sem, 4 * ((n - NQKV - 4) // 2 + 1))
                sp.dma_start(ring[:, n % RING], source).then_inc(r_landed[n % RING], 16)
            for j in range(PT):
                sp.wait_ge(xh_stored[j], 16 * (TURNS + 1))
                sp.wait_ge(out_stored[j], 16 * (TURNS + 1))

        @block.tensor
        def _(pe):
            for g in (proj, q_tr, k_tr, scored, p_tr, pv_done, o_tr, y_done, qa_done, ka_done, st_done, sa_done, va_done, pa_tr, pva,
                      oa_tr, z_done, x_tr, c_done):
                pe.sem_inc(g.sem, g.prime)
            def project(t, half, u):
                pe.wait_ge(xin_l[u], half * 16 + 16)
                pe.wait_ge(normed.sem, normed.at(t, 2 - 4))
                pe.wait_ge(v_copied.sem, v_copied.at(t, 1 - 2))
                for k in range(KD):
                    pe.wait_ge(s_wqkv[k], 16)
                    for part in range(2):
                        mm = pe.matmul(bank[2 * u + part][:], x_in[:, u, k, :], w_qkv[:, k, 512 * part:512 * part + 512],
                                       start=(k == 0), stop=(k == KD - 1))
                mm.then_inc(proj.sem, 1)

            def turn_queries(t, u):
                pe.wait_ge(roped.sem, roped.at(t, 2))
                pe.wait_ge(q_copied.sem, q_copied.at(t, 1 - 2))
                for n in range(4):
                    mm = pe.transpose(bank[4 + u][:, n * P:(n + 1) * P], qr[:, u, n * P:(n + 1) * P], ident)
                mm.then_inc(q_tr.sem, 1)

            def two_tiles(i):
                for u in range(2):
                    project(i * 2 + 2 + u, i + 1, u)
                    turn_queries(i * 2 + u, u)

            project(0, 0, 0)
            project(1, 0, 1)
            pe.wait_ge(s_consts, 32)
            with pe.Fori(0, 6) as i:
                two_tiles(i)
            pe.wait_ge(s_pre, PRE_IDX)
            for kind in range(2):
                for half in range(2):
                    n = 2 * kind + half
                    pe.transpose(bank[6][:, n * B:(n + 1) * B], idx_f[0:B, kind, half * P:(half + 1) * P], ident[0:B, 0:B])
            pe.transpose(bank[6][:, 4 * B:5 * B], idx_f[0:B, 2, 0:P], ident[0:B, 0:B]).then_inc(s_idx_t, 1)
            two_tiles(6)
            turn_queries(PAIRS - 2, 0)
            turn_queries(PAIRS - 1, 1)

            pe.wait_ge(s_weights, 16 * 11)
            pe.wait_ge(s_idx, 4)
            pe.wait_ge(q_copied.sem, q_copied.at(PAIRS, 0))
            pe.wait_ge(s_zero, 4)

            def turn_keys(i, j):
                pe.wait_ge(cached[j], i * 64 + 64)
                pe.wait_ge(fresh[j], i * 80 + 80)
                for n in range(3):
                    use = 3 * j + n
                    pe.wait_ge(misc.sem, misc.at(i, use + 1 - 2))
                    cols = range(4 * n, min(4 * n + 4, 10))
                    for m in cols:
                        g, tile = m // 5, (0, 1, 4, 2, 3)[m % 5]
                        mm = pe.transpose(bank[6 + use % 2][:, (m - cols[0]) * P:(m - cols[0] + 1) * P],
                                          kv[:, j, tile, g * P:(g + 1) * P], ident)
                    mm.then_inc(k_tr.sem, 1)

            def scores(i, s):
                j, b, g = s // 8, s // 4 % 2, s % 4
                pe.wait_ge(q_loaded[j], i * 32 + 32)
                pe.wait_ge(misc.sem, misc.at(i, 3 * (j + 1)))
                pe.wait_ge(masked.sem, masked.at(i, s + 1 - 2))
                pe.matmul(bank[s % 2][:, 0:SPAN], q_blk[:, j, b, g // 2, g % 2, :],
                          k_t[:, j, g // 2, b * SPAN:(b + 1) * SPAN], start=True, stop=True).then_inc(scored.sem, 1)

            def turn_probs(i, s):
                b, g = s // 4 % 2, s % 4
                pe.wait_ge(exped.sem, exped.at(i, s + 1))
                if s >= 2:
                    probs_copied(pe, i, s - 2)
                else:
                    probs_copied(pe, i - 1, STEPS - 2 + s)
                for c in range(3):
                    mm = pe.transpose(bank[2 + s % 2][:, c * P:(c + 1) * P], pc[:, 2 * b + g % 2, c * P:(c + 1) * P], ident)
                mm.then_inc(p_tr.sem, 1)

            def weigh_values(i, s):
                j, b, g = s // 8, s // 4 % 2, s % 4
                n = s // 4
                probs_copied(pe, i, s)
                if g == 0:
                    pe.wait_ge(o_norm.sem, o_norm.at(i, n + 1 - 2))
                for c, tile in enumerate((0, 1, 4) if b == 0 else (4, 2, 3)):
                    mm = pe.matmul(bank[4 + n % 2][:, g * CHD:(g + 1) * CHD], pc_t[:, s % 2, c * P:(c + 1) * P],
                                   kv[:, j, tile, CG * CHD + g * CHD:CG * CHD + (g + 1) * CHD],
                                   start=(c == 0), stop=(c == 2))
                mm.then_inc(pv_done.sem, 1)

            def turn_outputs(i, n):
                use = 3 * PT + n
                pe.wait_ge(o_norm.sem, o_norm.at(i, n + 1))
                pe.wait_ge(misc.sem, misc.at(i, use + 1 - 2))
                for g in range(2):
                    mm = pe.transpose(bank[6 + use % 2][:, g * P:(g + 1) * P], oc[:, n % 2, g * P:(g + 1) * P], ident)
                mm.then_inc(o_tr.sem, 1)

            def attend(i):
                pe.wait_ge(resid.sem, resid.at(i, 0))
                pe.wait_ge(x_cop.sem, x_cop.at(i, 0))
                for s in range(STEPS + 4):
                    if s < STEPS:
                        scores(i, s)
                    if s == 3:
                        pe.wait_ge(hid.sem, hid.at(i, 0))
                    if 2 <= s < STEPS + 2:
                        turn_probs(i, s - 2)
                    if 3 <= s < STEPS + 3:
                        weigh_values(i, s - 3)
                    if s >= 7 and (s - 7) % 4 == 0:
                        turn_outputs(i, (s - 7) // 4)

            def query_columns(i):
                for m0 in range(2):
                    for half in range(2):
                        if m0 == 0 and half == 1:
                            pe.wait_ge(y_act.sem, y_act.at(i, 1))
                        for m in (m0, m0 + 2):
                            for k in (2 * half, 2 * half + 1):
                                mm = pe.matmul(bank[2 + m // 2][:, m0 * TT:(m0 + 1) * TT],
                                               w_a_q[:, k, m * P:(m + 1) * P], y_t[:, k, :], start=(k == 0), stop=(k == KD - 1))
                            if m0 == 1 and half == 1:
                                mm.then_inc(qa_done.sem, 1)

            def columns_of(i, weights, moving, first_bank, done):
                for m in range(KD):
                    for k in range(KD):
                        mm = pe.matmul(bank[first_bank + m // 2][:, (m % 2) * TT:(m % 2 + 1) * TT],
                                       weights[:, k, m * P:(m + 1) * P], moving[:, k, :], start=(k == 0), stop=(k == KD - 1))
                    if m % 2:
                        mm.then_inc(done.sem, 1)

            def self_attention(i):
                pe.wait_ge(misc.sem, misc.at(i, 3 * PT + BT))
                pe.wait_ge(masked.sem, masked.at(i, STEPS))
                columns_of(i, w_c_o, o_t, 0, y_done)
                pe.wait_ge(y_dve.sem, y_dve.at(i, 1))
                probs_copied(pe, i, STEPS - 2)
                probs_copied(pe, i, STEPS - 1)
                query_columns(i)
                pe.wait_ge(o_norm.sem, o_norm.at(i, BT))
                columns_of(i, w_a_k, y_t, 4, ka_done)
                pe.wait_ge(qa_act.sem, qa_act.at(i, 1))
                pe.wait_ge(qa_dve.sem, qa_dve.at(i, 1))
                pe.wait_ge(ka_act.sem, ka_act.at(i, 1))
                for half in range(2):
                    if half == 1:
                        pe.wait_ge(ka_dve.sem, ka_dve.at(i, 1))
                    for j in range(PT):
                        for k in (2 * half, 2 * half + 1):
                            for b in range(2):
                                n = 2 * j + b
                                mm = pe.matmul(bank[2 + 2 * j + half][64 * b:64 * b + 64, k % 2 * 256:k % 2 * 256 + 256],
                                               ka_t[:, k, n * T:(n + 1) * T], qa_blk[:, k, n].rearrange("p h t -> p (h t)"), start=True, stop=True)
                        mm.then_inc(st_done.sem, 1)
                for j in range(PT):
                    pe.wait_ge(st_act.sem, st_act.at(i, j + 1))
                    pe.wait_ge(st_dve.sem, st_dve.at(i, j + 1))
                    for h in range(HP):
                        mm = pe.transpose(bank[(6, 0)[j] + h // 4][:, (h % 4) * P:(h % 4 + 1) * P],
                                          st[:, j, h // 4, (h % 4) * P:(h % 4 + 1) * P], ident)
                    mm.then_inc(sa_done.sem, 1)
                for j in range(PT):
                    for k in range(KD):
                        mm = pe.matmul(bank[2 + j][:], y_t[:, k, j * P:(j + 1) * P], w_a_v[:, k, :], start=(k == 0), stop=(k == KD - 1))
                    mm.then_inc(va_done.sem, 1)
                for j in range(PT):
                    pe.wait_ge(sa_exp.sem, sa_exp.at(i, j + 1))
                    if j == 1:
                        pe.wait_ge(sa_mask.sem, sa_mask.at(i, 4))
                    for h in range(HP):
                        mm = pe.transpose(bank[(4, 0)[j] + h // 4][:, (h % 4) * P:(h % 4 + 1) * P], pa[:, j, h], ident)
                    mm.then_inc(pa_tr.sem, 1)
                for j in range(PT):
                    pe.wait_ge(pa_cop.sem, pa_cop.at(i, j + 1))
                    pe.wait_ge(va_cop.sem, va_cop.at(i, 2))
                    pe.wait_ge(sa_mask.sem, sa_mask.at(i, 2))
                    for h in range(HP):
                        mm = pe.matmul(bank[(6, 2)[j] + h // 4][:, (h % 4) * P:(h % 4 + 1) * P], pa_t[:, j, h, :],
                                       va[:, j, :, h * T:(h + 1) * T], start=True, stop=True)
                    mm.then_inc(pva.sem, 1)

            def project_outputs(i, more):
                if more:
                    pe.wait_ge(oa_norm.sem, oa_norm.at(i, 1))
                    turn_keys(i + 1, 0)
                for j in range(PT):
                    pe.wait_ge(oa_norm.sem, oa_norm.at(i, j + 1))
                    pe.wait_ge(pa_cop.sem, pa_cop.at(i, 1))
                    for c in range(4):
                        mm = pe.transpose(bank[4 + j][:, c * P:(c + 1) * P], oa[:, j, c // 2, c % 2], ident)
                    mm.then_inc(oa_tr.sem, 1)
                for j in range(PT):
                    pe.wait_ge(oa_cop.sem, oa_cop.at(i, j + 1))
                    pe.wait_ge(pa_cop.sem, pa_cop.at(i, 2))
                    for k in range(KD):
                        mm = pe.matmul(bank[j][:], oa_t[:, j, k, :], w_a_o[:, k, :], start=(k == 0), stop=(k == KD - 1))
                    mm.then_inc(z_done.sem, 1)

            def experts(i, more):
                for j in range(PT):
                    if j == 1 and more:
                        turn_keys(i + 1, 1)
                    pe.wait_ge(resid.sem, resid.at(i, j + 1))
                    pe.wait_ge(oa_norm.sem, oa_norm.at(i, 2))
                    for k in range(KD):
                        mm = pe.transpose(bank[2 + j][:, k * P:(k + 1) * P], xh[:, j, k * P:(k + 1) * P], ident)
                    mm.then_inc(x_tr.sem, 1)
                for j in range(PT):
                    pe.wait_ge(x_cop.sem, x_cop.at(i, j + 1))
                    for b in range(2):
                        pe.wait_ge(we_loaded[2 * j + b], i * 16 + 16)
                    for k in range(KD):
                        for b in range(2):
                            mm = pe.matmul(bank[4 + j][64 * b:64 * b + 64, :], x_t[:, j, k, b * T:(b + 1) * T],
                                           w_exp[:, 2 * j + b, k, :], start=(k == 0), stop=(k == KD - 1))
                    mm.then_inc(c_done.sem, 1)

            def turn(i, more):
                attend(i)
                self_attention(i)
                project_outputs(i, more)
                experts(i, more)

            turn_keys(0, 0)
            turn_keys(0, 1)
            with pe.Fori(0, TURNS - 1) as i:
                turn(i, True)
            turn(TURNS - 1, False)

            pe.wait_ge(sc_cop.sem, sc_cop.at(TURNS, 0))
            pe.wait_ge(x_cop.sem, x_cop.at(TURNS, 0))
            pe.transpose(bank[0][0:PAIRS, 0:P], score, ident).then_inc(s_sct, 1)

            def turn_rows(n, use):
                pe.wait_ge(fh_ready.sem, fh_ready.at(0, use + 1))
                if use == 0:
                    pe.wait_ge(hid.sem, hid.at(TURNS, 0))
                if use >= 2:
                    pe.wait_ge(fo_cop.sem, fo_cop.at(0, FH))
                for k in range(KD):
                    mm = pe.transpose(bank[1 + n][:, k * P:(k + 1) * P], fh[:, n, k * P:(k + 1) * P], ident)
                mm.then_inc(fh_tr.sem, 1)

            def turn_heads(c, n):
                use = 2 * c + n
                pe.wait_ge(f_rope.sem, f_rope.at(0, use + 1))
                if use >= 4:
                    pe.wait_ge(fq_cop.sem, fq_cop.at(0, use + 1 - 4))
                else:
                    pe.wait_ge(fh_cop.sem, fh_cop.at(0, 2))
                    pe.wait_ge(s_pick, 1)
                for h in range(4):
                    mm = pe.transpose(bank[use % 4][:, h * P:(h + 1) * P], fq[:, n, c * 512 + h * P:c * 512 + (h + 1) * P], ident)
                mm.then_inc(fq_tr.sem, 1)

            pe.wait_ge(s_pick, PICKS)
            pe.wait_ge(x_cop.sem, x_cop.at(TURNS, 0))
            for kind in range(2):
                for n in range(SN):
                    mm = pe.matmul(bank[3][:, kind * SN + n:kind * SN + n + 1],
                                   spread[0:PAIRS, kind].rearrange("p q j -> p (q j)")[:, n * P:(n + 1) * P], one[0:PAIRS], start=True, stop=True)
            mm.then_inc(s_pick, 1)
            for n in range(SN):
                turn_rows(n, n)
            for c in range(NQKV):
                pe.wait_ge(r_landed[c % RING], 16 * (c // RING + 1))
                for n in range(SN):
                    use = 2 * c + n
                    if c == 0:
                        pe.wait_ge(fh_cop.sem, fh_cop.at(0, n + 1))
                    if use >= 4:
                        pe.wait_ge(fq_bias.sem, fq_bias.at(0, use + 1 - 4))
                    for k in range(KD):
                        mm = pe.matmul(bank[4 + use % 4][:], fh_t[:, k, n * P:(n + 1) * P], ring[:, c % RING, k, :], start=(k == 0), stop=(k == KD - 1))
                    mm.then_inc(fq_mm.sem, 1)
                if 2 <= c < 8:
                    for n in range(SN):
                        turn_heads(c - 2, n)
            PARTS = ((0, 0, P), (1, P, P + S))

            def f_scores(h):
                if h < 2:
                    pe.wait_ge(fq_cop.sem, fq_cop.at(0, 12))
                    pe.wait_ge(fq_bias.sem, fq_bias.at(0, 16))
                else:
                    pe.wait_ge(fmask.sem, fmask.at(0, 2 * (h - 1)))
                for n, lo, hi in PARTS:
                    mm = pe.matmul(bank[h % 2][:, lo:hi], fq_t[:, h, n * P:(n + 1) * P], fk_t[:, h // 2, 0:hi - lo], start=True, stop=True)
                mm.then_inc(fs.sem, 1)

            def f_turn(h):
                pe.wait_ge(fnorm.sem, fnorm.at(0, 2 * (h + 1)))
                if h >= 2:
                    pe.wait_ge(fp_cop.sem, fp_cop.at(0, h + 1 - 2))
                for c in range(3):
                    mm = pe.transpose(bank[2 + h % 2][:, c * P:(c + 1) * P], fp[:, h % 4, c * P:(c + 1) * P], ident)
                mm.then_inc(fp_tr.sem, 1)

            def f_weigh(h):
                pe.wait_ge(fp_cop.sem, fp_cop.at(0, h + 1))
                if h >= 4:
                    pe.wait_ge(fo_cop.sem, fo_cop.at(0, h + 1 - 4))
                v0 = (FH + FKV) * FHD + (h // 2) * FHD
                for n, lo, hi in PARTS:
                    for c in range(n + 1):
                        mm = pe.matmul(bank[4 + h % 4][:, n * P:(n + 1) * P], fq[:, c, v0:v0 + FHD], fp_t[:, h % 2, lo + c * P:lo + (c + 1) * P],
                                       start=(c == 0), stop=(c == n))
                mm.then_inc(fpv.sem, 1)

            for t in range(FH + 3):
                if t < FH:
                    f_scores(t)
                if 2 <= t < FH + 2:
                    f_turn(t - 2)
                if t >= 3:
                    f_weigh(t - 3)
            pe.wait_ge(fo_cop.sem, fo_cop.at(0, FH))
            for n in range(SN):
                for h in range(FH):
                    c = NQKV + h // 4
                    pe.wait_ge(r_landed[c % RING], 16 * (c // RING + 1))
                    mm = pe.matmul(bank[6 + n][:], fo_t[:, h, n * P:(n + 1) * P], ring[:, c % RING, h % 4, :], start=(h == 0), stop=(h == FH - 1))
                    if n == SN - 1 and h % 4 == 3 or h == FH - 1 and n == 0:
                        mm.then_inc(fwo.sem, 1)
            def gate_up(f, tiles):
                c = NQKV + 4 + 2 * (f // 4)
                cols = slice(tiles[0] * P, (tiles[-1] + 1) * P)
                for w in range(2):
                    pe.wait_ge(r_landed[(c + w) % RING], 16 * ((c + w) // RING + 1))
                if f >= 4:
                    pe.wait_ge(g_act.sem, g_act.at(0, f + 1 - 4))
                for w in range(2):
                    for k in range(KD):
                        mm = pe.matmul(bank[(3, 4, 5, 0)[f % 4]][:, w * S + cols.start:w * S + cols.stop],
                                       ring[:, (c + w) % RING, k, (f % 4) * P:(f % 4 + 1) * P], fh_t[:, k, cols], start=(k == 0), stop=(k == KD - 1))
                if tiles[-1] == SN - 1:
                    mm.then_inc(g_done.sem, 1)

            turn_rows(0, 2)
            pe.wait_ge(fh_cop.sem, fh_cop.at(0, 3))
            pe.wait_ge(fo_cop.sem, fo_cop.at(0, FH))
            for f in range(2):
                gate_up(f, (0,))
            turn_rows(1, 3)
            pe.wait_ge(fh_cop.sem, fh_cop.at(0, 4))
            for f in range(2):
                gate_up(f, (1,))
            for f in range(2, NIN):
                gate_up(f, (0, 1))
            pe.wait_ge(fh_ready.sem, fh_ready.at(0, 4))
            for n in range(SN):
                for f in range(NIN):
                    c = NQKV + 12 + f // 4
                    pe.wait_ge(r_landed[c % RING], 16 * (c // RING + 1))
                    pe.wait_ge(g_act.sem, g_act.at(0, f + 1))
                    mm = pe.matmul(bank[6 + n][:], act_t[:, f, n * P:(n + 1) * P], ring[:, c % RING, f % 4, :], start=(f == 0), stop=(f == NIN - 1))
                mm.then_inc(f_down.sem, 1)

        @block.scalar
        def _(act):
            for g in (summed, v_copied, rooted, q_copied, misc, exped, p_act, y_act, qa_act, ka_act, st_act, sa_exp, pa_cop, oa_cop, x_cop):
                act.sem_inc(g.sem, g.prime)

            for dst, source in ((blocks_i[0:B, 0:NBLK], a["tables"]), (lens_i[0:B, 0:1], a["lens"]), (k32[0:B, :], a["consts32"])):
                act.dma_start(dst, source).then_inc(s_early, 16)
            act.dma_start(ar.tensor[:, 0:CONST - 1 - PAIRS], a["consts"][:, 0:CONST - 1 - PAIRS]).then_inc(s_consts, 16)
            act.dma_start(scale1, a["qk_scale"].rearrange("p (h d) -> p h d", h=QK)).then_inc(s_consts, 16)

            act.wait_ge(s_consts, 32)

            def squares(t, half, u):
                act.wait_ge(proj.sem, proj.at(t, 1))
                act.wait_ge(rooted.sem, rooted.at(t, 1 - 2))
                for h in range(QK):
                    source = bank[2 * u + h // CH][:, h % CH * CHD:(h % CH + 1) * CHD]
                    ins = nc.scalar.activation(sq[:, h], source, ACT.Square, accum_out=ssum[:, u, h:h + 1])
                ins.then_inc(summed.sem, 1)
                act.wait_ge(kv_stored[u], half * 16 + 16)
                nc.scalar.copy(kvn[:, u, CG * CHD:], bank[2 * u + 1][:, CG * CHD:]).then_inc(v_copied.sem, 1)
                act.wait_ge(summed.sem, summed.at(t, 1))
                act.wait_ge(inverted.sem, inverted.at(t, 1 - 2))
                nc.scalar.activation(root[:, u], ssum[:, u], ACT.Sqrt, bias=eps, scale=1.0 / CHD).then_inc(rooted.sem, 1)

            def copy_queries(t, half, u):
                act.wait_ge(q_tr.sem, q_tr.at(t, 1))
                act.wait_ge(q_stored[u], half * 16 + 16)
                nc.scalar.copy(q_out[:, u].rearrange("p (b n t) -> p n b t", b=2, n=4),
                               bank[4 + u][:].rearrange("p (n b t) -> p n b t", n=4, b=2)).then_inc(q_copied.sem, 1)

            def two_tiles(i):
                for u in range(2):
                    squares(i * 2 + u, i, u)
                    copy_queries(i * 2 + u - 2, i - 1, u)

            squares(0, 0, 0)
            squares(1, 0, 1)
            act.wait_ge(s_win_in, 48)
            for dst, source in ((w_c_o, "w_c_o"), (w_a_q, "w_a_q"), (w_a_k, "w_a_k"), (w_a_v, "w_a_v"), (w_a_o, "w_a_o"), (bq, "bq"), (bk, "bk")):
                act.dma_start(dst, a[source]).then_inc(s_weights, 16)
            for dst, source in ((bv, "bv"), (bo, "bo"), (router, "router")):
                act.dma_start(dst, a[source].partition_broadcast(P)).then_inc(s_weights, 16)
            act.dma_start(expert_id[0:1, :], a["experts"]).then_inc(s_weights, 16)
            with act.Fori(1, 7) as i:
                two_tiles(i)
            act.wait_ge(s_idx_t, 1)
            nc.scalar.copy(cache_idx.rearrange("p h b -> p (h b)"), bank[6][:, 0:2 * B]).then_inc(s_idx, 1)
            nc.scalar.copy(over_idx.rearrange("p h b -> p (h b)"), bank[6][:, 2 * B:4 * B]).then_inc(s_idx, 1)
            for b in range(2):
                r = slice(T * b, T * b + T)
                nc.scalar.copy(fresh_idx[r], bank[6][r, 4 * B:5 * B].rearrange("p (q b) -> p b q", b=2)[:, b]).then_inc(s_idx, 1)
            two_tiles(7)
            for u in range(2):
                copy_queries(PAIRS - 2 + u, PAIRS // 2 - 1, u)

            act.wait_ge(s_weights, 16 * 11)
            act.wait_ge(s_zero, 4)
            for u in range(2):
                act.wait_ge(q_stored[u], 16 * (PAIRS // 2 + 1))
                act.wait_ge(kv_stored[u], 16 * (PAIRS // 2 + 1))

            def copy_keys(i, j):
                act.wait_ge(scored.sem, scored.at(i, 8 * (j + 1) - STEPS))
                act.wait_ge(pva.sem, pva.at(i, 0))
                for n in range(3):
                    use = 3 * j + n
                    act.wait_ge(k_tr.sem, k_tr.at(i, use + 1))
                    w = 4 * P if n < 2 else 2 * P
                    flat = k_t[:, j].rearrange("p g n -> p (g n)")
                    nc.scalar.copy(flat[:, n * 4 * P:n * 4 * P + w], bank[6 + use % 2][:, 0:w]).then_inc(misc.sem, 1)

            def exp_scores(i, s):
                n, b, g = s // 4, s // 4 % 2, s % 4
                act.wait_ge(negated.sem, negated.at(i, s + 1))
                if g == 0:
                    act.wait_ge(recd.sem, recd.at(i, n + 1 - 2))
                cols = pc[:, 2 * b + g % 2, b * T:b * T + SPAN]
                nc.scalar.activation(cols, cols, ACT.Exp, bias=neg_c[:, s % 4:s % 4 + 1], scale=1.0 / 16.0,
                                     accum_out=sum_c[:, b, g:g + 1]).then_inc(exped.sem, 1)

            def copy_probs(i, s):
                act.wait_ge(p_tr.sem, p_tr.at(i, s + 1))
                act.wait_ge(pv_done.sem, pv_done.at(i, s + 1 - 2))
                nc.scalar.copy(pc_t[:, s % 2], bank[2 + s % 2][:, 0:3 * P]).then_inc(p_act.sem, 1)

            def copy_outputs(i, n):
                use = 3 * PT + n
                act.wait_ge(o_tr.sem, o_tr.at(i, n + 1))
                act.wait_ge(z_done.sem, z_done.at(i, 0))
                nc.scalar.copy(o_t[:, :, n * T:(n + 1) * T].rearrange("p (g c) t -> p g c t", g=2),
                               bank[6 + use % 2][:, 0:2 * P].rearrange("p (g c t) -> p g c t", g=2, c=2)).then_inc(misc.sem, 1)

            def attend(i):
                for s in range(STEPS + 4):
                    if s < STEPS:
                        exp_scores(i, s)
                    if 2 <= s < STEPS + 2 and (s - 2) % 4 == 3:
                        copy_probs(i, s - 2)
                    if s >= 7 and (s - 7) % 4 == 0:
                        copy_outputs(i, (s - 7) // 4)

            def self_attention(i, more):
                act.wait_ge(y_done.sem, y_done.at(i, 2))
                nc.scalar.copy(y_t[:, 2:4].rearrange("p m t -> p (m t)"), bank[1][:]).then_inc(y_act.sem, 1)
                act.wait_ge(qa_done.sem, qa_done.at(i, 1))
                for m in range(2):
                    for h in range(4):
                        r = slice(32 * h, 32 * h + 32)
                        ins = nc.scalar.activation(qa_blk[r, m, :, h, :], bank[2][r, m * TT:(m + 1) * TT].rearrange("p (b t) -> p b t", b=BT),
                                                   ACT.Identity, bias=bq[r, m:m + 1])
                ins.then_inc(qa_act.sem, 1)
                act.wait_ge(ka_done.sem, ka_done.at(i, 1))
                for m in range(2):
                    ins = nc.scalar.activation(ka_t[:, m, :], bank[4][:, m * TT:(m + 1) * TT], ACT.Identity, bias=bk[:, m:m + 1])
                ins.then_inc(ka_act.sem, 1)
                for j in range(PT):
                    act.wait_ge(st_done.sem, st_done.at(i, j + 1))
                    nc.scalar.copy(st[:, j, 0], bank[2 + 2 * j][:]).then_inc(st_act.sem, 1)
                for j in range(PT):
                    act.wait_ge(sa_sub.sem, sa_sub.at(i, j + 1))
                    nc.scalar.activation(pa[:, j], pa[:, j], ACT.Exp).then_inc(sa_exp.sem, 1)
                for j in range(PT):
                    act.wait_ge(pa_tr.sem, pa_tr.at(i, j + 1))
                    for half in range(2):
                        ins = nc.scalar.copy(pa_t[:, j, 4 * half:4 * half + 4].rearrange("p h n -> p (h n)"), bank[(4, 0)[j] + half][:])
                    ins.then_inc(pa_cop.sem, 1)
                if more:
                    copy_keys(i + 1, 0)
                for j in range(PT):
                    act.wait_ge(oa_tr.sem, oa_tr.at(i, j + 1))
                    for c in range(2):
                        ins = nc.scalar.copy(oa_t[:, j, 2 * c:2 * c + 2].rearrange("p h (b t) -> p b h t", b=2),
                                             bank[4 + j][:, 2 * c * P:2 * (c + 1) * P].rearrange("p (b h t) -> p b h t", b=2, h=2))
                    ins.then_inc(oa_cop.sem, 1)
                for j in range(PT):
                    if j == 1 and more:
                        copy_keys(i + 1, 1)
                    act.wait_ge(x_tr.sem, x_tr.at(i, j + 1))
                    nc.scalar.copy(x_t[:, j].rearrange("p k n -> p (k n)"), bank[2 + j][:]).then_inc(x_cop.sem, 1)

            copy_keys(0, 0)
            copy_keys(0, 1)
            with act.Fori(0, TURNS - 1) as i:
                attend(i)
                self_attention(i, True)
            attend(TURNS - 1)
            self_attention(TURNS - 1, False)

            def root_mean_square(n, use):
                source = sel[:, n, D:] if use < 2 else x1[:, n]
                nc.scalar.activation(fjunk, source, ACT.Square, accum_out=small[:, use:use + 1]).then_inc(s_rms, 1)
                act.wait_ge(s_rms, 2 * use + 1)
                nc.scalar.activation(small[:, 4 + use:5 + use], small[:, use:use + 1], ACT.Sqrt, bias=eps, scale=1.0 / D).then_inc(s_rms, 1)

            def copy_rows(n, use):
                act.wait_ge(fh_tr.sem, fh_tr.at(0, use + 1))
                nc.scalar.copy(fh_t[:, :, n * P:(n + 1) * P], bank[1 + n][:].rearrange("p (k n) -> p k n", k=KD)).then_inc(fh_cop.sem, 1)

            for n in range(SN):
                act.wait_ge(s_sel[n], 16)
                if n == 1:
                    act.wait_ge(s_rms, 2)
                root_mean_square(n, n)
            for n in range(SN):
                copy_rows(n, n)
            for c in range(6):
                for n in range(SN):
                    act.wait_ge(fq_tr.sem, fq_tr.at(0, 2 * c + n + 1))
                    dst = fq_t[:, 4 * c:4 * c + 4, n * P:(n + 1) * P] if c < 4 else fk_t[:, 4 * (c - 4):4 * (c - 4) + 4, n * P:(n + 1) * P]
                    nc.scalar.copy(dst, bank[(2 * c + n) % 4][:].rearrange("p (h n) -> p h n", h=4)).then_inc(fq_cop.sem, 1)
            for t in range(FH + 4):
                if t < FH:
                    act.wait_ge(fneg.sem, fneg.at(0, t + 1))
                    if t >= 4:
                        act.wait_ge(frec.sem, frec.at(0, t + 1 - 4))
                    for n, lo, hi in ((0, 0, P), (1, P, P + S)):
                        nc.scalar.activation(fp[:, t % 4, lo:hi], fp[:, t % 4, lo:hi], ACT.Exp, bias=f_neg[:, t % 4, n:n + 1],
                                             scale=float(FHD) ** -0.5, accum_out=f_sum[:, t % 4, n:n + 1]).then_inc(fexp.sem, 1)
                if 2 <= t < FH + 2:
                    h = t - 2
                    act.wait_ge(fp_tr.sem, fp_tr.at(0, h + 1))
                    if h >= 2:
                        act.wait_ge(fpv.sem, fpv.at(0, h + 1 - 2))
                    nc.scalar.copy(fp_t[:, h % 2], bank[2 + h % 2][:, 0:P + S]).then_inc(fp_cop.sem, 1)
                if t >= 4:
                    h = t - 4
                    act.wait_ge(fpv.sem, fpv.at(0, h + 1))
                    nc.scalar.copy(fo_t[:, h], bank[4 + h % 4][:, 0:S]).then_inc(fo_cop.sem, 1)
            for n in range(SN):
                act.wait_ge(f_x1.sem, f_x1.at(0, n + 1))
                act.wait_ge(s_rms, 2 * (2 + n))
                root_mean_square(n, 2 + n)
                copy_rows(n, 2 + n)
            for n in range(SN):
                nc.scalar.activation(small[:, 12 + n:13 + n], small[:, 8 + n:9 + n], ACT.Exp, scale=-1.0).then_inc(s_esc, 1)
            for f in range(NIN):
                act.wait_ge(g_done.sem, g_done.at(0, f + 1))
                if f >= 2:
                    act.wait_ge(g_act.sem, g_act.at(0, f + 1 - 2))
                nc.scalar.activation(e_g[:, f % 2], bank[(3, 4, 5, 0)[f % 4]][:, 0:S], ACT.Exp, scale=-1.0).then_inc(g_exp.sem, 1)

        @block.vector
        def _(dve):
            for g in (inverted, normed, scaled, turned_v, cosd, roped, same_p, src_v, masked, negated, p_dve, recd, o_norm,
                      y_dve, qa_dve, ka_dve, st_dve, sa_mask, sa_max, sa_sum, sa_rec, va_cop, oa_norm, resid, hid, rscore, sc_cop):
                dve.sem_inc(g.sem, g.prime)

            steps = [0]

            def step(ins):
                steps[0] += 1
                ins.then_inc(s_pre, 1)
                dve.wait_ge(s_pre, steps[0])

            dve.wait_ge(s_lens, 32)
            step(nc.vector.tensor_copy(posf, len_all[:, 0:PAIRS]))
            step(nc.vector.tensor_scalar(pos_idx, posf, seq_base[:, 0:1], None, ALU.add))
            step(nc.vector.tensor_scalar(first_seen, len_all[:, PAIRS:], -1.0, float(WINDOW), ALU.mult, ALU.add))
            dve.wait_ge(s_early, 48)
            step(nc.vector.tensor_copy(blocks[0:B], blocks_i[0:B]))
            step(nc.vector.tensor_scalar(lens_i[0:B, 1:2], lens_i[0:B, 0:1], 4, None, ALU.logical_shift_right))
            step(nc.vector.tensor_scalar(lens_i[0:B, 2:3], lens_i[0:B, 0:1], BLOCK - 1, None, ALU.bitwise_and))
            for k in range(4):
                step(nc.vector.tensor_scalar(lens_i[0:B, 3 + k:4 + k], lens_i[0:B, 0:1], k, 1, ALU.logical_shift_right, ALU.bitwise_and))
            step(nc.vector.tensor_copy(lens[0:B, 0:7], lens_i[0:B, 0:7]))
            iota_blk = k32[0:B, 0:NBLK]
            iota_slot = k32[0:B, NBLK:NBLK + WSLOTS]
            iota_new = k32[0:B, NBLK + WSLOTS:NBLK + WSLOTS + NSLOTS * BLOCK]
            token1 = k32[0:B, NBLK + WSLOTS + NSLOTS * BLOCK:NBLK + WSLOTS + NSLOTS * BLOCK + 1]
            iota_off = k32[0:B, NBLK + WSLOTS + NSLOTS * BLOCK + 1:]
            step(nc.vector.tensor_scalar(slot_no[0:B], iota_slot, lens[0:B, 1:2], float(-WINDOW // BLOCK), ALU.add, ALU.add))
            for k in range(WSLOTS):
                step(nc.vector.scalar_tensor_tensor(out=hit[0:B], in0=iota_blk, scalar=slot_no[0:B, k:k + 1], in1=blocks[0:B],
                                                    op0=ALU.is_equal, op1=ALU.mult, accum_out=win[0:B, k:k + 1]))
            step(nc.vector.tensor_scalar(tok[0:B, 0], iota_new, lens[0:B, 2:3], None, ALU.subtract))
            step(nc.vector.tensor_scalar(tok[0:B, 1], tok[0:B, 0], 0.0, None, ALU.is_ge))
            step(nc.vector.scalar_tensor_tensor(out=tok[0:B, 1], in0=tok[0:B, 0], scalar=float(T), in1=tok[0:B, 1], op0=ALU.is_lt, op1=ALU.mult))
            step(nc.vector.scalar_tensor_tensor(out=tok[0:B, 2], in0=tok[0:B, 0], scalar=token1, in1=tok[0:B, 1], op0=ALU.add, op1=ALU.mult))
            assert steps[0] == PRE_WIN
            step(nc.vector.scalar_tensor_tensor(out=al[0:B, 0, 0].rearrange("p (s o) -> p s o", o=BLOCK),
                                                in0=win[0:B].unsqueeze(2).to_broadcast([B, WSLOTS, BLOCK]), scalar=float(BLOCK),
                                                in1=iota_off.unsqueeze(1).to_broadcast([B, WSLOTS, BLOCK]), op0=ALU.mult, op1=ALU.add))
            dve.wait_ge(s_consts, 32)
            step(nc.vector.tensor_scalar(scale1, scale1, 1.0, None, ALU.add))
            assert steps[0] == PRE_ALL

            def compare(g, par):
                dve.wait_ge(prod_p.sem, prod_p.at(g, 1 - 2))
                nc.vector.tensor_tensor(same[0:GP, par], blk_w[0:GP], blk_r[0:GP, bass.ds(g, 1)].to_broadcast([GP, WRITERS]),
                                        ALU.is_equal).then_inc(same_p.sem, 1)

            def last_writers(g, par):
                dve.wait_ge(prod_p.sem, prod_p.at(g, 1))
                nc.vector.tensor_reduce(src[0:GP, bass.ds(g, 1)].rearrange("p a o -> p (a o)"), prod[par][0:GP], AX.X, ALU.max).then_inc(src_v.sem, 1)

            def tile(t, half, u):
                dve.wait_ge(rooted.sem, rooted.at(t, 1))
                nc.vector.reciprocal(inv[:, u], root[:, u]).then_inc(inverted.sem, 1)
                dve.wait_ge(inverted.sem, inverted.at(t, 1))
                dve.wait_ge(turned_p.sem, turned_p.at(t, 1 - 2))
                for lo, hi, part in ((0, CH, 0), (CH, QK, 1)):
                    nc.vector.tensor_tensor(qk[:, u, lo:hi].rearrange("p h a d -> p h (a d)"),
                                            bank[2 * u + part][:, 0:(hi - lo) * CHD].rearrange("p (h d) -> p h d", h=hi - lo),
                                            inv[:, u, lo:hi].unsqueeze(2).to_broadcast([P, hi - lo, CHD]), ALU.mult).then_inc(normed.sem, 1)
                dve.wait_ge(normed.sem, normed.at(t, 2))
                flat = qk[:, u].rearrange("p h a d -> p h (a d)")
                nc.vector.tensor_tensor(flat, flat, scale1, ALU.mult).then_inc(scaled.sem, 1)
                dve.wait_ge(scaled.sem, scaled.at(t, 1))
                cos = rope[:, bass.ds(t, 1), 0:32].unsqueeze(2).to_broadcast([P, QK, 2, 32])
                sin = rope[:, bass.ds(t, 1), 64:96].to_broadcast([P, QK, 32])
                nc.vector.tensor_tensor(qk_cos[:, u], qk[:, u], cos, ALU.mult).then_inc(cosd.sem, 1)
                nc.vector.tensor_tensor(turned[:, u, :, 1, :], qk[:, u, :, 0, :], sin, ALU.mult).then_inc(turned_v.sem, 1)
                dve.wait_ge(cosd.sem, cosd.at(t, 1))
                dve.wait_ge(turned_v.sem, turned_v.at(t, 1))
                dve.wait_ge(turned_p.sem, turned_p.at(t, 1))
                dve.wait_ge(q_tr.sem, q_tr.at(t, 1 - 2))
                nc.vector.tensor_tensor(qr[:, u], qk_cos[:, u, 0:CH].rearrange("p h a d -> p (h a d)"),
                                        turned[:, u, 0:CH].rearrange("p h a d -> p (h a d)"), ALU.add).then_inc(roped.sem, 1)
                dve.wait_ge(kv_stored[u], half * 16 + 16)
                nc.vector.tensor_tensor(kvn[:, u, 0:CG * CHD], qk_cos[:, u, CH:].rearrange("p h a d -> p (h a d)"),
                                        turned[:, u, CH:].rearrange("p h a d -> p (h a d)"), ALU.add).then_inc(roped.sem, 1)

            dve.wait_ge(s_rope, 16 * PAIRS)
            tile(0, 0, 0)
            dve.wait_ge(s_win_in, 48)
            compare(0, 0)
            tile(1, 0, 1)
            with dve.Fori(1, 4) as i:
                for u in range(2):
                    compare(i * 2 + u - 1, 1 - u)
                    tile(i * 2 + u, i, u)
                    last_writers(i * 2 + u - 2, u)
            compare(GROUPS - 1, 1)
            tile(GROUPS, GROUPS // 2, 0)
            last_writers(GROUPS - 2, 0)
            tile(GROUPS + 1, GROUPS // 2, 1)
            last_writers(GROUPS - 1, 1)
            for u in range(2):
                tile(GROUPS + 2 + u, GROUPS // 2 + 1, u)

            dve.wait_ge(s_src_in, 16)
            cur, n = 0, WPOS
            for k in (3, 2, 1, 0):
                n -= 1 << k
                here, there = al[0:B, cur], al[0:B, 1 - cur, :, 0:n]
                step(nc.vector.tensor_tensor(there, here[:, :, 1 << k:n + (1 << k)], here[:, :, 0:n], ALU.subtract))
                step(nc.vector.scalar_tensor_tensor(out=there, in0=there, scalar=lens[0:B, 3 + k:4 + k], in1=here[:, :, 0:n], op0=ALU.mult, op1=ALU.add))
                cur = 1 - cur
            rows, last = al[0:B, cur, 0, 0:SPAN], al[0:B, cur, 1, 0:SPAN]
            step(nc.vector.tensor_scalar(idx_f[0:B, 3], last, 0.0, SKIP, ALU.is_gt, ALU.mult))
            step(nc.vector.tensor_tensor(idx_f[0:B, 0], rows, idx_f[0:B, 3], ALU.add))
            step(nc.vector.tensor_scalar(idx_f[0:B, 3], last, 0.0, SKIP, ALU.is_equal, ALU.mult))
            step(nc.vector.scalar_tensor_tensor(out=idx_f[0:B, 1], in0=last, scalar=-1.0, in1=idx_f[0:B, 3], op0=ALU.add, op1=ALU.add))
            step(nc.vector.tensor_copy(idx_f[0:B, 2, 0:P].rearrange("p (c t) -> p c t", c=2),
                                       idx_f[0:B, 1, WINDOW:SPAN].unsqueeze(1).to_broadcast([B, 2, T])))
            assert steps[0] == PRE_IDX
            with dve.Fori(6, 8) as i:
                for u in range(2):
                    tile(i * 2 + u, i, u)

            dve.wait_ge(s_weights, 16 * 11)
            dve.wait_ge(s_zero, 4)
            for u in range(2):
                dve.wait_ge(q_stored[u], 16 * (PAIRS // 2 + 1))
                dve.wait_ge(kv_stored[u], 16 * (PAIRS // 2 + 1))

            def mask_scores(i, s):
                n, b, g = s // 4, s // 4 % 2, s % 4
                dve.wait_ge(scored.sem, scored.at(i, s + 1))
                if g == 0:
                    dve.wait_ge(masks.sem, masks.at(i, n + 1))
                dve.wait_ge(p_tr.sem, p_tr.at(i, s + 1 - 2))
                dve.wait_ge(exped.sem, exped.at(i, s + 1 - 4))
                dve.sem_inc(s_passed, 1)
                nc.vector.tensor_tensor_reduce(out=pc[:, 2 * b + g % 2, b * T:b * T + SPAN], in0=bank[s % 2][:, 0:SPAN], in1=mk[:, b],
                                               scale=1.0, scalar=-3.0e38, op0=ALU.add, op1=ALU.max,
                                               accum_out=top_c[:, s % 4:s % 4 + 1]).then_inc(masked.sem, 1)
                dve.wait_ge(masked.sem, masked.at(i, s + 1))
                nc.vector.tensor_scalar(neg_c[:, s % 4:s % 4 + 1], top_c[:, s % 4:s % 4 + 1], -1.0 / 16.0, None, ALU.mult).then_inc(negated.sem, 1)

            def copy_probs(i, s):
                dve.wait_ge(p_tr.sem, p_tr.at(i, s + 1))
                dve.wait_ge(pv_done.sem, pv_done.at(i, s + 1 - 2))
                nc.vector.tensor_copy(pc_t[:, s % 2], bank[2 + s % 2][:, 0:3 * P]).then_inc(p_dve.sem, 1)

            def norm_outputs(i, n):
                dve.wait_ge(exped.sem, exped.at(i, 4 * n + 4))
                nc.vector.reciprocal(rec_c[:, n % 2], sum_c[:, n % 2]).then_inc(recd.sem, 1)
                dve.wait_ge(recd.sem, recd.at(i, n + 1))
                dve.wait_ge(pv_done.sem, pv_done.at(i, 4 * n + 4))
                dve.wait_ge(o_tr.sem, o_tr.at(i, n + 1 - 2))
                nc.vector.tensor_tensor(oc[:, n % 2].rearrange("p (g d) -> p g d", g=CG),
                                        bank[4 + n % 2][:, 0:CG * CHD].rearrange("p (g d) -> p g d", g=CG),
                                        rec_c[:, n % 2].unsqueeze(2).to_broadcast([P, CG, CHD]), ALU.mult).then_inc(o_norm.sem, 1)

            def attend(i):
                for s in range(STEPS + 3):
                    if s < STEPS:
                        mask_scores(i, s)
                    if 2 <= s < STEPS + 2 and (s - 2) % 4 != 3:
                        copy_probs(i, s - 2)
                    if s >= 6 and (s - 6) % 4 == 0:
                        norm_outputs(i, (s - 6) // 4)

            def self_attention(i):
                dve.wait_ge(y_done.sem, y_done.at(i, 1))
                dve.wait_ge(c_done.sem, c_done.at(i, 0))
                nc.vector.tensor_copy(y_t[:, 0:2].rearrange("p m t -> p (m t)"), bank[0][:]).then_inc(y_dve.sem, 1)
                dve.wait_ge(qa_done.sem, qa_done.at(i, 2))
                for m in range(2):
                    for h in range(4):
                        r = slice(32 * h, 32 * h + 32)
                        ins = nc.vector.tensor_scalar(qa_blk[r, 2 + m, :, h, :], bank[3][r, m * TT:(m + 1) * TT].rearrange("p (b t) -> p b t", b=BT),
                                                      bq[r, 2 + m:3 + m], None, ALU.add)
                ins.then_inc(qa_dve.sem, 1)
                dve.wait_ge(ka_done.sem, ka_done.at(i, 2))
                for m in range(2):
                    ins = nc.vector.tensor_scalar(ka_t[:, 2 + m, :], bank[5][:, m * TT:(m + 1) * TT], bk[:, 2 + m:3 + m], None, ALU.add)
                ins.then_inc(ka_dve.sem, 1)
                for j in range(PT):
                    dve.wait_ge(st_done.sem, st_done.at(i, PT + j + 1))
                    nc.vector.tensor_copy(st[:, j, 1], bank[3 + 2 * j][:]).then_inc(st_dve.sem, 1)
                for j in range(PT):
                    dve.wait_ge(sa_done.sem, sa_done.at(i, j + 1))
                    for half in range(2):
                        nc.vector.scalar_tensor_tensor(out=pa[:, j, 4 * half:4 * half + 4].rearrange("p h b t -> p (h b) t"),
                                                       in0=bank[(6, 0)[j] + half][:].rearrange("p (n t) -> p n t", t=T), scalar=float(AHD) ** -0.5,
                                                       in1=mask_a.unsqueeze(1).to_broadcast([P, 8, T]), op0=ALU.mult, op1=ALU.add).then_inc(sa_mask.sem, 1)
                    dve.wait_ge(sa_mask.sem, sa_mask.at(i, 2 * j + 2))
                    nc.vector.tensor_reduce(top_a[:, j], pa[:, j].rearrange("p h b t -> p (h b) t"), AX.X, ALU.max).then_inc(sa_max.sem, 1)
                for j in range(PT):
                    dve.wait_ge(va_done.sem, va_done.at(i, j + 1))
                    for b in range(2):
                        r = slice(64 * b, 64 * b + 64)
                        ins = nc.vector.tensor_tensor(va[r, j, b, :], bank[2 + j][r, :], bv[r, :], ALU.add)
                    ins.then_inc(va_cop.sem, 1)
                for j in range(PT):
                    dve.wait_ge(sa_exp.sem, sa_exp.at(i, j + 1))
                    nc.vector.tensor_reduce(sum_a[:, j], pa[:, j].rearrange("p h b t -> p (h b) t"), AX.X, ALU.add).then_inc(sa_sum.sem, 1)
                    dve.wait_ge(sa_sum.sem, sa_sum.at(i, j + 1))
                    nc.vector.reciprocal(rec_a[:, j], sum_a[:, j]).then_inc(sa_rec.sem, 1)
                    dve.wait_ge(sa_rec.sem, sa_rec.at(i, j + 1))
                    dve.wait_ge(pva.sem, pva.at(i, j + 1))
                    for c in range(2):
                        for r in range(2):
                            rows_r = slice(64 * r, 64 * r + 64)
                            ins = nc.vector.tensor_tensor(
                                oa[rows_r, j, c].rearrange("p b h d -> p h b d"),
                                bank[(6, 2)[j] + c][rows_r, :].rearrange("p (h b r d) -> p h b r d", b=2, r=2, d=AHD)[:, :, :, r, :],
                                rec_a[rows_r, j, 8 * c:8 * c + 8].rearrange("p (h b) -> p h b", b=2).unsqueeze(3).to_broadcast([64, 4, 2, AHD]), ALU.mult)
                    ins.then_inc(oa_norm.sem, 1)
                for j in range(PT):
                    dve.wait_ge(z_done.sem, z_done.at(i, j + 1))
                    dve.wait_ge(x_bias.sem, x_bias.at(i, j + 1))
                    dve.wait_ge(xh_stored[j], i * 16 + 16)
                    nc.vector.tensor_tensor(xh[:, j, 0:D], bank[j][:], xr[:, j], ALU.add).then_inc(resid.sem, 1)
                for j in range(PT):
                    dve.wait_ge(c_done.sem, c_done.at(i, j + 1))
                    dve.wait_ge(be_loaded[j], i * 32 + 32)
                    nc.vector.tensor_tensor(xh[:, j, D:], bank[4 + j][:], b_exp[:, j], ALU.add).then_inc(hid.sem, 1)
                    dve.wait_ge(hid.sem, hid.at(i, j + 1))
                    dve.wait_ge(rscore.sem, rscore.at(i, j))
                    dve.wait_ge(sc_cop.sem, sc_cop.at(i, 0))
                    nc.vector.tensor_tensor_reduce(out=junk, in0=xh[:, j, D:], in1=router, scale=1.0, scalar=0.0, op0=ALU.mult, op1=ALU.add,
                                                   accum_out=score_t[:, j:j + 1]).then_inc(rscore.sem, 1)
                dve.wait_ge(rscore.sem, rscore.at(i, PT))
                nc.vector.tensor_copy(score[:, bass.ds(i * PT, PT)], score_t).then_inc(sc_cop.sem, 1)

            with dve.Fori(0, TURNS) as i:
                attend(i)
                self_attention(i)

            picks = [0]

            def pick_step(ins):
                picks[0] += 1
                ins.then_inc(s_pick, 1)
                dve.wait_ge(s_pick, picks[0])

            Q = PAIRS
            for j in range(PT):
                dve.wait_ge(xh_stored[j], 16 * (TURNS + 1))
                dve.wait_ge(out_stored[j], 16 * (TURNS + 1))
            dve.wait_ge(s_sct, 1)
            pick_step(nc.vector.tensor_copy(score_b[0:Q], bank[0][0:Q, 0:P]))
            for b in range(2):
                pick_step(nc.vector.max(top8[0:Q, b], score_b[0:Q, b * T:(b + 1) * T]))
            for b in range(2):
                pick_step(nc.vector.max_index(at8[0:Q, b], top8[0:Q, b], score_b[0:Q, b * T:(b + 1) * T]))
            pick_step(nc.vector.tensor_scalar(neg8[0:Q], at8[0:Q], -1.0, None, ALU.mult))
            for b in range(2):
                pick_step(nc.vector.max(sorted8[0:Q, b], neg8[0:Q, b]))
            pick_step(nc.vector.tensor_scalar(pick8[0:Q, 0], sorted8[0:Q], -1.0, None, ALU.mult))
            for b in range(2):
                pick_step(nc.vector.tensor_scalar(pick8[0:Q, 1, b], sorted8[0:Q, b], -1.0, seq_base[0:Q, 1 + b:2 + b], ALU.mult, ALU.add))
            for kind in range(2):
                pick_step(nc.vector.tensor_tensor(spread[0:Q, kind], pick8[0:Q, kind].rearrange("p b j -> p (b j)").unsqueeze(1).to_broadcast([Q, Q, 2 * KEEP]),
                                                  ident[0:Q, 0:Q].unsqueeze(2).to_broadcast([Q, Q, 2 * KEEP]), ALU.mult))
            assert picks[0] == PICKS
            dve.wait_ge(s_pick, PICKS + 1)
            nc.vector.tensor_copy(picked.rearrange("p k n -> p (k n)"), bank[3][:, 0:2 * SN]).then_inc(s_pick, 1)

            def norm_rows(n, use):
                dve.wait_ge(s_rms, 2 * (use + 1))
                nc.vector.reciprocal(small[:, 16 + use:17 + use], small[:, 4 + use:5 + use]).then_inc(s_gate, 1)
                dve.wait_ge(s_gate, use + 1 if use < 2 else use + 3)
                if use >= 2:
                    dve.wait_ge(fh_tr.sem, fh_tr.at(0, 2))
                source, weight = (sel[:, n, D:], ln1) if use < 2 else (x1[:, n], ln2)
                nc.vector.scalar_tensor_tensor(out=fh[:, n], in0=source, scalar=small[:, 16 + use:17 + use], in1=weight,
                                               op0=ALU.mult, op1=ALU.mult).then_inc(fh_ready.sem, 1)

            dve.wait_ge(s_fin, 48)
            for n in range(SN):
                dve.wait_ge(s_sel[n], 16)
                norm_rows(n, n)
            dve.wait_ge(s_frope, 32)
            for n in range(SN):
                nc.vector.tensor_tensor_reduce(out=x1[:, n], in0=sel[:, n, D:], in1=router, scale=1.0, scalar=0.0, op0=ALU.mult, op1=ALU.add,
                                               accum_out=small[:, 8 + n:9 + n]).then_inc(s_gate, 1)
            for c in range(NQKV):
                for n in range(SN):
                    use = 2 * c + n
                    x = fq[:, n, c * 512:(c + 1) * 512]
                    dve.wait_ge(fq_mm.sem, fq_mm.at(0, use + 1))
                    nc.vector.tensor_tensor(x, bank[4 + use % 4][:], fbias[:, c * 512:(c + 1) * 512], ALU.add).then_inc(fq_bias.sem, 1)
                    if c < 6:
                        dve.wait_ge(fq_bias.sem, fq_bias.at(0, use + 1))
                        halves = x.rearrange("p (h a d) -> p h a d", a=2, d=64)
                        co, si = fcos[:, n], fsin[:, n].rearrange("p (h a d) -> p h a d", a=2, d=64)
                        nc.vector.tensor_tensor(co.rearrange("p (h d) -> p h d", d=64), x.rearrange("p (h d) -> p h d", d=64),
                                                frope[:, n, 0:64].unsqueeze(1).to_broadcast([P, 8, 64]), ALU.mult)
                        nc.vector.tensor_tensor(si[:, :, 0, :], halves[:, :, 1, :], frope[:, n, 128:192].unsqueeze(1).to_broadcast([P, 4, 64]), ALU.mult)
                        nc.vector.tensor_tensor(si[:, :, 1, :], halves[:, :, 0, :], frope[:, n, 192:256].unsqueeze(1).to_broadcast([P, 4, 64]),
                                                ALU.mult).then_inc(f_sin.sem, 1)
                        dve.wait_ge(f_sin.sem, f_sin.at(0, use + 1))
                        nc.vector.tensor_tensor(x, co, fsin[:, n], ALU.add).then_inc(f_rope.sem, 1)
            for t in range(FH + 1):
                if t < FH:
                    dve.wait_ge(fs.sem, fs.at(0, t + 1))
                    if t >= 4:
                        dve.wait_ge(fp_tr.sem, fp_tr.at(0, t + 1 - 4))
                    for n, lo, hi in ((0, 0, P), (1, P, P + S)):
                        mask = mask_f[:, 1] if n == 0 else mask_f.rearrange("p a n -> p (a n)")
                        nc.vector.tensor_tensor_reduce(out=fp[:, t % 4, lo:hi], in0=bank[t % 2][:, lo:hi], in1=mask, scale=1.0, scalar=-3.0e38,
                                                       op0=ALU.add, op1=ALU.max, accum_out=f_top[:, t % 4, n:n + 1]).then_inc(fmask.sem, 1)
                    dve.wait_ge(fmask.sem, fmask.at(0, 2 * (t + 1)))
                    nc.vector.tensor_scalar(f_neg[:, t % 4], f_top[:, t % 4], -float(FHD) ** -0.5, None, ALU.mult).then_inc(fneg.sem, 1)
                if t >= 1:
                    h = t - 1
                    dve.wait_ge(fexp.sem, fexp.at(0, 2 * (h + 1)))
                    nc.vector.reciprocal(f_rec[:, h % 4], f_sum[:, h % 4]).then_inc(frec.sem, 1)
                    dve.wait_ge(frec.sem, frec.at(0, h + 1))
                    for n, lo, hi in ((0, 0, P), (1, P, P + S)):
                        nc.vector.tensor_scalar(fp[:, h % 4, lo:hi], fp[:, h % 4, lo:hi], f_rec[:, h % 4, n:n + 1], None, ALU.mult).then_inc(fnorm.sem, 1)
            for n in range(SN):
                dve.wait_ge(fwo.sem, fwo.at(0, 1 if n == 0 else 5))
                nc.vector.tensor_tensor(x1[:, n], bank[6 + n][:], sel[:, n, D:], ALU.add).then_inc(f_x1.sem, 1)
                norm_rows(n, 2 + n)
            dve.wait_ge(s_esc, 2)
            nc.vector.tensor_scalar(small[:, 12:14], small[:, 12:14], 1.0, None, ALU.add).then_inc(s_gate, 1)
            dve.wait_ge(s_gate, 7)
            nc.vector.reciprocal(small[:, 14:16], small[:, 12:14]).then_inc(s_gate, 1)
            dve.wait_ge(s_gate, 8)
            nc.vector.tensor_scalar(small[:, 36:38], small[:, 14:16], -1.0, 1.0, ALU.mult, ALU.add).then_inc(s_gate, 1)
            dve.wait_ge(s_gate, 9)
            for f in range(NIN):
                if f < SN:
                    nc.vector.scalar_tensor_tensor(out=pre[:, f], in0=sel[:, f, D:], scalar=small[:, 36 + f:37 + f], in1=sel[:, f, 0:D],
                                                   op0=ALU.mult, op1=ALU.add).then_inc(s_last, 1)
                    dve.wait_ge(s_last, 2 * f + 1)
                    nc.vector.scalar_tensor_tensor(out=pre[:, f], in0=x1[:, f], scalar=small[:, 14 + f:15 + f], in1=pre[:, f],
                                                   op0=ALU.mult, op1=ALU.add).then_inc(s_last, 1)
                gb = bank[(3, 4, 5, 0)[f % 4]]
                r = r_g[:, f % 2]
                dve.wait_ge(g_exp.sem, g_exp.at(0, f + 1))
                nc.vector.tensor_scalar(r, e_g[:, f % 2], 1.0, None, ALU.add).then_inc(g_one.sem, 1)
                dve.wait_ge(g_one.sem, g_one.at(0, 3 * f + 1))
                nc.vector.reciprocal(r, r).then_inc(g_one.sem, 1)
                dve.wait_ge(g_one.sem, g_one.at(0, 3 * f + 2))
                nc.vector.tensor_tensor(r, r, gb[:, 0:S], ALU.mult).then_inc(g_one.sem, 1)
                dve.wait_ge(g_one.sem, g_one.at(0, 3 * f + 3))
                nc.vector.tensor_tensor(act_t[:, f], r, gb[:, S:2 * S], ALU.mult).then_inc(g_act.sem, 1)
            for n in range(SN):
                dve.wait_ge(f_down.sem, f_down.at(0, n + 1))
                nc.vector.scalar_tensor_tensor(out=fh[:, n], in0=bank[6 + n][:], scalar=small[:, 14 + n:15 + n], in1=pre[:, n],
                                               op0=ALU.mult, op1=ALU.add).then_inc(s_last, 1)

        @block.gpsimd
        def _(pool):
            for g in (turned_p, prod_p, idx_set, seen_set, mask_a1, masks, x_bias, sa_sub, out_add):
                pool.sem_inc(g.sem, g.prime)
            def gather(dst, table, idx, top):
                return pool.indirect_dma_start(out=dst, out_offset=None, in_=table, in_offset=bass.IndirectOffsetOnAxis(ap=idx, axis=0),
                                               bounds_check=top, oob_is_err=False)

            pool.wait_ge(s_pre, 2)
            for t in range(PAIRS):
                gather(rope[:, t], a["rope"], pos_idx[:, t:t + 1], NBLK * BLOCK - 1).then_inc(s_rope, 16)
            pool.wait_ge(s_rope, 16 * PAIRS)

            def turn_sine(t, u):
                pool.wait_ge(scaled.sem, scaled.at(t, 1))
                pool.wait_ge(roped.sem, roped.at(t, 2 - 4))
                nc.gpsimd.tensor_tensor(turned[:, u, :, 0, :], qk[:, u, :, 1, :], rope[:, bass.ds(t, 1), 32:64].to_broadcast([P, QK, 32]),
                                        ALU.mult).then_inc(turned_p.sem, 1)

            def mark_writers(g, par):
                pool.wait_ge(same_p.sem, same_p.at(g, 1))
                pool.wait_ge(src_v.sem, src_v.at(g, 1 - 2))
                nc.gpsimd.tensor_tensor(prod[par][0:GP], tok_all[0:GP].rearrange("p (w o) -> p o w", o=BLOCK),
                                        same[0:GP, par].unsqueeze(1).to_broadcast([GP, BLOCK, WRITERS]), ALU.mult).then_inc(prod_p.sem, 1)

            turn_sine(0, 0)
            turn_sine(1, 1)
            mark_writers(0, 0)
            with pool.Fori(1, 4) as i:
                for u in range(2):
                    turn_sine(i * 2 + u, u)
                    mark_writers(i * 2 + u - 1, 1 - u)
            turn_sine(GROUPS, 0)
            mark_writers(GROUPS - 1, 1)
            for u, parts in ((1, (q_blk.rearrange("p a b c d n -> p (a b c d n)"), qa_blk.rearrange("p a b c n -> p (a b c n)"))),
                             (0, (pc.rearrange("p a n -> p (a n)"), va.rearrange("p a b n -> p (a b n)")))):
                turn_sine(GROUPS + 2 - u, u)
                for part in parts:
                    nc.gpsimd.memset(part, 0.0).then_inc(s_zero, 1)
            turn_sine(GROUPS + 3, 1)
            turn_sine(PAIRS - 4, 0)
            turn_sine(PAIRS - 3, 1)

            def set_indices(i, j):
                pool.wait_ge(pv_done.sem, pv_done.at(i, 8 * (j + 1) - STEPS))
                nc.gpsimd.tensor_copy(turn_idx[:, j, 0:4].rearrange("p (b h) -> p h b", h=2), cache_idx[:, :, bass.ds(i * BT + 2 * j, 2)]).then_inc(idx_set.sem, 1)
                nc.gpsimd.tensor_copy(turn_idx[:, j, 4:8].rearrange("p (b h) -> p h b", h=2), over_idx[:, :, bass.ds(i * BT + 2 * j, 2)]).then_inc(idx_set.sem, 1)
                nc.gpsimd.tensor_copy(turn_idx[:, j, 8:9], fresh_idx[:, bass.ds(i * PT + j, 1)]).then_inc(idx_set.sem, 1)
                pool.wait_ge(idx_set.sem, idx_set.at(i, 3 * j + 3))
                pool.sem_inc(s_passed, 1)

            def gather_cached(i, j):
                set_indices(i, j)
                for n in range(4):
                    gather(kv[:, j, n], a["cache"], turn_idx[:, j, n:n + 1], POOL_BLOCKS * BLOCK - 1).then_inc(cached[j], 16)

            def gather_fresh(i, j):
                pool.wait_ge(cached[j], i * 64 + 64)
                pool.sem_inc(s_passed, 1)
                for n in (4, 0, 1, 2, 3):
                    col = 8 if n == 4 else 4 + n
                    gather(kv[:, j, n], kv_new, turn_idx[:, j, col:col + 1], NT - 1).then_inc(fresh[j], 16)

            def make_mask(i, n):
                b = n % 2
                pool.wait_ge(masked.sem, masked.at(i, 4 * (n - 1)))
                pool.sem_inc(s_passed, 1)
                nc.gpsimd.tensor_scalar(mk[:, b], place_c[:, b], turn_seen[:, n:n + 1], NEG, ALU.is_lt, ALU.mult).then_inc(mask_a1.sem, 1)
                pool.wait_ge(mask_a1.sem, mask_a1.at(i, n + 1))
                nc.gpsimd.tensor_tensor(mk[:, b], mk[:, b], mask_c[:, b], ALU.add).then_inc(masks.sem, 1)

            def first_masks(i):
                nc.gpsimd.tensor_copy(turn_seen, first_seen[:, bass.ds(i * BT, BT)]).then_inc(seen_set.sem, 1)
                pool.wait_ge(seen_set.sem, seen_set.at(i, 1))
                make_mask(i, 0)
                make_mask(i, 1)

            def turn(i, more):
                for j in range(PT):
                    pool.wait_ge(x_loaded[j], i * 16 + 16)
                    nc.gpsimd.tensor_tensor(xr[:, j], xr[:, j], bo, ALU.add).then_inc(x_bias.sem, 1)
                make_mask(i, 2)
                make_mask(i, 3)
                if more:
                    gather_cached(i + 1, 0)
                    gather_cached(i + 1, 1)
                    gather_fresh(i + 1, 0)
                    gather_fresh(i + 1, 1)
                    first_masks(i + 1)
                for j in range(PT):
                    pool.wait_ge(sa_max.sem, sa_max.at(i, j + 1))
                    scores = pa[:, j].rearrange("p h b t -> p (h b) t")
                    nc.gpsimd.tensor_tensor(scores, scores, top_a[:, j].unsqueeze(2).to_broadcast([P, 2 * HP, T]), ALU.subtract).then_inc(sa_sub.sem, 1)
                for j in range(PT):
                    pool.wait_ge(hid.sem, hid.at(i, j + 1))
                    nc.gpsimd.tensor_tensor(xr[:, j], xh[:, j, 0:D], xh[:, j, D:], ALU.add).then_inc(out_add.sem, 1)

            turn_sine(PAIRS - 2, 0)
            pool.wait_ge(s_idx, 4)
            gather_cached(0, 0)
            turn_sine(PAIRS - 1, 1)
            gather_cached(0, 1)
            for u in range(2):
                pool.wait_ge(kv_stored[u], 16 * (PAIRS // 2 + 1))
            for j in range(PT):
                gather_fresh(0, j)
            first_masks(0)
            pool.wait_ge(s_weights, 16 * 11)
            for u in range(2):
                pool.wait_ge(q_stored[u], 16 * (PAIRS // 2 + 1))
            with pool.Fori(0, TURNS - 1) as i:
                turn(i, True)
            turn(TURNS - 1, False)

            pool.wait_ge(s_pick, PICKS + 2)
            for n in range(SN):
                gather(sel[:, n], xh_rows, picked[:, 1, n:n + 1], NT - 1).then_inc(s_sel[n], 16)
            for n in range(SN):
                gather(frope[:, n], a["f_rope"], picked[:, 0, n:n + 1], T - 1).then_inc(s_frope, 16)
            for n in range(SN):
                pool.wait_ge(s_last, 2 * SN + n + 1)
                pool.indirect_dma_start(out=out.rearrange("q p n -> (q p) n"), out_offset=bass.IndirectOffsetOnAxis(ap=picked[:, 1, n:n + 1], axis=0),
                                        in_=fh[:, n], in_offset=None, bounds_check=NT - 1, oob_is_err=False).then_inc(s_fout, 16)
            pool.wait_ge(s_fout, 32)


def build(nc, ins, out_shape):
    args = {}
    for name, (shape, dt) in ins.items():
        args[name] = nc.dram_tensor(f"in_{name}", shape, dt, kind="ExternalInput").ap()
    out = nc.dram_tensor("out_0", out_shape, F32, kind="ExternalOutput").ap()
    block_kernel(nc, args, out)


def constants():
    f = np.float32
    t = np.arange(T)
    c = np.arange(WINDOW)
    seen = np.where(c[None, :] > t[:, None], 0.0, NEG)
    new = np.where(t[None, :] <= t[:, None], 0.0, NEG)
    far = np.full(T, 1.0e9)
    mask_c = np.stack([np.concatenate([seen, new], 1), np.concatenate([new, seen], 1)], 1)
    place = np.stack([np.concatenate([c, far]), np.concatenate([far, c])], 0)
    causal = np.where(np.arange(P)[None, :] <= np.arange(P)[:, None], 0.0, NEG)
    p = np.arange(P)
    seq = np.zeros((P, 1 + PAIRS))
    seq[:, 0] = p % T
    seq[:, 1] = p * P
    seq[:, 2] = p * P + T
    consts = np.concatenate([
        np.eye(P), np.tile(mask_c, (2, 1, 1)).reshape(P, -1), np.broadcast_to(place.reshape(1, -1), (P, 2 * SPAN)),
        np.tile(new, (2, 1)), np.concatenate([np.zeros((P, P)), causal], 1), np.full((P, 1), 1e-6), np.ones((P, 1)), seq], 1).astype(f)
    b = np.arange(B)[:, None]
    consts32 = np.concatenate([
        np.broadcast_to(np.arange(NBLK), (B, NBLK)), np.broadcast_to(np.arange(WSLOTS), (B, WSLOTS)),
        np.broadcast_to(np.arange(NSLOTS * BLOCK), (B, NSLOTS * BLOCK)), b * T + 1,
        np.broadcast_to(np.arange(BLOCK), (B, BLOCK))], 1).astype(f)
    half = CHD // 2
    inv = (f(1.0) / np.power(f(10000.0), np.arange(half, dtype=f) / f(half))).astype(f)
    ang = np.arange(NBLK * BLOCK, dtype=f)[:, None] * inv
    rope = np.concatenate([np.cos(ang), -np.sin(ang), np.sin(ang)], 1).astype(f)
    inv = (f(1.0) / np.power(f(10000.0), np.arange(0, FHD, 2, dtype=f) / f(FHD))).astype(f)
    ang = np.arange(T, dtype=f)[:, None] * inv
    f_rope = np.concatenate([np.cos(ang), np.cos(ang), -np.sin(ang), np.sin(ang)], 1).astype(f)
    return {"consts": consts, "consts32": consts32, "rope": rope, "f_rope": f_rope}


def laid_out(v):
    c = np.ascontiguousarray

    def parts(w):
        return c(w.reshape(w.shape[0] // P, P, w.shape[1]).transpose(1, 0, 2))

    def chunks(w):
        k = w.reshape(w.shape[0] // 512, KD, P, w.shape[1] // 512, 512)
        return c(k.transpose(3, 0, 2, 1, 4).reshape(-1, P, KD, 512))

    x = v["x"].reshape(PAIRS, P, KD, P)
    lens, tables = v["itok_B_37_3939"], v["itok_Bx257_0_4111"]
    d = {
        "x_t": c(x.transpose(0, 3, 2, 1)),
        "x_rows": v["x"].reshape(PAIRS, P, D),
        "lens_rep": c(np.concatenate([np.repeat(lens.reshape(PAIRS, 2).T, T, axis=0), np.broadcast_to(lens, (P, B))], 1)),
        "lens": lens.reshape(B, 1),
        "tables": tables,
        "experts": v["itok_B_0_15"].reshape(1, B),
        "qk_scale": c(np.broadcast_to(np.concatenate([np.tile(v["L0_cond_q_norm_scale"], CH), np.tile(v["L0_cond_k_norm_scale"], CG)]), (P, QK * CHD))),
        "w_qkv": parts(np.concatenate([v["L0_cond_Wq"].reshape(2, 2, 2, CHD, D).transpose(0, 2, 1, 3, 4).reshape(CH * CHD, D), v["L0_cond_Wk"], v["L0_cond_Wv"]], 0).T),
        "cache": np.concatenate([v["L0_cond_k_blocks"].transpose(0, 2, 1, 3).reshape(POOL_BLOCKS * BLOCK, CG * CHD),
                                 v["L0_cond_v_blocks"].transpose(0, 2, 1, 3).reshape(POOL_BLOCKS * BLOCK, CG * CHD)], 1),
        "w_c_o": c(v["L0_cond_Wo"].T.reshape(2, 2, 2, CHD, D).transpose(1, 3, 0, 2, 4).reshape(P, KD, D)),
        "w_a_q": parts(v["L0_attn_Wq"].T), "w_a_k": parts(v["L0_attn_Wk"].T), "w_a_v": parts(v["L0_attn_Wv"].T),
        "w_a_o": c(v["L0_attn_Wo"].T.reshape(2, 4, 2, AHD, D).transpose(1, 3, 0, 2, 4).reshape(P, KD, D)),
        "bq": c(v["L0_attn_bq"].reshape(KD, P).T), "bk": c(v["L0_attn_bk"].reshape(KD, P).T),
        "bv": v["L0_attn_bv"], "bo": v["L0_attn_bo"], "router": v["L0_ffn_w_router"],
        "w_exp": c(v["L0_cond2_W"].reshape(16, KD, P, D).transpose(0, 2, 1, 3)),
        "b_exp": v["L0_cond2_b"],
        "f_qkv": chunks(np.concatenate([v["L0_ffn_wq"], v["L0_ffn_wk"], v["L0_ffn_wv"]], 1)),
        "f_bias": np.concatenate([v["L0_ffn_bq"], v["L0_ffn_bk"], v["L0_ffn_bv"]]),
        "f_wo": chunks(v["L0_ffn_wo"]), "f_gate": chunks(v["L0_ffn_w_gate"]), "f_up": chunks(v["L0_ffn_w_up"]),
        "f_down": chunks(v["L0_ffn_w_down"]), "ln1": v["L0_ffn_ln1_w"], "ln2": v["L0_ffn_ln2_w"],
    }
    d.update(constants())
    return {k: c(x) for k, x in d.items()}


def kernel(**inputs):
    import numpy as _np
    import concourse.bacc as _bacc
    from concourse import mybir as _mybir
    from concourse.bass_utils import run_bass_kernel_spmd as _run

    nc = _bacc.Bacc("TRN2", target_bir_lowering=False, num_devices=1)
    arrays = laid_out({k: _np.asarray(x) for k, x in inputs.items()})
    build(nc, {k: (x.shape, _mybir.dt.from_np(x.dtype)) for k, x in arrays.items()}, (PAIRS, P, D))
    r = _run(nc, [{f"in_{k}": x for k, x in arrays.items()}], core_ids=[0])
    return r.results[0]["out_0"].reshape(B, T, D)
```

```python
from contextlib import ExitStack

import numpy as np

import concourse.bass as bass
from concourse import mybir

ALU = mybir.AluOpType
ACT = mybir.ActivationFunctionType
AX = mybir.AxisListType
F32 = mybir.dt.float32
I32 = mybir.dt.int32
U32 = mybir.dt.uint32

P = 128
B, T, D = 32, 64, 512
NT = B * T
PAIRS = B // 2
KD = D // P
CH, CG, CHD = 8, 4, 64
BLOCK, WINDOW, NBLK = 16, 256, 257
POOL_BLOCKS = 16 * NBLK
ROW = 2 * CG * CHD
WSLOTS = WINDOW // BLOCK + T // BLOCK + 1
NSLOTS = T // BLOCK + 1
WPOS = WSLOTS * BLOCK
SPAN = WINDOW + T
QK = CH + CG
SKIP = 1.0e6
GROUPS = 6
GP = B * WSLOTS // GROUPS
WRITERS = B * NSLOTS
NEG = -1.0e30
AH, AHD = 16, 32
HP = AH // 2
PT = 2
TURNS = PAIRS // PT
BT = 2 * PT
TT = PT * P
STEPS = BT * CG
KEEP = 8
S = B * KEEP
SN = S // P
FH, FKV, FHD = 16, 8, 128
FI = 2048
FQKV = (FH + 2 * FKV) * FHD
NQKV = FQKV // 512
NIN = FI // P
WPARTS = 10
COLS = 53200
RING = 6


class Signal:

    def __init__(self, sem, per_turn, prime=0):
        self.sem, self.per_turn, self.prime = sem, per_turn, prime

    def at(self, turn, n):
        return turn * self.per_turn + (self.prime + n)


class Arena:

    def __init__(self, tensor):
        self.tensor, self.next = tensor, 0

    def take(self, *shape):
        n = int(np.prod(shape))
        assert self.next + n <= self.tensor.shape[1], (self.next, n)
        ap = self.tensor[:, self.next:self.next + n]
        self.next += n
        if len(shape) > 1:
            names = "abcdef"[:len(shape)]
            kept = {c: k for c, k in zip(names[1:], shape[1:])}
            ap = ap.rearrange(f"p ({' '.join(names)}) -> p {' '.join(names)}", **kept)
        return ap


def block_kernel(nc, a, out):
    ctx = ExitStack()
    with ctx:
        def sem(name):
            return ctx.enter_context(nc.semaphore(name))

        def sig(name, per_turn, prime=4):
            return Signal(sem(name), per_turn, prime)

        def dram(name, shape, dt=F32):
            return nc.dram_tensor(name, shape, dt).ap()

        kv_new = dram("kv_new", (NT, ROW))
        q_turned = dram("q_turned", (PAIRS, P, 512))
        xh_rows = dram("xh_rows", (NT, 2 * D))
        win_d = dram("win_d", (B, WSLOTS))
        tok_d = dram("tok_d", (B, NSLOTS * BLOCK))
        src_d = dram("src_d", (B * WSLOTS, BLOCK))

        ar = Arena(ctx.enter_context(nc.sbuf_tensor("arena", [P, COLS], F32)))
        ident = ar.take(P)
        mask_c = ar.take(2, SPAN)
        place_c = ar.take(2, SPAN)
        mask_a = ar.take(T)
        mask_f = ar.take(2, P)
        eps = ar.take(1)
        one = ar.take(1)
        seq_base = ar.take(1)
        kept_row = ar.take(SN)
        CONST = ar.next
        first_seen = ar.take(B)
        score = ar.take(PAIRS)
        score_t = ar.take(PT)
        cache_idx = ar.take(2, B).bitcast(I32)
        over_idx = ar.take(2, B).bitcast(I32)
        fresh_idx = ar.take(PAIRS).bitcast(I32)
        turn_idx = ar.take(PT, 9).bitcast(I32)
        turn_seen = ar.take(BT)
        expert_id = ar.take(B).bitcast(I32)
        router = ar.take(D)
        top8 = ar.take(2, KEEP)
        at8 = ar.take(2, KEEP).bitcast(U32)
        neg8 = ar.take(2, KEEP)
        sorted8 = ar.take(2, KEEP)
        spread = ar.take(PAIRS, 2 * KEEP)
        picked = ar.take(2, SN).bitcast(I32)
        bv = ar.take(D)
        bo = ar.take(D)
        bq = ar.take(KD)
        bk = ar.take(KD)
        routed_base = ar.next
        at = ar.next
        w_main = ar.take(WPARTS, 2 * D)
        ar.next = at
        w_c_t = ar.take(KD, D)
        w_a_q = ar.take(KD, D)
        w_a_k = ar.take(KD, D)
        w_a_v = ar.take(KD, D)
        w_a_o = ar.take(KD, D)
        base = ar.next
        kv = ar.take(PT, 5, ROW)
        at = ar.next
        k_t = ar.take(PT, 2, 2 * SPAN)
        ar.next = at
        pa_t = ar.take(PT, HP, P)
        ar.next = at
        st = ar.take(PT, 2, 512)
        ar.next = at + PT * 4 * SPAN
        at = ar.next
        o_t = ar.take(KD, TT)
        ar.next = at
        oa_t = ar.take(PT, KD, P)
        x_t = ar.take(PT, KD, P)
        ka_t = ar.take(KD, TT)
        zeroed = ar.next
        q_blk = ar.take(PT, 2, 2, 2, P)
        qa_blk = ar.take(KD, BT, 4, T)
        pc = ar.take(4, 3 * P)
        va = ar.take(PT, 2, D)
        first = ar.next
        pc_t = ar.take(4, 3 * P)
        mk = ar.take(2, SPAN)
        top_c = ar.take(4)
        neg_c = ar.take(4)
        sum_c = ar.take(4)
        rec_c = ar.take(4)
        pa = ar.take(PT, HP, 2, T)
        top_a = ar.take(PT, 2 * HP)
        sum_a = ar.take(PT, 2 * HP)
        rec_a = ar.take(PT, 2 * HP)
        oa = ar.take(PT, 2, 2, 4, AHD)
        xr = ar.take(PT, D)
        xh = ar.take(PT, 2 * D)
        junk = ar.take(D)
        b_exp = ar.take(PT, D)
        w_exp = ar.take(BT, KD, D)
        ar.next = first
        w_qkv = ar.take(KD, 1024)
        x_in = ar.take(2, KD, P)
        kvn = ar.take(2, ROW)
        rope = ar.take(PAIRS, 96)
        scale1 = ar.take(QK, CHD)
        sq = ar.take(QK, CHD)
        ssum = ar.take(2, QK)
        root = ar.take(2, QK)
        inv = ar.take(2, QK)
        qk = ar.take(2, QK, 2, 32)
        turned = ar.take(2, QK, 2, 32)
        qk_cos = ar.take(2, QK, 2, 32)
        qr = ar.take(2, 512)
        q_out = ar.take(2, 512)
        prod = [ar.take(BLOCK, WRITERS)]
        ar.next = base
        pos_idx = ar.take(PAIRS).bitcast(I32)
        len_all = ar.take(PAIRS + B).bitcast(I32)
        posf = ar.take(PAIRS)
        blocks_i = ar.take(NBLK).bitcast(I32)
        blocks = ar.take(NBLK)
        lens_i = ar.take(8).bitcast(I32)
        lens = ar.take(8)
        k32 = ar.take(NBLK + WSLOTS + NSLOTS * BLOCK + 1 + BLOCK)
        slot_no = ar.take(WSLOTS)
        hit = ar.take(4, NBLK)
        win = ar.take(WSLOTS)
        tok = ar.take(3, NSLOTS * BLOCK)
        tok_all = ar.take(WRITERS * BLOCK)
        blk_w = ar.take(WRITERS)
        blk_r = ar.take(GROUPS)
        same = ar.take(2, WRITERS)
        prod.append(ar.take(BLOCK, WRITERS))
        src = ar.take(GROUPS, BLOCK)
        al = ar.take(2, 2, WPOS)
        idx_f = ar.take(4, SPAN)
        assert ar.next <= zeroed
        ar.next = routed_base
        ring = ar.take(RING, KD, D)
        fq = ar.take(SN, FQKV)
        fq_t = ar.take(FH, S)
        fk_t = ar.take(FKV, S)
        fbias = ar.take(FQKV)
        fo_t = ar.take(FH, S)
        sel = ar.take(SN, 2 * D)
        fh = ar.take(SN, D)
        fh_t = ar.take(KD, S)
        x1 = ar.take(SN, D)
        frope = ar.take(SN, 256)
        fcos = ar.take(2, D)
        fsin = ar.take(2, D)
        fp = ar.take(4, P + S)
        fp_t = ar.take(2, P + S)
        f_top, f_neg, f_sum, f_rec = (ar.take(4, SN) for _ in range(4))
        ln1 = ar.take(D)
        ln2 = ar.take(D)
        fjunk = ar.take(D)
        small = ar.take(64)
        pre = ar.take(SN, D)
        after = ar.next
        ar.next = routed_base + RING * KD * D
        act_t = ar.take(NIN, S)
        e_g = ar.take(2, S)
        r_g = ar.take(2, S)
        assert ar.next <= routed_base + RING * KD * D + SN * FQKV
        ar.next = after

        bank = [ctx.enter_context(nc.psum_tensor(f"bank{i}", [P, 512], F32)) for i in range(8)]

        s_early = sem("small_inputs_loaded")
        s_weights = sem("loop_weights_loaded")
        s_lens = sem("lengths_loaded")
        s_consts = sem("constants_loaded")
        s_wqkv = [sem(f"wqkv_loaded{k}") for k in range(KD)]
        s_rope = sem("rope_gathered")
        s_win_out = sem("window_blocks_stored")
        s_win_in = sem("window_blocks_back")
        s_src_out = sem("sources_stored")
        s_src_in = sem("sources_back")
        s_pre = sem("vector_setup_step")
        s_zero = sem("zeros_written")
        s_idx_t = sem("index_transposed")
        s_idx = sem("indices_ready")
        s_passed = sem("passed_waits")
        xin_l = [sem(f"x_in_loaded{u}") for u in range(2)]
        proj = sig("projected", 1)
        summed = sig("squares_summed", 1)
        v_copied = sig("new_values_copied", 1)
        rooted = sig("rooted", 1)
        inverted = sig("inverted", 1)
        normed = sig("normed", 2)
        scaled = sig("scaled", 1)
        turned_p = sig("turned_by_pool", 1)
        turned_v = sig("turned_by_vector", 1)
        cosd = sig("cosine_part", 1)
        roped = sig("roped", 2)
        q_tr = sig("q_transposed", 1)
        q_copied = sig("q_copied", 1)
        q_stored = [sem(f"q_stored{u}") for u in range(2)]
        kv_stored = [sem(f"kv_stored{u}") for u in range(2)]
        same_p = sig("blocks_compared", 1)
        prod_p = sig("writers_marked", 1)
        src_v = sig("last_writer_found", 1)
        q_loaded = [sem(f"q_loaded{j}") for j in range(PT)]
        cached = [sem(f"cached_rows{j}") for j in range(PT)]
        fresh = [sem(f"fresh_rows{j}") for j in range(PT)]
        x_loaded = [sem(f"x_rows{j}") for j in range(PT)]
        we_loaded = [sem(f"expert{n}") for n in range(BT)]
        be_loaded = [sem(f"expert_bias{j}") for j in range(PT)]
        xh_stored = [sem(f"xh_stored{j}") for j in range(PT)]
        out_stored = [sem(f"out_stored{j}") for j in range(PT)]
        idx_set = sig("turn_indices", 3 * PT)
        seen_set = sig("turn_first_places", 1)
        mask_a1 = sig("mask_begun", BT)
        masks = sig("mask_made", BT)
        k_tr = sig("keys_transposed", 3 * PT)
        keys_cop = sig("keys_copied", 3 * PT)
        scored = sig("scored", STEPS, STEPS)
        masked = sig("masked", STEPS)
        negated = sig("max_negated", STEPS)
        exped = sig("exped", STEPS)
        recd = sig("sum_inverted", STEPS)
        weighed = sig("probs_divided", STEPS)
        p_tr = sig("probs_transposed", STEPS)
        p_cop = sig("probs_copied", STEPS)
        pv_done = sig("values_weighted", STEPS // 2, STEPS)
        o_cop = sig("outputs_copied", STEPS // 2)
        folded = sem("weights_multiplied")
        folded_act = sem("weights_copied_by_scalar")
        folded_dve = sem("weights_copied_by_vector")
        qa_done = sig("qa_done", 2)
        qa_act = sig("qa_copied_by_scalar", 1)
        qa_dve = sig("qa_copied_by_vector", 1)
        ka_done = sig("ka_done", 2)
        ka_act = sig("ka_copied_by_scalar", 1)
        ka_dve = sig("ka_copied_by_vector", 1)
        st_done = sig("sa_scored_by_key", 2 * PT)
        st_act = sig("sa_scores_copied_by_scalar", PT)
        st_dve = sig("sa_scores_copied_by_vector", PT)
        sa_done = sig("sa_scored", PT)
        sa_mask = sig("sa_masked", 2 * PT)
        sa_max = sig("sa_max", PT)
        sa_sub = sig("sa_max_subtracted", PT)
        sa_exp = sig("sa_exped", PT)
        sa_sum = sig("sa_summed", PT)
        sa_rec = sig("sa_inverted", PT)
        va_done = sig("va_done", PT)
        va_cop = sig("va_copied", PT)
        pa_tr = sig("pa_transposed", PT)
        pa_act = sig("pa_copied_by_scalar", PT)
        pa_dve = sig("pa_copied_by_vector", PT)
        pva = sig("pva_done", PT)
        oa_norm = sig("oa_normed", PT)
        oa_tr = sig("oa_transposed", PT)
        oa_cop = sig("oa_copied", PT)
        z_done = sig("z_done", PT)
        x_bias = sig("x_plus_bias", PT)
        resid = sig("residual_added", PT)
        x_tr = sig("x_transposed", PT)
        x_cop = sig("x_copied", PT)
        c_done = sig("expert_done", PT)
        hid = sig("hidden_made", PT)
        rscore = sig("router_scored", PT)
        sc_cop = sig("scores_kept", 1)
        out_add = sig("out_rows_made", PT)
        s_ln1 = sem("routed_input_norm_loaded")
        s_fin = sem("routed_bias_and_second_norm_loaded")
        s_sct = sem("scores_transposed")
        s_pick = sem("pick_step")
        s_sel = [sem(f"selected_rows{n}") for n in range(SN)]
        s_frope = sem("routed_rope_gathered")
        s_gate = sem("row_gate_step")
        s_last = sem("last_rows_step")
        f_x1 = sig("f_residual_added", 0, 0)
        s_rms = sem("routed_square_root")
        s_esc = sem("routed_gate_exp")
        r_landed = [sem(f"ring_landed{n}") for n in range(RING)]
        fh_ready = sig("fh_ready", 0, 0)
        fh_tr = sig("fh_transposed", 0, 0)
        fh_cop = sig("fh_copied", 0, 0)
        fq_mm = sig("fq_done", 0, 0)
        fq_bias = sig("fq_biased", 0, 0)
        f_sin = sig("f_sin_part", 0, 0)
        f_cos = sig("f_cos_part", 0, 0)
        f_rope = sig("f_roped", 0, 0)
        fq_tr = sig("fq_transposed", 0, 0)
        fq_cop = sig("fq_copied", 0, 0)
        fs = sig("f_scored", 0, 0)
        fmask = sig("f_masked", 0, 0)
        fneg = sig("f_negated", 0, 0)
        fexp = sig("f_exped", 0, 0)
        frec = sig("f_inverted", 0, 0)
        fnorm = sig("f_normed", 0, 0)
        fp_tr = sig("f_probs_transposed", 0, 0)
        fp_cop = sig("f_probs_copied", 0, 0)
        fpv = sig("f_values_weighted", 0, 0)
        fo_cop = sig("f_outputs_copied", 0, 0)
        fwo = sig("f_projected", 0, 0)
        g_done = sig("gate_up_done", 0, 0)
        g_exp = sig("gate_exped", 0, 0)
        g_one = sig("gate_step", 0, 0)
        g_act = sig("gated_made", 0, 0)
        f_down = sig("down_done", 0, 0)
        s_fout = sem("routed_rows_stored")

        PRE_WIN = 12 + WSLOTS + 4
        PRE_ALL = PRE_WIN + 1
        PRE_IDX = PRE_ALL + 14
        LEAD = 4
        PICKS = 7

        block = ctx.enter_context(nc.Block())

        @block.sync
        def _(sp):
            for u in range(PT):
                sp.sem_inc(xh_stored[u], 16)
                sp.sem_inc(out_stored[u], 16)
                sp.sem_inc(q_stored[u], 16)
                sp.sem_inc(kv_stored[u], 16)
            sp.dma_start(len_all, a["lens_rep"]).then_inc(s_lens, 16)
            sp.dma_start(ar.tensor[:, CONST - 1 - SN:CONST], a["consts"][:, CONST - 1 - SN:CONST]).then_inc(s_lens, 16)
            for dst, source in ((blocks_i[0:B, 0:NBLK], a["tables"]), (lens_i[0:B, 0:1], a["lens"]), (k32[0:B, :], a["consts32"])):
                sp.dma_start(dst, source).then_inc(s_early, 16)
            sp.dma_start(ar.tensor[:, 0:CONST - 1 - SN], a["consts"][:, 0:CONST - 1 - SN]).then_inc(s_consts, 16)
            sp.dma_start(scale1, a["qk_scale"].rearrange("p (h d) -> p h d", h=QK)).then_inc(s_consts, 16)
            def store_kv(t, u):
                sp.wait_ge(roped.sem, roped.at(t, 2))
                sp.dma_start(kv_new.rearrange("(t p) n -> t p n", p=P)[bass.ds(t, 1)].rearrange("a p n -> p (a n)"), kvn[:, u]).then_inc(kv_stored[u], 16)

            def store_q(t, u):
                sp.wait_ge(q_copied.sem, q_copied.at(t, 1))
                sp.dma_start(q_turned[bass.ds(t, 1)].rearrange("a p n -> p (a n)"), q_out[:, u]).then_inc(q_stored[u], 16)

            sp.wait_ge(s_pre, PRE_WIN)
            sp.dma_start(win_d, win[0:B, :]).then_inc(s_win_out, 16)
            sp.dma_start(tok_d, tok[0:B, 2, :]).then_inc(s_win_out, 16)
            sp.wait_ge(s_win_out, 32)
            with nc.allow_non_contiguous_dma(reason="a few block numbers"):
                sp.dma_start(blk_r[0:GP, :], win_d.rearrange("b s -> (b s)").rearrange("(g p) -> p g", p=GP)).then_inc(s_win_in, 16)
                sp.dma_start(blk_w[0:GP, :].rearrange("p (b s) -> p b s", s=NSLOTS),
                             win_d[:, WSLOTS - NSLOTS:WSLOTS].partition_broadcast(GP)).then_inc(s_win_in, 16)
            sp.dma_start(tok_all[0:GP, :], tok_d.rearrange("b s -> (b s)").partition_broadcast(GP)).then_inc(s_win_in, 16)
            for t in range(2):
                store_kv(t, t)

            def two_tiles(i):
                for u in range(2):
                    store_kv(i * 2 + u, u)
                    store_q(i * 2 + u - 2, u)

            with sp.Fori(1, 5) as i:
                two_tiles(i)
            sp.wait_ge(src_v.sem, src_v.at(GROUPS, 0))
            sp.dma_start(src_d.rearrange("(g p) o -> p g o", p=GP), src[0:GP]).then_inc(s_src_out, 16)
            sp.wait_ge(s_src_out, 16)
            sp.dma_start(al[0:B, 0, 1, :], src_d.rearrange("(b s) o -> b (s o)", b=B)).then_inc(s_src_in, 16)
            with sp.Fori(5, 7) as i:
                two_tiles(i)
            for t in (PAIRS - 2, PAIRS - 1):
                store_kv(t, t % 2)
                store_q(t - 2, t % 2)
            for t in (PAIRS - 2, PAIRS - 1):
                store_q(t, t % 2)
            for u in range(2):
                sp.wait_ge(q_stored[u], 16 * (PAIRS // 2 + 1))
            sp.wait_ge(s_weights, 16 * (WPARTS + 6))
            sp.wait_ge(s_zero, 4)

            def load_queries(i):
                for j in range(PT):
                    sp.wait_ge(scored.sem, scored.at(i, 8 * (j + 1) - STEPS))
                    source = q_turned[bass.ds(i * PT + j, 1)].rearrange("a p (c n) -> p (a c) n", c=4)
                    for g2 in range(2):
                        rows = slice(64 * g2, 64 * g2 + 64)
                        sp.dma_start(q_blk[rows, j, :, :, g2, :].rearrange("p b g n -> p (b g) n"), source[rows]).then_inc(q_loaded[j], 16)

            def load_turn(i):
                for j in range(PT):
                    sp.wait_ge(out_stored[j], i * 16 + 16)
                    sp.dma_start(xr[:, j], a["x_rows"][bass.ds(i * PT + j, 1)].rearrange("a p n -> p (a n)")).then_inc(x_loaded[j], 16)
                    sp.wait_ge(c_done.sem, c_done.at(i, j + 1 - PT))
                    sp.wait_ge(hid.sem, hid.at(i, j + 1 - PT))
                    for b in range(2):
                        n = 2 * j + b
                        e = sp.value_load(expert_id[0:1, bass.ds(i * BT + n, 1)], min_val=0, max_val=15)
                        sp.dma_start(w_exp[:, n], a["w_exp"][bass.ds(e, 1)].rearrange("e p k n -> p (e k) n")).then_inc(we_loaded[n], 16)
                        sp.dma_start(b_exp[64 * b:64 * b + 64, j, :], a["b_exp"][bass.ds(e, 1), :].rearrange("e n -> (e n)").partition_broadcast(64)).then_inc(be_loaded[j], 16)

            def store_turn(i):
                for j in range(PT):
                    sp.wait_ge(hid.sem, hid.at(i, j + 1))
                    sp.dma_start(xh_rows[bass.ds((i * PT + j) * P, P), :], xh[:, j]).then_inc(xh_stored[j], 16)
                    sp.wait_ge(out_add.sem, out_add.at(i, j + 1))
                    sp.dma_start(out[bass.ds(i * PT + j, 1)].rearrange("a p n -> p (a n)"), xr[:, j]).then_inc(out_stored[j], 16)

            load_queries(0)
            with sp.Fori(0, TURNS - 1) as i:
                load_turn(i)
                load_queries(i + 1)
                store_turn(i)
            load_turn(TURNS - 1)
            chunks = [a["f_qkv"][c] for c in range(NQKV)] + [a["f_wo"][c] for c in range(4)]
            for c in range(4):
                chunks += [a["f_gate"][c], a["f_up"][c]]
            chunks += [a["f_down"][c] for c in range(4)]
            for slot, left in ((0, scored), (5, pv_done), (1, qa_done), (2, ka_done), (3, va_done)):
                sp.wait_ge(left.sem, left.at(TURNS, 0))
                sp.dma_start(ring[:, slot], chunks[slot]).then_inc(r_landed[slot], 16)
            store_turn(TURNS - 1)
            sp.wait_ge(rscore.sem, rscore.at(TURNS, 0))
            sp.wait_ge(out_add.sem, out_add.at(TURNS, 0))
            sp.dma_start(ln1, a["ln1"].partition_broadcast(P)).then_inc(s_ln1, 16)
            for n in range(SN):
                sp.wait_ge(s_sel[n], 16)
            sp.dma_start(fbias, a["f_bias"].partition_broadcast(P)).then_inc(s_fin, 16)
            sp.dma_start(ln2, a["ln2"].partition_broadcast(P)).then_inc(s_fin, 16)
            sp.wait_ge(z_done.sem, z_done.at(TURNS, 0))
            sp.dma_start(ring[:, 4], chunks[4]).then_inc(r_landed[4], 16)
            for n, source in enumerate(chunks[RING:]):
                if n < NQKV:
                    sp.wait_ge(fq_mm.sem, 2 * (n + 1))
                elif n < NQKV + 4:
                    sp.wait_ge(fwo.sem, 1 + n - NQKV + 1)
                else:
                    sp.wait_ge(g_done.sem, 4 * ((n - NQKV - 4) // 2 + 1))
                sp.dma_start(ring[:, n % RING], source).then_inc(r_landed[n % RING], 16)
            for j in range(PT):
                sp.wait_ge(xh_stored[j], 16 * (TURNS + 1))
                sp.wait_ge(out_stored[j], 16 * (TURNS + 1))

        @block.tensor
        def _(pe):
            for g in (proj, q_tr, k_tr, scored, p_tr, pv_done, qa_done, ka_done, st_done, sa_done, va_done, pa_tr, pva,
                      oa_tr, z_done, x_tr, c_done):
                pe.sem_inc(g.sem, g.prime)
            def project(t, half, u):
                pe.wait_ge(xin_l[u], half * 16 + 16)
                pe.wait_ge(normed.sem, normed.at(t, 2 - 4))
                pe.wait_ge(v_copied.sem, v_copied.at(t, 1 - 2))
                for k in range(KD):
                    pe.wait_ge(s_wqkv[k], 16)
                    for part in range(2):
                        mm = pe.matmul(bank[2 * u + part][:], x_in[:, u, k, :], w_qkv[:, k, 512 * part:512 * part + 512],
                                       start=(k == 0), stop=(k == KD - 1))
                mm.then_inc(proj.sem, 1)

            def turn_queries(t, u):
                pe.wait_ge(roped.sem, roped.at(t, 2))
                pe.wait_ge(q_copied.sem, q_copied.at(t, 1 - 2))
                for n in range(4):
                    mm = pe.transpose(bank[4 + u][:, n * P:(n + 1) * P], qr[:, u, n * P:(n + 1) * P], ident)
                mm.then_inc(q_tr.sem, 1)

            def two_tiles(i):
                for u in range(2):
                    project(i * 2 + 2 + u, i + 1, u)
                    turn_queries(i * 2 + u, u)

            project(0, 0, 0)
            project(1, 0, 1)
            pe.wait_ge(s_consts, 32)
            with pe.Fori(0, 6) as i:
                two_tiles(i)
            two_tiles(6)

            def fold(n, banks, parts):
                for m in parts:
                    for k in range(KD):
                        mm = pe.matmul(bank[banks[m]][:], w_c_t[:, k, m * P:(m + 1) * P], (w_a_q, w_a_k, w_a_v)[n][:, k, :],
                                       start=(k == 0), stop=(k == KD - 1))
                if parts[-1] == KD - 1:
                    mm.then_inc(folded, 1)

            turn_queries(PAIRS - 2, 0)
            pe.wait_ge(s_weights, 16 * (WPARTS + 6))
            fold(0, (6, 7, 0, 1), (0, 1))
            turn_queries(PAIRS - 1, 1)
            pe.wait_ge(normed.sem, normed.at(PAIRS, 0))
            pe.wait_ge(v_copied.sem, v_copied.at(PAIRS, 0))
            fold(0, (6, 7, 0, 1), (2, 3))
            pe.wait_ge(q_copied.sem, q_copied.at(PAIRS, 0))
            pe.wait_ge(s_pre, PRE_IDX)
            for kind in range(2):
                for half in range(2):
                    n = 2 * kind + half
                    pe.transpose(bank[4][:, n * B:(n + 1) * B], idx_f[0:B, kind, half * P:(half + 1) * P], ident[0:B, 0:B])
            pe.transpose(bank[4][:, 4 * B:5 * B], idx_f[0:B, 2, 0:P], ident[0:B, 0:B]).then_inc(s_idx_t, 1)
            fold(1, (2, 3, 5, 4), (0, 1, 2))
            pe.wait_ge(s_idx, 4)
            fold(1, (2, 3, 5, 4), (3,))
            pe.wait_ge(folded_dve, 1)
            pe.wait_ge(folded_act, 2)
            fold(2, (0, 1, 2, 3), (0, 1, 2, 3))

            pe.wait_ge(s_zero, 4)

            def turn_keys(i, j, parts=(0, 1, 2)):
                pe.wait_ge(cached[j], i * 64 + 64)
                pe.wait_ge(fresh[j], i * 80 + 80)
                for n in parts:
                    use = 3 * j + n
                    pe.wait_ge(keys_cop.sem, keys_cop.at(i, use + 1 - 2))
                    cols = range(4 * n, min(4 * n + 4, 10))
                    for m in cols:
                        g, tile = m // 5, (0, 1, 4, 2, 3)[m % 5]
                        mm = pe.transpose(bank[6 + use % 2][:, (m - cols[0]) * P:(m - cols[0] + 1) * P],
                                          kv[:, j, tile, g * P:(g + 1) * P], ident)
                    mm.then_inc(k_tr.sem, 1)

            def scores(i, s):
                j, b, g = s // 8, s // 4 % 2, s % 4
                pe.wait_ge(q_loaded[j], i * 32 + 32)
                pe.wait_ge(keys_cop.sem, keys_cop.at(i, 3 * (j + 1)))
                pe.wait_ge(masked.sem, masked.at(i, s + 1 - 2))
                pe.matmul(bank[s % 2][:, 0:SPAN], q_blk[:, j, b, g // 2, g % 2, :],
                          k_t[:, j, g // 2, b * SPAN:(b + 1) * SPAN], start=True, stop=True).then_inc(scored.sem, 1)

            def turn_probs(i, s):
                pe.wait_ge(weighed.sem, weighed.at(i, s + 1))
                pe.wait_ge(p_cop.sem, p_cop.at(i, s + 1 - 2))
                for c in range(3):
                    mm = pe.transpose(bank[2 + s % 2][:, c * P:(c + 1) * P], pc[:, s % 4, c * P:(c + 1) * P], ident)
                mm.then_inc(p_tr.sem, 1)

            def weigh_values(i, m):
                j, b = m // 4, m // 2 % 2
                pe.wait_ge(p_cop.sem, p_cop.at(i, 2 * m + 2))
                pe.wait_ge(o_cop.sem, o_cop.at(i, m + 1 - 2))
                for c, tile in ((0, 0), (1, 1), (2, 4)) if b == 0 else ((1, 2), (2, 3), (0, 4)):
                    r = slice(T * b, T * b + T) if tile == 4 else slice(0, P)
                    for g2 in range(2):
                        g = 2 * (m % 2) + g2
                        mm = pe.matmul(bank[4 + m % 2][64 * g2:64 * g2 + 64, 0:P], kv[r, j, tile, CG * CHD + g * CHD:CG * CHD + (g + 1) * CHD],
                                       pc_t[r, (2 * m + g2) % 4, c * P:(c + 1) * P], start=(tile in (0, 2)), stop=(tile == 4))
                mm.then_inc(pv_done.sem, 1)

            def attend(i):
                for s in range(3, STEPS + 4):
                    if LEAD <= s < STEPS:
                        scores(i, s)
                    if s == 3:
                        pe.wait_ge(x_cop.sem, x_cop.at(i, 0))
                    if 3 <= s < STEPS + 3:
                        turn_probs(i, s - 3)
                    if s == 5:
                        pe.wait_ge(hid.sem, hid.at(i, 0))
                    if s == STEPS + 3:
                        pe.wait_ge(o_cop.sem, o_cop.at(i, STEPS // 4))
                        query_columns(i, 0, (0, 1))
                    if s >= 5 and s % 2:
                        weigh_values(i, (s - 5) // 2)
                query_columns(i, 0, (2, 3))

            def query_columns(i, j, parts):
                for m in parts:
                    for k in range(KD):
                        mm = pe.matmul(bank[6 + m // 2][:, (m % 2) * TT + j * P:(m % 2) * TT + (j + 1) * P],
                                       w_a_q[:, k, m * P:(m + 1) * P], o_t[:, k, j * P:(j + 1) * P], start=(k == 0), stop=(k == KD - 1))
                    if j == PT - 1 and m % 2:
                        mm.then_inc(qa_done.sem, 1)

            def columns_of(i, weights, moving, first_bank, done):
                for m in range(KD):
                    for k in range(KD):
                        mm = pe.matmul(bank[first_bank + m // 2][:, (m % 2) * TT:(m % 2 + 1) * TT],
                                       weights[:, k, m * P:(m + 1) * P], moving[:, k, :], start=(k == 0), stop=(k == KD - 1))
                    if m % 2:
                        mm.then_inc(done.sem, 1)

            def self_attention(i):
                pe.wait_ge(o_cop.sem, o_cop.at(i, STEPS // 2))
                query_columns(i, 1, (0, 1, 2, 3))
                columns_of(i, w_a_k, o_t, 4, ka_done)
                pe.wait_ge(masked.sem, masked.at(i, STEPS))
                pe.wait_ge(p_cop.sem, p_cop.at(i, STEPS))
                pe.wait_ge(qa_act.sem, qa_act.at(i, 1))
                pe.wait_ge(qa_dve.sem, qa_dve.at(i, 1))
                pe.wait_ge(ka_act.sem, ka_act.at(i, 1))
                for half in range(2):
                    if half == 1:
                        pe.wait_ge(ka_dve.sem, ka_dve.at(i, 1))
                    for j in range(PT):
                        for k in (2 * half, 2 * half + 1):
                            for b in range(2):
                                n = 2 * j + b
                                mm = pe.matmul(bank[2 + 2 * j + half][64 * b:64 * b + 64, k % 2 * 256:k % 2 * 256 + 256],
                                               ka_t[:, k, n * T:(n + 1) * T], qa_blk[:, k, n].rearrange("p h t -> p (h t)"), start=True, stop=True)
                        mm.then_inc(st_done.sem, 1)
                for j in range(PT):
                    pe.wait_ge(st_act.sem, st_act.at(i, j + 1))
                    pe.wait_ge(st_dve.sem, st_dve.at(i, j + 1))
                    for h in range(HP):
                        mm = pe.transpose(bank[(6, 0)[j] + h // 4][:, (h % 4) * P:(h % 4 + 1) * P],
                                          st[:, j, h // 4, (h % 4) * P:(h % 4 + 1) * P], ident)
                    mm.then_inc(sa_done.sem, 1)
                for j in range(PT):
                    for k in range(KD):
                        mm = pe.matmul(bank[2 + j][:], o_t[:, k, j * P:(j + 1) * P], w_a_v[:, k, :], start=(k == 0), stop=(k == KD - 1))
                    mm.then_inc(va_done.sem, 1)
                for j in range(PT):
                    pe.wait_ge(sa_exp.sem, sa_exp.at(i, j + 1))
                    if j == 1:
                        pe.wait_ge(sa_mask.sem, sa_mask.at(i, 4))
                    for h in range(HP):
                        mm = pe.transpose(bank[(4, 0)[j] + h // 4][:, (h % 4) * P:(h % 4 + 1) * P], pa[:, j, h], ident)
                    mm.then_inc(pa_tr.sem, 1)
                for j in range(PT):
                    pe.wait_ge(pa_act.sem, pa_act.at(i, j + 1))
                    pe.wait_ge(pa_dve.sem, pa_dve.at(i, j + 1))
                    pe.wait_ge(va_cop.sem, va_cop.at(i, 2))
                    pe.wait_ge(sa_mask.sem, sa_mask.at(i, 2))
                    for h in range(HP):
                        mm = pe.matmul(bank[(6, 2)[j] + h // 4][:, (h % 4) * P:(h % 4 + 1) * P], pa_t[:, j, h, :],
                                       va[:, j, :, h * T:(h + 1) * T], start=True, stop=True)
                    mm.then_inc(pva.sem, 1)

            def project_outputs(i, more):
                pe.wait_ge(pa_act.sem, pa_act.at(i, 2))
                pe.wait_ge(pa_dve.sem, pa_dve.at(i, 2))
                for j in range(PT):
                    pe.wait_ge(oa_norm.sem, oa_norm.at(i, j + 1))
                    for c in range(4):
                        mm = pe.transpose(bank[4 + j][:, c * P:(c + 1) * P], oa[:, j, c // 2, c % 2], ident)
                    mm.then_inc(oa_tr.sem, 1)
                    if more:
                        turn_keys(i + 1, j, (0, 1))
                    pe.wait_ge(oa_cop.sem, oa_cop.at(i, j + 1))
                    for k in range(KD):
                        mm = pe.matmul(bank[j][:], oa_t[:, j, k, :], w_a_o[:, k, :], start=(k == 0), stop=(k == KD - 1))
                    mm.then_inc(z_done.sem, 1)
                    if more:
                        turn_keys(i + 1, j, (2,))

            def experts(i, more):
                for j in range(PT):
                    pe.wait_ge(resid.sem, resid.at(i, j + 1))
                    pe.wait_ge(oa_norm.sem, oa_norm.at(i, 2))
                    for k in range(KD):
                        mm = pe.transpose(bank[2 + j][:, k * P:(k + 1) * P], xh[:, j, k * P:(k + 1) * P], ident)
                    mm.then_inc(x_tr.sem, 1)
                    if more:
                        scores(i + 1, j)
                for j in range(PT):
                    if j == 1 and more:
                        scores(i + 1, 2)
                    pe.wait_ge(x_cop.sem, x_cop.at(i, j + 1))
                    for b in range(2):
                        pe.wait_ge(we_loaded[2 * j + b], i * 16 + 16)
                    for k in range(KD):
                        for b in range(2):
                            mm = pe.matmul(bank[4 + j][64 * b:64 * b + 64, :], x_t[:, j, k, b * T:(b + 1) * T],
                                           w_exp[:, 2 * j + b, k, :], start=(k == 0), stop=(k == KD - 1))
                    mm.then_inc(c_done.sem, 1)
                if more:
                    scores(i + 1, 3)

            def turn(i, more):
                attend(i)
                self_attention(i)
                project_outputs(i, more)
                experts(i, more)

            turn_keys(0, 0)
            turn_keys(0, 1)
            pe.wait_ge(folded_act, 3)
            pe.wait_ge(folded_dve, 3)
            for s in range(LEAD):
                scores(0, s)
            with pe.Fori(0, TURNS - 1) as i:
                turn(i, True)
            turn(TURNS - 1, False)

            pe.wait_ge(sc_cop.sem, sc_cop.at(TURNS, 0))
            pe.wait_ge(x_cop.sem, x_cop.at(TURNS, 0))
            pe.transpose(bank[0][0:PAIRS, 0:P], score, ident).then_inc(s_sct, 1)

            def turn_rows(n, use):
                pe.wait_ge(fh_ready.sem, fh_ready.at(0, use + 1))
                if use == 0:
                    pe.wait_ge(hid.sem, hid.at(TURNS, 0))
                if use >= 2:
                    pe.wait_ge(fo_cop.sem, fo_cop.at(0, FH))
                for k in range(KD):
                    mm = pe.transpose(bank[1 + n][:, k * P:(k + 1) * P], fh[:, n, k * P:(k + 1) * P], ident)
                mm.then_inc(fh_tr.sem, 1)

            def turn_heads(c, n):
                use = 2 * c + n
                pe.wait_ge(f_rope.sem, f_rope.at(0, use + 1))
                if use >= 4:
                    pe.wait_ge(fq_cop.sem, fq_cop.at(0, use + 1 - 4))
                else:
                    pe.wait_ge(fh_cop.sem, fh_cop.at(0, 2))
                    pe.wait_ge(s_pick, PICKS)
                for h in range(4):
                    mm = pe.transpose(bank[use % 4][:, h * P:(h + 1) * P], fq[:, n, c * 512 + h * P:c * 512 + (h + 1) * P], ident)
                mm.then_inc(fq_tr.sem, 1)

            pe.wait_ge(s_pick, PICKS)
            pe.wait_ge(x_cop.sem, x_cop.at(TURNS, 0))
            for n in range(SN):
                mm = pe.matmul(bank[3][:, n:n + 1], spread[0:PAIRS].rearrange("p q j -> p (q j)")[:, n * P:(n + 1) * P], one[0:PAIRS],
                               start=True, stop=True)
            mm.then_inc(s_pick, 1)
            for n in range(SN):
                turn_rows(n, n)
            for c in range(NQKV):
                pe.wait_ge(r_landed[c % RING], 16 * (c // RING + 1))
                for n in range(SN):
                    use = 2 * c + n
                    if c == 0:
                        pe.wait_ge(fh_cop.sem, fh_cop.at(0, n + 1))
                    if use >= 4:
                        pe.wait_ge(fq_bias.sem, fq_bias.at(0, use + 1 - 4))
                    for k in range(KD):
                        mm = pe.matmul(bank[4 + use % 4][:], fh_t[:, k, n * P:(n + 1) * P], ring[:, c % RING, k, :], start=(k == 0), stop=(k == KD - 1))
                    mm.then_inc(fq_mm.sem, 1)
                if 2 <= c < 8:
                    for n in range(SN):
                        turn_heads(c - 2, n)
            PARTS = ((0, 0, P), (1, P, P + S))

            def f_scores(h):
                if h < 2:
                    pe.wait_ge(fq_cop.sem, fq_cop.at(0, 12))
                    pe.wait_ge(fq_bias.sem, fq_bias.at(0, 16))
                else:
                    pe.wait_ge(fmask.sem, fmask.at(0, 2 * (h - 1)))
                for n, lo, hi in PARTS:
                    mm = pe.matmul(bank[h % 2][:, lo:hi], fq_t[:, h, n * P:(n + 1) * P], fk_t[:, h // 2, 0:hi - lo], start=True, stop=True)
                mm.then_inc(fs.sem, 1)

            def f_turn(h):
                pe.wait_ge(fnorm.sem, fnorm.at(0, 2 * (h + 1)))
                if h >= 2:
                    pe.wait_ge(fp_cop.sem, fp_cop.at(0, h + 1 - 2))
                for c in range(3):
                    mm = pe.transpose(bank[2 + h % 2][:, c * P:(c + 1) * P], fp[:, h % 4, c * P:(c + 1) * P], ident)
                mm.then_inc(fp_tr.sem, 1)

            def f_weigh(h):
                pe.wait_ge(fp_cop.sem, fp_cop.at(0, h + 1))
                if h >= 4:
                    pe.wait_ge(fo_cop.sem, fo_cop.at(0, h + 1 - 4))
                v0 = (FH + FKV) * FHD + (h // 2) * FHD
                for n, lo, hi in PARTS:
                    for c in range(n + 1):
                        mm = pe.matmul(bank[4 + h % 4][:, n * P:(n + 1) * P], fq[:, c, v0:v0 + FHD], fp_t[:, h % 2, lo + c * P:lo + (c + 1) * P],
                                       start=(c == 0), stop=(c == n))
                mm.then_inc(fpv.sem, 1)

            for t in range(FH + 3):
                if t < FH:
                    f_scores(t)
                if 2 <= t < FH + 2:
                    f_turn(t - 2)
                if t >= 3:
                    f_weigh(t - 3)
            pe.wait_ge(fo_cop.sem, fo_cop.at(0, FH))
            for n in range(SN):
                for h in range(FH):
                    c = NQKV + h // 4
                    pe.wait_ge(r_landed[c % RING], 16 * (c // RING + 1))
                    mm = pe.matmul(bank[6 + n][:], fo_t[:, h, n * P:(n + 1) * P], ring[:, c % RING, h % 4, :], start=(h == 0), stop=(h == FH - 1))
                    if n == SN - 1 and h % 4 == 3 or h == FH - 1 and n == 0:
                        mm.then_inc(fwo.sem, 1)
            def gate_up(f, tiles):
                c = NQKV + 4 + 2 * (f // 4)
                cols = slice(tiles[0] * P, (tiles[-1] + 1) * P)
                for w in range(2):
                    pe.wait_ge(r_landed[(c + w) % RING], 16 * ((c + w) // RING + 1))
                if f >= 4:
                    pe.wait_ge(g_act.sem, g_act.at(0, f + 1 - 4))
                for w in range(2):
                    for k in range(KD):
                        mm = pe.matmul(bank[(3, 4, 5, 0)[f % 4]][:, w * S + cols.start:w * S + cols.stop],
                                       ring[:, (c + w) % RING, k, (f % 4) * P:(f % 4 + 1) * P], fh_t[:, k, cols], start=(k == 0), stop=(k == KD - 1))
                if tiles[-1] == SN - 1:
                    mm.then_inc(g_done.sem, 1)

            turn_rows(0, 2)
            pe.wait_ge(fh_cop.sem, fh_cop.at(0, 3))
            pe.wait_ge(fo_cop.sem, fo_cop.at(0, FH))
            for f in range(2):
                gate_up(f, (0,))
            turn_rows(1, 3)
            pe.wait_ge(fh_cop.sem, fh_cop.at(0, 4))
            for f in range(2):
                gate_up(f, (1,))
            for f in range(2, NIN):
                gate_up(f, (0, 1))
            pe.wait_ge(fh_ready.sem, fh_ready.at(0, 4))
            for n in range(SN):
                for f in range(NIN):
                    c = NQKV + 12 + f // 4
                    pe.wait_ge(r_landed[c % RING], 16 * (c // RING + 1))
                    pe.wait_ge(g_act.sem, g_act.at(0, f + 1))
                    mm = pe.matmul(bank[6 + n][:], act_t[:, f, n * P:(n + 1) * P], ring[:, c % RING, f % 4, :], start=(f == 0), stop=(f == NIN - 1))
                mm.then_inc(f_down.sem, 1)

        @block.scalar
        def _(act):
            for g in (summed, v_copied, rooted, q_copied, keys_cop, exped, p_cop, o_cop, qa_act, ka_act, st_act, sa_exp, pa_act, oa_cop, x_cop):
                act.sem_inc(g.sem, g.prime)

            act.dma_start(x_in[:, 0], a["x_t"][0]).then_inc(xin_l[0], 16)
            for k in range(KD):
                act.dma_start(w_qkv[:, k, :], a["w_qkv"][:, k, :]).then_inc(s_wqkv[k], 16)
            act.dma_start(x_in[:, 1], a["x_t"][1]).then_inc(xin_l[1], 16)

            act.wait_ge(s_consts, 32)

            def squares(t, half, u, load=True):
                act.wait_ge(proj.sem, proj.at(t, 1))
                if load:
                    act.dma_start(x_in[:, u], a["x_t"][bass.ds(t + 2, 1)].rearrange("a p k n -> p (a k) n")).then_inc(xin_l[u], 16)
                act.wait_ge(rooted.sem, rooted.at(t, 1 - 2))
                for h in range(QK):
                    source = bank[2 * u + h // CH][:, h % CH * CHD:(h % CH + 1) * CHD]
                    ins = nc.scalar.activation(sq[:, h], source, ACT.Square, accum_out=ssum[:, u, h:h + 1])
                ins.then_inc(summed.sem, 1)
                act.wait_ge(kv_stored[u], half * 16 + 16)
                nc.scalar.copy(kvn[:, u, CG * CHD:], bank[2 * u + 1][:, CG * CHD:]).then_inc(v_copied.sem, 1)
                act.wait_ge(summed.sem, summed.at(t, 1))
                act.wait_ge(inverted.sem, inverted.at(t, 1 - 2))
                nc.scalar.activation(root[:, u], ssum[:, u], ACT.Sqrt, bias=eps, scale=1.0 / CHD).then_inc(rooted.sem, 1)

            def copy_queries(t, half, u):
                act.wait_ge(q_tr.sem, q_tr.at(t, 1))
                act.wait_ge(q_stored[u], half * 16 + 16)
                nc.scalar.copy(q_out[:, u].rearrange("p (b n t) -> p n b t", b=2, n=4),
                               bank[4 + u][:].rearrange("p (n b t) -> p n b t", n=4, b=2)).then_inc(q_copied.sem, 1)

            def two_tiles(i, load=True):
                for u in range(2):
                    squares(i * 2 + u, i, u, load)
                    copy_queries(i * 2 + u - 2, i - 1, u)

            squares(0, 0, 0)
            squares(1, 0, 1)
            act.wait_ge(s_win_in, 48)
            for dst, source in ((bq, "bq"), (bk, "bk")):
                act.dma_start(dst, a[source]).then_inc(s_weights, 16)
            for dst, source in ((bv, "bv"), (bo, "bo"), (router, "router")):
                act.dma_start(dst, a[source].partition_broadcast(P)).then_inc(s_weights, 16)
            act.dma_start(expert_id[0:1, :], a["experts"]).then_inc(s_weights, 16)
            with act.Fori(1, 1 + WPARTS // 2) as i:
                for u in range(2):
                    piece = i * 2 + u - 2
                    act.dma_start(w_main[:, bass.ds(piece, 1)].rearrange("p a n -> p (a n)"),
                                  a["w_main"][bass.ds(piece, 1)].rearrange("a p n -> p (a n)")).then_inc(s_weights, 16)
                two_tiles(i)
            two_tiles(6)
            two_tiles(7, False)
            for u in range(2):
                copy_queries(PAIRS - 2 + u, PAIRS // 2 - 1, u)
            act.wait_ge(s_idx_t, 1)
            nc.scalar.copy(cache_idx.rearrange("p h b -> p (h b)"), bank[4][:, 0:2 * B]).then_inc(s_idx, 1)
            nc.scalar.copy(over_idx.rearrange("p h b -> p (h b)"), bank[4][:, 2 * B:4 * B]).then_inc(s_idx, 1)
            for b in range(2):
                r = slice(T * b, T * b + T)
                nc.scalar.copy(fresh_idx[r], bank[4][r, 4 * B:5 * B].rearrange("p (q b) -> p b q", b=2)[:, b]).then_inc(s_idx, 1)

            for n, banks in enumerate(((6, 7), (2, 3), (0, 1))):
                act.wait_ge(folded, n + 1)
                for m in range(2):
                    ins = nc.scalar.copy((w_a_q, w_a_k, w_a_v)[n][:, m, :], bank[banks[m]][:])
                ins.then_inc(folded_act, 1)
            act.wait_ge(s_weights, 16 * (WPARTS + 6))
            act.wait_ge(s_zero, 4)
            for u in range(2):
                act.wait_ge(q_stored[u], 16 * (PAIRS // 2 + 1))
                act.wait_ge(kv_stored[u], 16 * (PAIRS // 2 + 1))

            def copy_keys(i, j):
                act.wait_ge(scored.sem, scored.at(i, 8 * (j + 1) - STEPS))
                act.wait_ge(pva.sem, pva.at(i, 0))
                for n in range(3):
                    use = 3 * j + n
                    act.wait_ge(k_tr.sem, k_tr.at(i, use + 1))
                    w = 4 * P if n < 2 else 2 * P
                    flat = k_t[:, j].rearrange("p g n -> p (g n)")
                    nc.scalar.copy(flat[:, n * 4 * P:n * 4 * P + w], bank[6 + use % 2][:, 0:w]).then_inc(keys_cop.sem, 1)

            def exp_scores(i, s):
                b = s // 4 % 2
                act.wait_ge(negated.sem, negated.at(i, s + 1))
                act.wait_ge(recd.sem, recd.at(i, s + 1 - 4))
                cols = pc[:, s % 4, b * T:b * T + SPAN]
                nc.scalar.activation(cols, cols, ACT.Exp, bias=neg_c[:, s % 4:s % 4 + 1], scale=1.0 / 16.0,
                                     accum_out=sum_c[:, s % 4:s % 4 + 1]).then_inc(exped.sem, 1)

            def copy_probs(i, s):
                act.wait_ge(p_tr.sem, p_tr.at(i, s + 1))
                act.wait_ge(pv_done.sem, pv_done.at(i, s // 2 + 1 - 2))
                nc.scalar.copy(pc_t[:, s % 4], bank[2 + s % 2][:, 0:3 * P]).then_inc(p_cop.sem, 1)

            def copy_outputs(i, m):
                n = m // 2
                act.wait_ge(pv_done.sem, pv_done.at(i, m + 1))
                act.wait_ge(z_done.sem, z_done.at(i, 0))
                nc.scalar.copy(o_t[:, 2 * (m % 2):2 * (m % 2) + 2, n * T:(n + 1) * T],
                               bank[4 + m % 2][:, 0:P].rearrange("p (c t) -> p c t", c=2)).then_inc(o_cop.sem, 1)

            def attend(i):
                for s in range(3, STEPS + 5):
                    if 3 <= s < STEPS + 3:
                        copy_probs(i, s - 3)
                    if LEAD <= s < STEPS:
                        exp_scores(i, s)
                    if s >= 6 and s % 2 == 0:
                        copy_outputs(i, (s - 6) // 2)

            def self_attention(i, more):
                act.wait_ge(qa_done.sem, qa_done.at(i, 1))
                for m in range(2):
                    for h in range(4):
                        r = slice(32 * h, 32 * h + 32)
                        ins = nc.scalar.activation(qa_blk[r, m, :, h, :], bank[6][r, m * TT:(m + 1) * TT].rearrange("p (b t) -> p b t", b=BT),
                                                   ACT.Identity, bias=bq[r, m:m + 1])
                ins.then_inc(qa_act.sem, 1)
                act.wait_ge(ka_done.sem, ka_done.at(i, 1))
                for m in range(2):
                    ins = nc.scalar.activation(ka_t[:, m, :], bank[4][:, m * TT:(m + 1) * TT], ACT.Identity, bias=bk[:, m:m + 1])
                ins.then_inc(ka_act.sem, 1)
                for j in range(PT):
                    act.wait_ge(st_done.sem, st_done.at(i, j + 1))
                    nc.scalar.copy(st[:, j, 0], bank[2 + 2 * j][:]).then_inc(st_act.sem, 1)
                for j in range(PT):
                    act.wait_ge(sa_sub.sem, sa_sub.at(i, j + 1))
                    nc.scalar.activation(pa[:, j], pa[:, j], ACT.Exp).then_inc(sa_exp.sem, 1)
                for j in range(PT):
                    act.wait_ge(pa_tr.sem, pa_tr.at(i, j + 1))
                    nc.scalar.copy(pa_t[:, j, 0:4].rearrange("p h n -> p (h n)"), bank[(4, 0)[j]][:]).then_inc(pa_act.sem, 1)
                for j in range(PT):
                    act.wait_ge(oa_tr.sem, oa_tr.at(i, j + 1))
                    for c in range(2):
                        ins = nc.scalar.copy(oa_t[:, j, 2 * c:2 * c + 2].rearrange("p h (b t) -> p b h t", b=2),
                                             bank[4 + j][:, 2 * c * P:2 * (c + 1) * P].rearrange("p (b h t) -> p b h t", b=2, h=2))
                    ins.then_inc(oa_cop.sem, 1)
                    if more:
                        copy_keys(i + 1, j)
                for j in range(PT):
                    act.wait_ge(x_tr.sem, x_tr.at(i, j + 1))
                    nc.scalar.copy(x_t[:, j].rearrange("p k n -> p (k n)"), bank[2 + j][:]).then_inc(x_cop.sem, 1)
                if more:
                    for s in range(LEAD):
                        exp_scores(i + 1, s)

            copy_keys(0, 0)
            copy_keys(0, 1)
            for s in range(LEAD):
                exp_scores(0, s)
            with act.Fori(0, TURNS - 1) as i:
                attend(i)
                self_attention(i, True)
            attend(TURNS - 1)
            self_attention(TURNS - 1, False)

            def root_mean_square(n, use):
                source = sel[:, n, D:] if use < 2 else x1[:, n]
                nc.scalar.activation(fjunk, source, ACT.Square, accum_out=small[:, use:use + 1]).then_inc(s_rms, 1)
                act.wait_ge(s_rms, 2 * use + 1)
                nc.scalar.activation(small[:, 4 + use:5 + use], small[:, use:use + 1], ACT.Sqrt, bias=eps, scale=1.0 / D).then_inc(s_rms, 1)

            def copy_rows(n, use):
                act.wait_ge(fh_tr.sem, fh_tr.at(0, use + 1))
                nc.scalar.copy(fh_t[:, :, n * P:(n + 1) * P], bank[1 + n][:].rearrange("p (k n) -> p k n", k=KD)).then_inc(fh_cop.sem, 1)

            act.wait_ge(s_pick, 1)
            nc.scalar.activation(small[:, 62:63], eps, ACT.Sqrt)
            for n in range(SN):
                act.wait_ge(s_sel[n], 16)
                if n == 1:
                    act.wait_ge(s_rms, 2)
                root_mean_square(n, n)
            for n in range(SN):
                copy_rows(n, n)
            for c in range(6):
                for n in range(SN):
                    act.wait_ge(fq_tr.sem, fq_tr.at(0, 2 * c + n + 1))
                    dst = fq_t[:, 4 * c:4 * c + 4, n * P:(n + 1) * P] if c < 4 else fk_t[:, 4 * (c - 4):4 * (c - 4) + 4, n * P:(n + 1) * P]
                    nc.scalar.copy(dst, bank[(2 * c + n) % 4][:].rearrange("p (h n) -> p h n", h=4)).then_inc(fq_cop.sem, 1)
            for t in range(FH + 4):
                if t < FH:
                    act.wait_ge(fneg.sem, fneg.at(0, t + 1))
                    if t >= 4:
                        act.wait_ge(frec.sem, frec.at(0, t + 1 - 4))
                    for n, lo, hi in ((0, 0, P), (1, P, P + S)):
                        nc.scalar.activation(fp[:, t % 4, lo:hi], fp[:, t % 4, lo:hi], ACT.Exp, bias=f_neg[:, t % 4, n:n + 1],
                                             scale=float(FHD) ** -0.5, accum_out=f_sum[:, t % 4, n:n + 1]).then_inc(fexp.sem, 1)
                if 2 <= t < FH + 2:
                    h = t - 2
                    act.wait_ge(fp_tr.sem, fp_tr.at(0, h + 1))
                    if h >= 2:
                        act.wait_ge(fpv.sem, fpv.at(0, h + 1 - 2))
                    nc.scalar.copy(fp_t[:, h % 2], bank[2 + h % 2][:, 0:P + S]).then_inc(fp_cop.sem, 1)
                if t >= 4:
                    h = t - 4
                    act.wait_ge(fpv.sem, fpv.at(0, h + 1))
                    nc.scalar.copy(fo_t[:, h], bank[4 + h % 4][:, 0:S]).then_inc(fo_cop.sem, 1)
            for n in range(SN):
                act.wait_ge(f_x1.sem, f_x1.at(0, n + 1))
                act.wait_ge(s_rms, 2 * (2 + n))
                root_mean_square(n, 2 + n)
                copy_rows(n, 2 + n)
            for n in range(SN):
                nc.scalar.activation(small[:, 12 + n:13 + n], small[:, 8 + n:9 + n], ACT.Exp, scale=-1.0).then_inc(s_esc, 1)
            for f in range(NIN):
                act.wait_ge(g_done.sem, g_done.at(0, f + 1))
                if f >= 2:
                    act.wait_ge(g_act.sem, g_act.at(0, f + 1 - 2))
                nc.scalar.activation(e_g[:, f % 2], bank[(3, 4, 5, 0)[f % 4]][:, 0:S], ACT.Exp, scale=-1.0).then_inc(g_exp.sem, 1)

        @block.vector
        def _(dve):
            for g in (inverted, normed, scaled, turned_v, cosd, roped, same_p, src_v, masked, negated, recd, weighed,
                      qa_dve, ka_dve, st_dve, pa_dve, sa_mask, sa_max, sa_sum, sa_rec, va_cop, oa_norm, resid, hid, rscore, sc_cop):
                dve.sem_inc(g.sem, g.prime)

            steps = [0]

            def step(ins):
                steps[0] += 1
                ins.then_inc(s_pre, 1)
                dve.wait_ge(s_pre, steps[0])

            dve.wait_ge(s_lens, 32)
            step(nc.vector.tensor_copy(posf, len_all[:, 0:PAIRS]))
            step(nc.vector.tensor_scalar(pos_idx, posf, seq_base[:, 0:1], None, ALU.add))
            step(nc.vector.tensor_scalar(first_seen, len_all[:, PAIRS:], -1.0, float(WINDOW), ALU.mult, ALU.add))
            dve.wait_ge(s_early, 48)
            step(nc.vector.tensor_copy(blocks[0:B], blocks_i[0:B]))
            step(nc.vector.tensor_scalar(lens_i[0:B, 1:2], lens_i[0:B, 0:1], 4, None, ALU.logical_shift_right))
            step(nc.vector.tensor_scalar(lens_i[0:B, 2:3], lens_i[0:B, 0:1], BLOCK - 1, None, ALU.bitwise_and))
            for k in range(4):
                step(nc.vector.tensor_scalar(lens_i[0:B, 3 + k:4 + k], lens_i[0:B, 0:1], k, 1, ALU.logical_shift_right, ALU.bitwise_and))
            step(nc.vector.tensor_copy(lens[0:B, 0:7], lens_i[0:B, 0:7]))
            iota_blk = k32[0:B, 0:NBLK]
            iota_slot = k32[0:B, NBLK:NBLK + WSLOTS]
            iota_new = k32[0:B, NBLK + WSLOTS:NBLK + WSLOTS + NSLOTS * BLOCK]
            token1 = k32[0:B, NBLK + WSLOTS + NSLOTS * BLOCK:NBLK + WSLOTS + NSLOTS * BLOCK + 1]
            iota_off = k32[0:B, NBLK + WSLOTS + NSLOTS * BLOCK + 1:]
            step(nc.vector.tensor_scalar(slot_no[0:B], iota_slot, lens[0:B, 1:2], float(-WINDOW // BLOCK), ALU.add, ALU.add))
            for k in range(WSLOTS):
                if k >= 4:
                    dve.wait_ge(s_pre, steps[0] - 3)
                steps[0] += 1
                nc.vector.scalar_tensor_tensor(out=hit[0:B, k % 4], in0=iota_blk, scalar=slot_no[0:B, k:k + 1], in1=blocks[0:B],
                                               op0=ALU.is_equal, op1=ALU.mult, accum_out=win[0:B, k:k + 1]).then_inc(s_pre, 1)
            step(nc.vector.tensor_scalar(tok[0:B, 0], iota_new, lens[0:B, 2:3], None, ALU.subtract))
            step(nc.vector.tensor_scalar(tok[0:B, 1], tok[0:B, 0], 0.0, None, ALU.is_ge))
            step(nc.vector.scalar_tensor_tensor(out=tok[0:B, 1], in0=tok[0:B, 0], scalar=float(T), in1=tok[0:B, 1], op0=ALU.is_lt, op1=ALU.mult))
            step(nc.vector.scalar_tensor_tensor(out=tok[0:B, 2], in0=tok[0:B, 0], scalar=token1, in1=tok[0:B, 1], op0=ALU.add, op1=ALU.mult))
            assert steps[0] == PRE_WIN
            dve.wait_ge(s_consts, 32)
            step(nc.vector.tensor_scalar(scale1, scale1, 1.0, None, ALU.add))
            assert steps[0] == PRE_ALL

            def compare(g, par):
                dve.wait_ge(prod_p.sem, prod_p.at(g, 1 - 2))
                nc.vector.tensor_tensor(same[0:GP, par], blk_w[0:GP], blk_r[0:GP, bass.ds(g, 1)].to_broadcast([GP, WRITERS]),
                                        ALU.is_equal).then_inc(same_p.sem, 1)

            def last_writers(g, par):
                dve.wait_ge(prod_p.sem, prod_p.at(g, 1))
                nc.vector.tensor_reduce(src[0:GP, bass.ds(g, 1)].rearrange("p a o -> p (a o)"), prod[par][0:GP], AX.X, ALU.max).then_inc(src_v.sem, 1)

            def tile(t, half, u):
                dve.wait_ge(rooted.sem, rooted.at(t, 1))
                nc.vector.reciprocal(inv[:, u], root[:, u]).then_inc(inverted.sem, 1)
                dve.wait_ge(inverted.sem, inverted.at(t, 1))
                dve.wait_ge(turned_p.sem, turned_p.at(t, 1 - 2))
                for lo, hi, part in ((0, CH, 0), (CH, QK, 1)):
                    nc.vector.tensor_tensor(qk[:, u, lo:hi].rearrange("p h a d -> p h (a d)"),
                                            bank[2 * u + part][:, 0:(hi - lo) * CHD].rearrange("p (h d) -> p h d", h=hi - lo),
                                            inv[:, u, lo:hi].unsqueeze(2).to_broadcast([P, hi - lo, CHD]), ALU.mult).then_inc(normed.sem, 1)
                dve.wait_ge(normed.sem, normed.at(t, 2))
                flat = qk[:, u].rearrange("p h a d -> p h (a d)")
                nc.vector.tensor_tensor(flat, flat, scale1, ALU.mult).then_inc(scaled.sem, 1)
                dve.wait_ge(scaled.sem, scaled.at(t, 1))
                cos = rope[:, bass.ds(t, 1), 0:32].unsqueeze(2).to_broadcast([P, QK, 2, 32])
                sin = rope[:, bass.ds(t, 1), 64:96].to_broadcast([P, QK, 32])
                nc.vector.tensor_tensor(qk_cos[:, u], qk[:, u], cos, ALU.mult).then_inc(cosd.sem, 1)
                nc.vector.tensor_tensor(turned[:, u, :, 1, :], qk[:, u, :, 0, :], sin, ALU.mult).then_inc(turned_v.sem, 1)
                dve.wait_ge(cosd.sem, cosd.at(t, 1))
                dve.wait_ge(turned_v.sem, turned_v.at(t, 1))
                dve.wait_ge(turned_p.sem, turned_p.at(t, 1))
                dve.wait_ge(q_tr.sem, q_tr.at(t, 1 - 2))
                nc.vector.tensor_tensor(qr[:, u], qk_cos[:, u, 0:CH].rearrange("p h a d -> p (h a d)"),
                                        turned[:, u, 0:CH].rearrange("p h a d -> p (h a d)"), ALU.add).then_inc(roped.sem, 1)
                dve.wait_ge(kv_stored[u], half * 16 + 16)
                nc.vector.tensor_tensor(kvn[:, u, 0:CG * CHD], qk_cos[:, u, CH:].rearrange("p h a d -> p (h a d)"),
                                        turned[:, u, CH:].rearrange("p h a d -> p (h a d)"), ALU.add).then_inc(roped.sem, 1)

            dve.wait_ge(s_rope, 16 * PAIRS)
            tile(0, 0, 0)
            dve.wait_ge(s_win_in, 48)
            compare(0, 0)
            tile(1, 0, 1)
            with dve.Fori(1, GROUPS // 2) as i:
                for u in range(2):
                    compare(i * 2 + u - 1, 1 - u)
                    tile(i * 2 + u, i, u)
                    last_writers(i * 2 + u - 2, u)
            compare(GROUPS - 1, 1)
            tile(GROUPS, GROUPS // 2, 0)
            last_writers(GROUPS - 2, 0)
            tile(GROUPS + 1, GROUPS // 2, 1)
            last_writers(GROUPS - 1, 1)
            with dve.Fori(GROUPS // 2 + 1, PAIRS // 2) as i:
                for u in range(2):
                    tile(i * 2 + u, i, u)

            step(nc.vector.scalar_tensor_tensor(out=al[0:B, 0, 0].rearrange("p (s o) -> p s o", o=BLOCK),
                                                in0=win[0:B].unsqueeze(2).to_broadcast([B, WSLOTS, BLOCK]), scalar=float(BLOCK),
                                                in1=iota_off.unsqueeze(1).to_broadcast([B, WSLOTS, BLOCK]), op0=ALU.mult, op1=ALU.add))
            dve.wait_ge(s_src_in, 16)
            cur, n = 0, WPOS
            for k in (3, 2, 1, 0):
                n -= 1 << k
                here, there = al[0:B, cur], al[0:B, 1 - cur, :, 0:n]
                step(nc.vector.tensor_tensor(there, here[:, :, 1 << k:n + (1 << k)], here[:, :, 0:n], ALU.subtract))
                step(nc.vector.scalar_tensor_tensor(out=there, in0=there, scalar=lens[0:B, 3 + k:4 + k], in1=here[:, :, 0:n], op0=ALU.mult, op1=ALU.add))
                cur = 1 - cur
            rows, last = al[0:B, cur, 0, 0:SPAN], al[0:B, cur, 1, 0:SPAN]
            step(nc.vector.tensor_scalar(idx_f[0:B, 3], last, 0.0, SKIP, ALU.is_gt, ALU.mult))
            step(nc.vector.tensor_tensor(idx_f[0:B, 0], rows, idx_f[0:B, 3], ALU.add))
            step(nc.vector.tensor_scalar(idx_f[0:B, 3], last, 0.0, SKIP, ALU.is_equal, ALU.mult))
            step(nc.vector.scalar_tensor_tensor(out=idx_f[0:B, 1], in0=last, scalar=-1.0, in1=idx_f[0:B, 3], op0=ALU.add, op1=ALU.add))
            step(nc.vector.tensor_copy(idx_f[0:B, 2, 0:P].rearrange("p (c t) -> p c t", c=2),
                                       idx_f[0:B, 1, WINDOW:SPAN].unsqueeze(1).to_broadcast([B, 2, T])))
            assert steps[0] == PRE_IDX

            for n, banks in enumerate(((0, 1), (5, 4), (2, 3))):
                dve.wait_ge(folded, n + 1)
                for m in range(2):
                    ins = nc.vector.tensor_copy((w_a_q, w_a_k, w_a_v)[n][:, 2 + m, :], bank[banks[m]][:])
                ins.then_inc(folded_dve, 1)
            dve.wait_ge(s_weights, 16 * (WPARTS + 6))
            dve.wait_ge(s_zero, 4)
            for u in range(2):
                dve.wait_ge(q_stored[u], 16 * (PAIRS // 2 + 1))
                dve.wait_ge(kv_stored[u], 16 * (PAIRS // 2 + 1))

            def mask_scores(i, s):
                n, b, g = s // 4, s // 4 % 2, s % 4
                dve.wait_ge(scored.sem, scored.at(i, s + 1))
                if g == 0:
                    dve.wait_ge(masks.sem, masks.at(i, n + 1))
                dve.wait_ge(p_tr.sem, p_tr.at(i, s + 1 - 4))
                dve.wait_ge(exped.sem, exped.at(i, s + 1 - 4))
                dve.sem_inc(s_passed, 1)
                nc.vector.tensor_tensor_reduce(out=pc[:, s % 4, b * T:b * T + SPAN], in0=bank[s % 2][:, 0:SPAN], in1=mk[:, b],
                                               scale=1.0, scalar=-3.0e38, op0=ALU.add, op1=ALU.max,
                                               accum_out=top_c[:, s % 4:s % 4 + 1]).then_inc(masked.sem, 1)
                dve.wait_ge(masked.sem, masked.at(i, s + 1))
                nc.vector.tensor_scalar(neg_c[:, s % 4:s % 4 + 1], top_c[:, s % 4:s % 4 + 1], -1.0 / 16.0, None, ALU.mult).then_inc(negated.sem, 1)

            def divide_probs(i, s):
                b = s // 4 % 2
                dve.wait_ge(exped.sem, exped.at(i, s + 1))
                nc.vector.reciprocal(rec_c[:, s % 4:s % 4 + 1], sum_c[:, s % 4:s % 4 + 1]).then_inc(recd.sem, 1)
                dve.wait_ge(recd.sem, recd.at(i, s + 1))
                cols = pc[:, s % 4, b * T:b * T + SPAN]
                nc.vector.tensor_scalar(cols, cols, rec_c[:, s % 4:s % 4 + 1], None, ALU.mult).then_inc(weighed.sem, 1)

            def attend(i):
                for s in range(LEAD, STEPS + 2):
                    divide_probs(i, s - 2)
                    if s < STEPS:
                        mask_scores(i, s)

            def self_attention(i, more):
                dve.wait_ge(qa_done.sem, qa_done.at(i, 2))
                for m in range(2):
                    for h in range(4):
                        r = slice(32 * h, 32 * h + 32)
                        ins = nc.vector.tensor_scalar(qa_blk[r, 2 + m, :, h, :], bank[7][r, m * TT:(m + 1) * TT].rearrange("p (b t) -> p b t", b=BT),
                                                      bq[r, 2 + m:3 + m], None, ALU.add)
                ins.then_inc(qa_dve.sem, 1)
                dve.wait_ge(ka_done.sem, ka_done.at(i, 2))
                for m in range(2):
                    ins = nc.vector.tensor_scalar(ka_t[:, 2 + m, :], bank[5][:, m * TT:(m + 1) * TT], bk[:, 2 + m:3 + m], None, ALU.add)
                ins.then_inc(ka_dve.sem, 1)
                for j in range(PT):
                    dve.wait_ge(st_done.sem, st_done.at(i, PT + j + 1))
                    nc.vector.tensor_copy(st[:, j, 1], bank[3 + 2 * j][:]).then_inc(st_dve.sem, 1)
                for j in range(PT):
                    dve.wait_ge(sa_done.sem, sa_done.at(i, j + 1))
                    for half in range(2):
                        nc.vector.scalar_tensor_tensor(out=pa[:, j, 4 * half:4 * half + 4].rearrange("p h b t -> p (h b) t"),
                                                       in0=bank[(6, 0)[j] + half][:].rearrange("p (n t) -> p n t", t=T), scalar=float(AHD) ** -0.5,
                                                       in1=mask_a.unsqueeze(1).to_broadcast([P, 8, T]), op0=ALU.mult, op1=ALU.add).then_inc(sa_mask.sem, 1)
                    dve.wait_ge(sa_mask.sem, sa_mask.at(i, 2 * j + 2))
                    nc.vector.tensor_reduce(top_a[:, j], pa[:, j].rearrange("p h b t -> p (h b) t"), AX.X, ALU.max).then_inc(sa_max.sem, 1)
                for j in range(PT):
                    dve.wait_ge(va_done.sem, va_done.at(i, j + 1))
                    for b in range(2):
                        r = slice(64 * b, 64 * b + 64)
                        ins = nc.vector.tensor_tensor(va[r, j, b, :], bank[2 + j][r, :], bv[r, :], ALU.add)
                    ins.then_inc(va_cop.sem, 1)
                for j in range(PT):
                    dve.wait_ge(pa_tr.sem, pa_tr.at(i, j + 1))
                    nc.vector.tensor_copy(pa_t[:, j, 4:8].rearrange("p h n -> p (h n)"), bank[(5, 1)[j]][:]).then_inc(pa_dve.sem, 1)
                for j in range(PT):
                    dve.wait_ge(sa_exp.sem, sa_exp.at(i, j + 1))
                    nc.vector.tensor_reduce(sum_a[:, j], pa[:, j].rearrange("p h b t -> p (h b) t"), AX.X, ALU.add).then_inc(sa_sum.sem, 1)
                    dve.wait_ge(sa_sum.sem, sa_sum.at(i, j + 1))
                    nc.vector.reciprocal(rec_a[:, j], sum_a[:, j]).then_inc(sa_rec.sem, 1)
                    dve.wait_ge(sa_rec.sem, sa_rec.at(i, j + 1))
                    dve.wait_ge(pva.sem, pva.at(i, j + 1))
                    for c in range(2):
                        for r in range(2):
                            rows_r = slice(64 * r, 64 * r + 64)
                            ins = nc.vector.tensor_tensor(
                                oa[rows_r, j, c].rearrange("p b h d -> p h b d"),
                                bank[(6, 2)[j] + c][rows_r, :].rearrange("p (h b r d) -> p h b r d", b=2, r=2, d=AHD)[:, :, :, r, :],
                                rec_a[rows_r, j, 8 * c:8 * c + 8].rearrange("p (h b) -> p h b", b=2).unsqueeze(3).to_broadcast([64, 4, 2, AHD]), ALU.mult)
                    ins.then_inc(oa_norm.sem, 1)
                for j in range(PT):
                    dve.wait_ge(z_done.sem, z_done.at(i, j + 1))
                    dve.wait_ge(x_bias.sem, x_bias.at(i, j + 1))
                    dve.wait_ge(xh_stored[j], i * 16 + 16)
                    nc.vector.tensor_tensor(xh[:, j, 0:D], bank[j][:], xr[:, j], ALU.add).then_inc(resid.sem, 1)
                if more:
                    for s in range(2):
                        mask_scores(i + 1, s)
                for j in range(PT):
                    dve.wait_ge(c_done.sem, c_done.at(i, j + 1))
                    dve.wait_ge(be_loaded[j], i * 32 + 32)
                    nc.vector.tensor_tensor(xh[:, j, D:], bank[4 + j][:], b_exp[:, j], ALU.add).then_inc(hid.sem, 1)
                    dve.wait_ge(hid.sem, hid.at(i, j + 1))
                    dve.wait_ge(rscore.sem, rscore.at(i, j))
                    dve.wait_ge(sc_cop.sem, sc_cop.at(i, 0))
                    nc.vector.tensor_tensor_reduce(out=junk, in0=xh[:, j, D:], in1=router, scale=1.0, scalar=0.0, op0=ALU.mult, op1=ALU.add,
                                                   accum_out=score_t[:, j:j + 1]).then_inc(rscore.sem, 1)
                    if more:
                        divide_probs(i + 1, j)
                    if more:
                        mask_scores(i + 1, 2 + j)
                dve.wait_ge(rscore.sem, rscore.at(i, PT))
                nc.vector.tensor_copy(score[:, bass.ds(i * PT, PT)], score_t).then_inc(sc_cop.sem, 1)

            for s in range(LEAD):
                mask_scores(0, s)
            for s in range(2):
                divide_probs(0, s)
            with dve.Fori(0, TURNS - 1) as i:
                attend(i)
                self_attention(i, True)
            attend(TURNS - 1)
            self_attention(TURNS - 1, False)

            picks = [0]

            def pick_step(ins):
                picks[0] += 1
                ins.then_inc(s_pick, 1)
                dve.wait_ge(s_pick, picks[0])

            Q = PAIRS
            dve.wait_ge(s_sct, 1)
            for b in range(2):
                pick_step(nc.vector.max(top8[0:Q, b], bank[0][0:Q, b * T:(b + 1) * T]))
            for b in range(2):
                pick_step(nc.vector.max_index(at8[0:Q, b], top8[0:Q, b], bank[0][0:Q, b * T:(b + 1) * T]))
            pick_step(nc.vector.tensor_scalar(neg8[0:Q], at8[0:Q], -1.0, None, ALU.mult))
            for b in range(2):
                ins = nc.vector.max(sorted8[0:Q, b], neg8[0:Q, b])
            pick_step(ins)
            pick_step(nc.vector.tensor_tensor(spread[0:Q], sorted8[0:Q].rearrange("p b j -> p (b j)").unsqueeze(1).to_broadcast([Q, Q, 2 * KEEP]),
                                              ident[0:Q, 0:Q].unsqueeze(2).to_broadcast([Q, Q, 2 * KEEP]), ALU.mult))
            assert picks[0] == PICKS
            dve.wait_ge(s_pick, PICKS + 1)
            nc.vector.scalar_tensor_tensor(out=picked[:, 1], in0=bank[3][:, 0:SN], scalar=-1.0, in1=kept_row, op0=ALU.mult, op1=ALU.add).then_inc(s_pick, 1)
            nc.vector.tensor_scalar(picked[:, 0], bank[3][:, 0:SN], -1.0, None, ALU.mult).then_inc(s_pick, 1)

            def norm_rows(n, use):
                dve.wait_ge(s_rms, 2 * (use + 1))
                nc.vector.reciprocal(small[:, 16 + use:17 + use], small[:, 4 + use:5 + use]).then_inc(s_gate, 1)
                dve.wait_ge(s_gate, use + 1 if use < 2 else use + 3)
                if use >= 2:
                    dve.wait_ge(fh_tr.sem, fh_tr.at(0, 2))
                source, weight = (sel[:, n, D:], ln1) if use < 2 else (x1[:, n], ln2)
                nc.vector.scalar_tensor_tensor(out=fh[:, n], in0=source, scalar=small[:, 16 + use:17 + use], in1=weight,
                                               op0=ALU.mult, op1=ALU.mult).then_inc(fh_ready.sem, 1)

            dve.wait_ge(s_ln1, 16)
            for n in range(SN):
                dve.wait_ge(s_sel[n], 16)
                norm_rows(n, n)
            dve.wait_ge(s_frope, 32)
            for n in range(SN):
                nc.vector.tensor_tensor_reduce(out=x1[:, n], in0=sel[:, n, D:], in1=router, scale=1.0, scalar=0.0, op0=ALU.mult, op1=ALU.add,
                                               accum_out=small[:, 8 + n:9 + n]).then_inc(s_gate, 1)
            dve.wait_ge(s_fin, 32)
            for c in range(NQKV):
                for n in range(SN):
                    use = 2 * c + n
                    x = fq[:, n, c * 512:(c + 1) * 512]
                    dve.wait_ge(fq_mm.sem, fq_mm.at(0, use + 1))
                    nc.vector.tensor_tensor(x, bank[4 + use % 4][:], fbias[:, c * 512:(c + 1) * 512], ALU.add).then_inc(fq_bias.sem, 1)
                    if c < 6:
                        dve.wait_ge(fq_bias.sem, fq_bias.at(0, use + 1))
                        halves = x.rearrange("p (h a d) -> p h a d", a=2, d=64)
                        co, si = fcos[:, n], fsin[:, n].rearrange("p (h a d) -> p h a d", a=2, d=64)
                        nc.vector.tensor_tensor(co.rearrange("p (h d) -> p h d", d=64), x.rearrange("p (h d) -> p h d", d=64),
                                                frope[:, n, 0:64].unsqueeze(1).to_broadcast([P, 8, 64]), ALU.mult)
                        nc.vector.tensor_tensor(si[:, :, 0, :], halves[:, :, 1, :], frope[:, n, 128:192].unsqueeze(1).to_broadcast([P, 4, 64]), ALU.mult)
                        nc.vector.tensor_tensor(si[:, :, 1, :], halves[:, :, 0, :], frope[:, n, 192:256].unsqueeze(1).to_broadcast([P, 4, 64]),
                                                ALU.mult).then_inc(f_sin.sem, 1)
                        dve.wait_ge(f_sin.sem, f_sin.at(0, use + 1))
                        nc.vector.tensor_tensor(x, co, fsin[:, n], ALU.add).then_inc(f_rope.sem, 1)
            for t in range(FH + 1):
                if t < FH:
                    dve.wait_ge(fs.sem, fs.at(0, t + 1))
                    if t >= 4:
                        dve.wait_ge(fp_tr.sem, fp_tr.at(0, t + 1 - 4))
                    for n, lo, hi in ((0, 0, P), (1, P, P + S)):
                        mask = mask_f[:, 1] if n == 0 else mask_f.rearrange("p a n -> p (a n)")
                        nc.vector.tensor_tensor_reduce(out=fp[:, t % 4, lo:hi], in0=bank[t % 2][:, lo:hi], in1=mask, scale=1.0, scalar=-3.0e38,
                                                       op0=ALU.add, op1=ALU.max, accum_out=f_top[:, t % 4, n:n + 1]).then_inc(fmask.sem, 1)
                    dve.wait_ge(fmask.sem, fmask.at(0, 2 * (t + 1)))
                    nc.vector.tensor_scalar(f_neg[:, t % 4], f_top[:, t % 4], -float(FHD) ** -0.5, None, ALU.mult).then_inc(fneg.sem, 1)
                if t >= 1:
                    h = t - 1
                    dve.wait_ge(fexp.sem, fexp.at(0, 2 * (h + 1)))
                    nc.vector.reciprocal(f_rec[:, h % 4], f_sum[:, h % 4]).then_inc(frec.sem, 1)
                    dve.wait_ge(frec.sem, frec.at(0, h + 1))
                    for n, lo, hi in ((0, 0, P), (1, P, P + S)):
                        nc.vector.tensor_scalar(fp[:, h % 4, lo:hi], fp[:, h % 4, lo:hi], f_rec[:, h % 4, n:n + 1], None, ALU.mult).then_inc(fnorm.sem, 1)
            for n in range(SN):
                dve.wait_ge(fwo.sem, fwo.at(0, 1 if n == 0 else 5))
                nc.vector.tensor_tensor(x1[:, n], bank[6 + n][:], sel[:, n, D:], ALU.add).then_inc(f_x1.sem, 1)
                norm_rows(n, 2 + n)
            dve.wait_ge(s_esc, 2)
            nc.vector.tensor_scalar(small[:, 12:14], small[:, 12:14], 1.0, None, ALU.add).then_inc(s_gate, 1)
            dve.wait_ge(s_gate, 7)
            nc.vector.reciprocal(small[:, 14:16], small[:, 12:14]).then_inc(s_gate, 1)
            dve.wait_ge(s_gate, 8)
            nc.vector.tensor_scalar(small[:, 36:38], small[:, 14:16], -1.0, 1.0, ALU.mult, ALU.add).then_inc(s_gate, 1)
            dve.wait_ge(s_gate, 9)
            for f in range(NIN):
                if f < SN:
                    nc.vector.scalar_tensor_tensor(out=pre[:, f], in0=sel[:, f, D:], scalar=small[:, 36 + f:37 + f], in1=sel[:, f, 0:D],
                                                   op0=ALU.mult, op1=ALU.add).then_inc(s_last, 1)
                    dve.wait_ge(s_last, 2 * f + 1)
                    nc.vector.scalar_tensor_tensor(out=pre[:, f], in0=x1[:, f], scalar=small[:, 14 + f:15 + f], in1=pre[:, f],
                                                   op0=ALU.mult, op1=ALU.add).then_inc(s_last, 1)
                gb = bank[(3, 4, 5, 0)[f % 4]]
                r = r_g[:, f % 2]
                dve.wait_ge(g_exp.sem, g_exp.at(0, f + 1))
                nc.vector.tensor_scalar(r, e_g[:, f % 2], 1.0, None, ALU.add).then_inc(g_one.sem, 1)
                dve.wait_ge(g_one.sem, g_one.at(0, 3 * f + 1))
                nc.vector.reciprocal(r, r).then_inc(g_one.sem, 1)
                dve.wait_ge(g_one.sem, g_one.at(0, 3 * f + 2))
                nc.vector.tensor_tensor(r, r, gb[:, 0:S], ALU.mult).then_inc(g_one.sem, 1)
                dve.wait_ge(g_one.sem, g_one.at(0, 3 * f + 3))
                nc.vector.tensor_tensor(act_t[:, f], r, gb[:, S:2 * S], ALU.mult).then_inc(g_act.sem, 1)
            for n in range(SN):
                dve.wait_ge(f_down.sem, f_down.at(0, n + 1))
                nc.vector.scalar_tensor_tensor(out=fh[:, n], in0=bank[6 + n][:], scalar=small[:, 14 + n:15 + n], in1=pre[:, n],
                                               op0=ALU.mult, op1=ALU.add).then_inc(s_last, 1)

        @block.gpsimd
        def _(pool):
            for g in (turned_p, prod_p, idx_set, seen_set, mask_a1, masks, x_bias, sa_sub, out_add):
                pool.sem_inc(g.sem, g.prime)
            def gather(dst, table, idx, top):
                return pool.indirect_dma_start(out=dst, out_offset=None, in_=table, in_offset=bass.IndirectOffsetOnAxis(ap=idx, axis=0),
                                               bounds_check=top, oob_is_err=False)

            pool.wait_ge(s_pre, 2)
            for t in range(PAIRS):
                gather(rope[:, t], a["rope"], pos_idx[:, t:t + 1], NBLK * BLOCK - 1).then_inc(s_rope, 16)
            pool.wait_ge(s_rope, 16 * PAIRS)

            def turn_sine(t, u):
                pool.wait_ge(scaled.sem, scaled.at(t, 1))
                pool.wait_ge(roped.sem, roped.at(t, 2 - 4))
                nc.gpsimd.tensor_tensor(turned[:, u, :, 0, :], qk[:, u, :, 1, :], rope[:, bass.ds(t, 1), 32:64].to_broadcast([P, QK, 32]),
                                        ALU.mult).then_inc(turned_p.sem, 1)

            def mark_writers(g, par):
                pool.wait_ge(same_p.sem, same_p.at(g, 1))
                pool.wait_ge(src_v.sem, src_v.at(g, 1 - 2))
                nc.gpsimd.tensor_tensor(prod[par][0:GP], tok_all[0:GP].rearrange("p (w o) -> p o w", o=BLOCK),
                                        same[0:GP, par].unsqueeze(1).to_broadcast([GP, BLOCK, WRITERS]), ALU.mult).then_inc(prod_p.sem, 1)

            turn_sine(0, 0)
            turn_sine(1, 1)
            mark_writers(0, 0)
            with pool.Fori(1, GROUPS // 2) as i:
                for u in range(2):
                    turn_sine(i * 2 + u, u)
                    mark_writers(i * 2 + u - 1, 1 - u)
            turn_sine(GROUPS, 0)
            mark_writers(GROUPS - 1, 1)
            for u, parts in ((1, (q_blk.rearrange("p a b c d n -> p (a b c d n)"), qa_blk.rearrange("p a b c n -> p (a b c n)"))),
                             (0, (pc.rearrange("p a n -> p (a n)"), va.rearrange("p a b n -> p (a b n)")))):
                turn_sine(GROUPS + 2 - u, u)
                for part in parts:
                    nc.gpsimd.memset(part, 0.0).then_inc(s_zero, 1)
            turn_sine(GROUPS + 3, 1)
            with pool.Fori(GROUPS // 2 + 2, PAIRS // 2) as i:
                for u in range(2):
                    turn_sine(i * 2 + u, u)

            def set_indices(i, j):
                pool.wait_ge(pv_done.sem, pv_done.at(i, 4 * (j + 1) - STEPS // 2))
                nc.gpsimd.tensor_copy(turn_idx[:, j, 0:4].rearrange("p (b h) -> p h b", h=2), cache_idx[:, :, bass.ds(i * BT + 2 * j, 2)]).then_inc(idx_set.sem, 1)
                nc.gpsimd.tensor_copy(turn_idx[:, j, 4:8].rearrange("p (b h) -> p h b", h=2), over_idx[:, :, bass.ds(i * BT + 2 * j, 2)]).then_inc(idx_set.sem, 1)
                nc.gpsimd.tensor_copy(turn_idx[:, j, 8:9], fresh_idx[:, bass.ds(i * PT + j, 1)]).then_inc(idx_set.sem, 1)
                pool.wait_ge(idx_set.sem, idx_set.at(i, 3 * j + 3))
                pool.sem_inc(s_passed, 1)

            def gather_cached(i, j):
                set_indices(i, j)
                for n in range(4):
                    gather(kv[:, j, n], a["cache"], turn_idx[:, j, n:n + 1], POOL_BLOCKS * BLOCK - 1).then_inc(cached[j], 16)

            def gather_fresh(i, j):
                pool.wait_ge(cached[j], i * 64 + 64)
                pool.sem_inc(s_passed, 1)
                for n in (4, 0, 1, 2, 3):
                    col = 8 if n == 4 else 4 + n
                    gather(kv[:, j, n], kv_new, turn_idx[:, j, col:col + 1], NT - 1).then_inc(fresh[j], 16)

            def make_mask(i, n):
                b = n % 2
                pool.wait_ge(masked.sem, masked.at(i, 4 * (n - 1)))
                pool.sem_inc(s_passed, 1)
                nc.gpsimd.tensor_scalar(mk[:, b], place_c[:, b], turn_seen[:, n:n + 1], NEG, ALU.is_lt, ALU.mult).then_inc(mask_a1.sem, 1)
                pool.wait_ge(mask_a1.sem, mask_a1.at(i, n + 1))
                nc.gpsimd.tensor_tensor(mk[:, b], mk[:, b], mask_c[:, b], ALU.add).then_inc(masks.sem, 1)

            def first_masks(i):
                nc.gpsimd.tensor_copy(turn_seen, first_seen[:, bass.ds(i * BT, BT)]).then_inc(seen_set.sem, 1)
                pool.wait_ge(seen_set.sem, seen_set.at(i, 1))
                make_mask(i, 0)
                make_mask(i, 1)

            def turn(i, more):
                make_mask(i, 2)
                make_mask(i, 3)
                if more:
                    gather_cached(i + 1, 0)
                    gather_cached(i + 1, 1)
                    gather_fresh(i + 1, 0)
                    gather_fresh(i + 1, 1)
                for j in range(PT):
                    pool.wait_ge(sa_max.sem, sa_max.at(i, j + 1))
                    scores = pa[:, j].rearrange("p h b t -> p (h b) t")
                    nc.gpsimd.tensor_tensor(scores, scores, top_a[:, j].unsqueeze(2).to_broadcast([P, 2 * HP, T]), ALU.subtract).then_inc(sa_sub.sem, 1)
                for j in range(PT):
                    pool.wait_ge(x_loaded[j], i * 16 + 16)
                    nc.gpsimd.tensor_tensor(xr[:, j], xr[:, j], bo, ALU.add).then_inc(x_bias.sem, 1)
                if more:
                    first_masks(i + 1)
                for j in range(PT):
                    pool.wait_ge(hid.sem, hid.at(i, j + 1))
                    nc.gpsimd.tensor_tensor(xr[:, j], xh[:, j, 0:D], xh[:, j, D:], ALU.add).then_inc(out_add.sem, 1)

            pool.wait_ge(s_idx, 4)
            gather_cached(0, 0)
            gather_cached(0, 1)
            for u in range(2):
                pool.wait_ge(kv_stored[u], 16 * (PAIRS // 2 + 1))
            for j in range(PT):
                gather_fresh(0, j)
            first_masks(0)
            pool.wait_ge(s_weights, 16 * (WPARTS + 6))
            for u in range(2):
                pool.wait_ge(q_stored[u], 16 * (PAIRS // 2 + 1))
            with pool.Fori(0, TURNS - 1) as i:
                turn(i, True)
            turn(TURNS - 1, False)

            for j in range(PT):
                pool.wait_ge(xh_stored[j], 16 * (TURNS + 1))
                pool.wait_ge(out_stored[j], 16 * (TURNS + 1))
            pool.wait_ge(s_pick, PICKS + 3)
            for n in range(SN):
                gather(sel[:, n], xh_rows, picked[:, 1, n:n + 1], NT - 1).then_inc(s_sel[n], 16)
            for n in range(SN):
                gather(frope[:, n], a["f_rope"], picked[:, 0, n:n + 1], T - 1).then_inc(s_frope, 16)
            for n in range(SN):
                pool.wait_ge(s_last, 2 * SN + n + 1)
                pool.indirect_dma_start(out=out.rearrange("q p n -> (q p) n"), out_offset=bass.IndirectOffsetOnAxis(ap=picked[:, 1, n:n + 1], axis=0),
                                        in_=fh[:, n], in_offset=None, bounds_check=NT - 1, oob_is_err=False).then_inc(s_fout, 16)
            pool.wait_ge(s_fout, 32)


def build(nc, ins, out_shape):
    args = {}
    for name, (shape, dt) in ins.items():
        args[name] = nc.dram_tensor(f"in_{name}", shape, dt, kind="ExternalInput").ap()
    out = nc.dram_tensor("out_0", out_shape, F32, kind="ExternalOutput").ap()
    block_kernel(nc, args, out)


def constants():
    f = np.float32
    t = np.arange(T)
    c = np.arange(WINDOW)
    seen = np.where(c[None, :] > t[:, None], 0.0, NEG)
    new = np.where(t[None, :] <= t[:, None], 0.0, NEG)
    far = np.full(T, 1.0e9)
    mask_c = np.stack([np.concatenate([seen, new], 1), np.concatenate([new, seen], 1)], 1)
    place = np.stack([np.concatenate([c, far]), np.concatenate([far, c])], 0)
    causal = np.where(np.arange(P)[None, :] <= np.arange(P)[:, None], 0.0, NEG)
    p = np.arange(P)
    seq = np.concatenate([(p % T)[:, None], (p[:, None] + P * np.arange(SN)[None, :]) // KEEP * T], 1)
    consts = np.concatenate([
        np.eye(P), np.tile(mask_c, (2, 1, 1)).reshape(P, -1), np.broadcast_to(place.reshape(1, -1), (P, 2 * SPAN)),
        np.tile(new, (2, 1)), np.concatenate([np.zeros((P, P)), causal], 1), np.full((P, 1), 1e-6), np.ones((P, 1)), seq], 1).astype(f)
    b = np.arange(B)[:, None]
    consts32 = np.concatenate([
        np.broadcast_to(np.arange(NBLK), (B, NBLK)), np.broadcast_to(np.arange(WSLOTS), (B, WSLOTS)),
        np.broadcast_to(np.arange(NSLOTS * BLOCK), (B, NSLOTS * BLOCK)), b * T + 1,
        np.broadcast_to(np.arange(BLOCK), (B, BLOCK))], 1).astype(f)
    half = CHD // 2
    inv = (f(1.0) / np.power(f(10000.0), np.arange(half, dtype=f) / f(half))).astype(f)
    ang = np.arange(NBLK * BLOCK, dtype=f)[:, None] * inv
    rope = np.concatenate([np.cos(ang), -np.sin(ang), np.sin(ang)], 1).astype(f)
    inv = (f(1.0) / np.power(f(10000.0), np.arange(0, FHD, 2, dtype=f) / f(FHD))).astype(f)
    ang = np.arange(T, dtype=f)[:, None] * inv
    f_rope = np.concatenate([np.cos(ang), np.cos(ang), -np.sin(ang), np.sin(ang)], 1).astype(f)
    return {"consts": consts, "consts32": consts32, "rope": rope, "f_rope": f_rope}


def laid_out(v):
    c = np.ascontiguousarray

    def parts(w):
        return c(w.reshape(w.shape[0] // P, P, w.shape[1]).transpose(1, 0, 2))

    def chunks(w):
        k = w.reshape(w.shape[0] // 512, KD, P, w.shape[1] // 512, 512)
        return c(k.transpose(3, 0, 2, 1, 4).reshape(-1, P, KD, 512))

    x = v["x"].reshape(PAIRS, P, KD, P)
    lens, tables = v["itok_B_37_3939"], v["itok_Bx257_0_4111"]
    d = {
        "x_t": c(x.transpose(0, 3, 2, 1)),
        "x_rows": v["x"].reshape(PAIRS, P, D),
        "lens_rep": c(np.concatenate([np.repeat(lens.reshape(PAIRS, 2).T, T, axis=0), np.broadcast_to(lens, (P, B))], 1)),
        "lens": lens.reshape(B, 1),
        "tables": tables,
        "experts": v["itok_B_0_15"].reshape(1, B),
        "qk_scale": c(np.broadcast_to(np.concatenate([np.tile(v["L0_cond_q_norm_scale"], CH), np.tile(v["L0_cond_k_norm_scale"], CG)]), (P, QK * CHD))),
        "w_qkv": parts(np.concatenate([v["L0_cond_Wq"].reshape(2, 2, 2, CHD, D).transpose(0, 2, 1, 3, 4).reshape(CH * CHD, D), v["L0_cond_Wk"], v["L0_cond_Wv"]], 0).T),
        "cache": np.concatenate([v["L0_cond_k_blocks"].transpose(0, 2, 1, 3).reshape(POOL_BLOCKS * BLOCK, CG * CHD),
                                 v["L0_cond_v_blocks"].transpose(0, 2, 1, 3).reshape(POOL_BLOCKS * BLOCK, CG * CHD)], 1),
        "w_main": c(np.concatenate([w.reshape(P, 2, 2 * D).transpose(1, 0, 2) for w in (
            parts(v["L0_cond_Wo"].reshape(D, 2, 2, 2, CHD).transpose(0, 1, 3, 2, 4).reshape(D, D)),
            parts(v["L0_attn_Wq"].T), parts(v["L0_attn_Wk"].T), parts(v["L0_attn_Wv"].T),
            v["L0_attn_Wo"].T.reshape(2, 4, 2, AHD, D).transpose(1, 3, 0, 2, 4).reshape(P, KD, D))], 0)),
        "bq": c(v["L0_attn_bq"].reshape(KD, P).T), "bk": c(v["L0_attn_bk"].reshape(KD, P).T),
        "bv": v["L0_attn_bv"], "bo": v["L0_attn_bo"], "router": v["L0_ffn_w_router"],
        "w_exp": c(v["L0_cond2_W"].reshape(16, KD, P, D).transpose(0, 2, 1, 3)),
        "b_exp": v["L0_cond2_b"],
        "f_qkv": chunks(np.concatenate([v["L0_ffn_wq"], v["L0_ffn_wk"], v["L0_ffn_wv"]], 1)),
        "f_bias": np.concatenate([v["L0_ffn_bq"], v["L0_ffn_bk"], v["L0_ffn_bv"]]),
        "f_wo": chunks(v["L0_ffn_wo"]), "f_gate": chunks(v["L0_ffn_w_gate"]), "f_up": chunks(v["L0_ffn_w_up"]),
        "f_down": chunks(v["L0_ffn_w_down"]), "ln1": v["L0_ffn_ln1_w"], "ln2": v["L0_ffn_ln2_w"],
    }
    d.update(constants())
    return {k: c(x) for k, x in d.items()}


def kernel(**inputs):
    import numpy as _np
    import concourse.bacc as _bacc
    from concourse import mybir as _mybir
    from concourse.bass_utils import run_bass_kernel_spmd as _run

    nc = _bacc.Bacc("TRN2", target_bir_lowering=False, num_devices=1)
    arrays = laid_out({k: _np.asarray(x) for k, x in inputs.items()})
    build(nc, {k: (x.shape, _mybir.dt.from_np(x.dtype)) for k, x in arrays.items()}, (PAIRS, P, D))
    r = _run(nc, [{f"in_{k}": x for k, x in arrays.items()}], core_ids=[0])
    return r.results[0]["out_0"].reshape(B, T, D)
```
